# Optimizing a Trainium2 kernel written in Bass

```python
import numpy as np
import jax
import jax.numpy as jnp

def _softmax(x, axis=-1):
    return jax.nn.softmax(x, axis=axis)

def _gelu(x):
    return jax.nn.gelu(x, approximate=True)

def _silu(x):
    return jax.nn.silu(x)

def _sigmoid(x):
    return jax.nn.sigmoid(x)

def _layernorm(x, axis=-1, eps=1e-05):
    m = jnp.mean(x, axis=axis, keepdims=True)
    v = jnp.var(x, axis=axis, keepdims=True)
    return (x - m) / jnp.sqrt(v + eps)

def _scatter_add(tgt, idx, src, axis=0):
    return tgt.at[idx].add(src)

def _segment_sum(src, seg, n):
    return jax.ops.segment_sum(src, seg, n)
kernel_name = 'mk_adaln_ffn_d2_seqx_r4_1476fa'

def setup_inputs(seed: int=0):
    np.random.seed(seed)
    _w = jnp.asarray

    def _rec_inputs():
        import jax
        import jax.numpy as jnp
        _rk = jax.random.key(seed)
        x = -0.000125 + 0.9999 * jax.random.normal(jax.random.fold_in(_rk, 1), (4, 512, 512), jnp.float32)
        _lenS = 512 - jax.random.randint(jax.random.fold_in(_rk, 7), (4,), 0, max(1, 512 // 4) + 1, jnp.int32)
        _lenS2 = 512 - jax.random.randint(jax.random.fold_in(_rk, 8), (4,), 0, max(1, 512 // 4) + 1, jnp.int32)
        fside_BxSxS_0 = -1.52775e-05 + 0.999936 * jax.random.normal(jax.random.fold_in(_rk, 11), (4, 512, 512), jnp.float32)
        cond_512 = -5.03954e-05 + 1.00559 * jax.random.normal(jax.random.fold_in(_rk, 12), (4, 128), jnp.float32)
        return (x, fside_BxSxS_0, cond_512)
    x, fside_BxSxS_0, cond_512 = _rec_inputs()

    def _L0_cond_setup():
        import jax, jax.numpy as jnp
        from jax import lax
        import numpy as np
        B, T, C, TD = (8, 512, 512, 128)

        def _bi_wkv(r, k, v, w, u, time_emb):
            tf = jax.nn.sigmoid(jnp.sum(time_emb, axis=-1))[:, None, None]
            decay = jnp.exp(-jnp.exp(w.astype(jnp.float32)))[None, :] * (0.5 + 0.5 * tf[:, :, 0])
            kf = k.astype(jnp.float32)
            vf = v.astype(jnp.float32)
            ek = jnp.exp(jnp.minimum(kf, 30.0))
            ekv = ek * vf

            def step(carry, x):
                a, b = carry
                ekv_t, ek_t = x
                a = a * decay + ekv_t
                b = b * decay + ek_t
                return ((a, b), (a, b))
            ekv_t = jnp.swapaxes(ekv, 0, 1)
            ek_t = jnp.swapaxes(ek, 0, 1)
            init = (jnp.zeros_like(decay), jnp.zeros_like(decay))
            _, (nf, df) = lax.scan(step, init, (ekv_t, ek_t))
            _, (nb, db) = lax.scan(step, init, (ekv_t, ek_t), reverse=True)
            nf = jnp.swapaxes(nf, 0, 1)
            df = jnp.swapaxes(df, 0, 1)
            nb = jnp.swapaxes(nb, 0, 1)
            db = jnp.swapaxes(db, 0, 1)
            euk = jnp.exp(jnp.minimum(u.astype(jnp.float32)[None, None, :] + kf, 30.0))
            num = nf + nb - ekv + euk * vf
            den = df + db - ek + euk
            base = jax.nn.sigmoid(r.astype(jnp.float32)) * (num / jnp.maximum(den, 1e-08))
            out = base * (0.8 + 0.2 * tf)
            return out.astype(r.dtype)
        key = jax.random.key(seed)
        ks = jax.random.split(key, 6)
        return {'r': jax.random.normal(ks[0], (B, T, C), dtype=jnp.float32), 'k': jax.random.normal(ks[1], (B, T, C), dtype=jnp.float32), 'v': jax.random.normal(ks[2], (B, T, C), dtype=jnp.float32), 'w': jax.random.normal(ks[3], (C,), dtype=jnp.float32), 'u': jax.random.normal(ks[4], (C,), dtype=jnp.float32), 'time_emb': jax.random.normal(ks[5], (B, TD), dtype=jnp.float32)}
    _L0_cond_all = _L0_cond_setup()
    _L0_cond_in = {k: v for k, v in _L0_cond_all.items() if k in ('w', 'u')}
    del _L0_cond_all

    def _L0_ffn_setup():
        import jax, jax.numpy as jnp
        import numpy as np
        E, K, H, I = (64, 6, 512, 352)
        NS = 2
        IS = NS * I
        CAP = 64
        T_TOKENS = (1, 256)
        SCALE = 0.02

        def _moe_infer(x, gate_w, w_gate, w_up, w_down):
            T = x.shape[0]
            TK = T * K
            logits = x @ gate_w.T
            scores = jax.nn.softmax(logits, axis=-1)
            topk_w, topk_i = jax.lax.top_k(scores, K)
            flat_i = topk_i.reshape(-1)
            flat_w = topk_w.reshape(-1)
            token_ids = jnp.arange(TK, dtype=jnp.int32) // K
            order = jnp.argsort(flat_i)
            sorted_e = flat_i[order]
            counts = jnp.bincount(flat_i, length=E)
            starts = jnp.concatenate([jnp.zeros((1,), counts.dtype), jnp.cumsum(counts)[:-1]])
            pos_sorted = jnp.arange(TK) - starts[sorted_e]
            pos = jnp.zeros((TK,), jnp.int32).at[order].set(pos_sorted.astype(jnp.int32))
            valid = pos < CAP
            slot = jnp.where(valid, pos, CAP)
            buf = jnp.zeros((E, CAP + 1, H), x.dtype).at[flat_i, slot].set(x[token_ids])
            g = jnp.einsum('ech,ehi->eci', buf, w_gate)
            u = jnp.einsum('ech,ehi->eci', buf, w_up)
            y = jnp.einsum('eci,eih->ech', jax.nn.silu(g) * u, w_down)
            out_slots = y[flat_i, slot] * (flat_w * valid)[:, None]
            return out_slots.reshape(T, K, H).sum(axis=1)
        key = jax.random.key(seed)
        ks = jax.random.split(key, 8)
        f32 = jnp.float32
        return {'hidden_states': jax.random.normal(ks[0], (*T_TOKENS, H), f32), 'gate_w': jax.random.normal(ks[1], (E, H), f32) * SCALE, 'w_gate': jax.random.normal(ks[2], (E, H, I), f32) * SCALE, 'w_up': jax.random.normal(ks[3], (E, H, I), f32) * SCALE, 'w_down': jax.random.normal(ks[4], (E, I, H), f32) * SCALE, 'sw_gate': jax.random.normal(ks[5], (H, IS), f32) * SCALE, 'sw_up': jax.random.normal(ks[6], (H, IS), f32) * SCALE, 'sw_down': jax.random.normal(ks[7], (IS, H), f32) * SCALE}
    _L0_ffn_all = _L0_ffn_setup()
    _L0_ffn_in = {k: v for k, v in _L0_ffn_all.items() if k in ('gate_w', 'w_gate', 'w_up', 'w_down', 'sw_gate', 'sw_up', 'sw_down')}
    del _L0_ffn_all

    def _L1_cond_setup():
        import jax, jax.numpy as jnp
        from jax import lax
        import numpy as np
        B, T, C, TD = (8, 512, 512, 128)

        def _bi_wkv(r, k, v, w, u, time_emb):
            tf = jax.nn.sigmoid(jnp.sum(time_emb, axis=-1))[:, None, None]
            decay = jnp.exp(-jnp.exp(w.astype(jnp.float32)))[None, :] * (0.5 + 0.5 * tf[:, :, 0])
            kf = k.astype(jnp.float32)
            vf = v.astype(jnp.float32)
            ek = jnp.exp(jnp.minimum(kf, 30.0))
            ekv = ek * vf

            def step(carry, x):
                a, b = carry
                ekv_t, ek_t = x
                a = a * decay + ekv_t
                b = b * decay + ek_t
                return ((a, b), (a, b))
            ekv_t = jnp.swapaxes(ekv, 0, 1)
            ek_t = jnp.swapaxes(ek, 0, 1)
            init = (jnp.zeros_like(decay), jnp.zeros_like(decay))
            _, (nf, df) = lax.scan(step, init, (ekv_t, ek_t))
            _, (nb, db) = lax.scan(step, init, (ekv_t, ek_t), reverse=True)
            nf = jnp.swapaxes(nf, 0, 1)
            df = jnp.swapaxes(df, 0, 1)
            nb = jnp.swapaxes(nb, 0, 1)
            db = jnp.swapaxes(db, 0, 1)
            euk = jnp.exp(jnp.minimum(u.astype(jnp.float32)[None, None, :] + kf, 30.0))
            num = nf + nb - ekv + euk * vf
            den = df + db - ek + euk
            base = jax.nn.sigmoid(r.astype(jnp.float32)) * (num / jnp.maximum(den, 1e-08))
            out = base * (0.8 + 0.2 * tf)
            return out.astype(r.dtype)
        key = jax.random.key(seed)
        ks = jax.random.split(key, 6)
        return {'r': jax.random.normal(ks[0], (B, T, C), dtype=jnp.float32), 'k': jax.random.normal(ks[1], (B, T, C), dtype=jnp.float32), 'v': jax.random.normal(ks[2], (B, T, C), dtype=jnp.float32), 'w': jax.random.normal(ks[3], (C,), dtype=jnp.float32), 'u': jax.random.normal(ks[4], (C,), dtype=jnp.float32), 'time_emb': jax.random.normal(ks[5], (B, TD), dtype=jnp.float32)}
    _L1_cond_all = _L1_cond_setup()
    _L1_cond_in = {k: v for k, v in _L1_cond_all.items() if k in ('w', 'u')}
    del _L1_cond_all

    def _L1_ffn_setup():
        import jax, jax.numpy as jnp
        import numpy as np
        HIDDEN = 512
        INTER = 2048
        BATCH, LOCAL_SEQ = (2, 1024)
        key = jax.random.key(seed)
        k1, k2, k3 = jax.random.split(key, 3)
        h_shard = jax.random.normal(k1, (BATCH, LOCAL_SEQ, HIDDEN), dtype=jnp.float32)
        w_gate_up = jax.random.normal(k2, (2 * INTER, HIDDEN), dtype=jnp.float32) * 0.02
        w_down = jax.random.normal(k3, (HIDDEN, INTER), dtype=jnp.float32) * 0.02
        return {'h_shard': h_shard, 'w_gate_up': w_gate_up, 'w_down': w_down}
    _L1_ffn_all = _L1_ffn_setup()
    _L1_ffn_in = {k: v for k, v in _L1_ffn_all.items() if k in ('w_gate_up', 'w_down')}
    del _L1_ffn_all
    return {'x': x, 'fside_BxSxS_0': fside_BxSxS_0, 'cond_512': cond_512, 'L0_cond_w': _L0_cond_in['w'], 'L0_cond_u': _L0_cond_in['u'], 'L0_ffn_gate_w': _L0_ffn_in['gate_w'], 'L0_ffn_w_gate': _L0_ffn_in['w_gate'], 'L0_ffn_w_up': _L0_ffn_in['w_up'], 'L0_ffn_w_down': _L0_ffn_in['w_down'], 'L0_ffn_sw_gate': _L0_ffn_in['sw_gate'], 'L0_ffn_sw_up': _L0_ffn_in['sw_up'], 'L0_ffn_sw_down': _L0_ffn_in['sw_down'], 'L1_cond_w': _L1_cond_in['w'], 'L1_cond_u': _L1_cond_in['u'], 'L1_ffn_w_gate_up': _L1_ffn_in['w_gate_up'], 'L1_ffn_w_down': _L1_ffn_in['w_down']}

def reference(x, fside_BxSxS_0, cond_512, L0_cond_w, L0_cond_u, L0_ffn_gate_w, L0_ffn_w_gate, L0_ffn_w_up, L0_ffn_w_down, L0_ffn_sw_gate, L0_ffn_sw_up, L0_ffn_sw_down, L1_cond_w, L1_cond_u, L1_ffn_w_gate_up, L1_ffn_w_down):
    import jax
    import jax.numpy as jnp

    def _L0_cond_ref(r, k, v, w, u, time_emb):
        import jax, jax.numpy as jnp
        from jax import lax
        import numpy as np
        B, T, C, TD = (8, 512, 512, 128)

        def _bi_wkv(r, k, v, w, u, time_emb):
            tf = jax.nn.sigmoid(jnp.sum(time_emb, axis=-1))[:, None, None]
            decay = jnp.exp(-jnp.exp(w.astype(jnp.float32)))[None, :] * (0.5 + 0.5 * tf[:, :, 0])
            kf = k.astype(jnp.float32)
            vf = v.astype(jnp.float32)
            ek = jnp.exp(jnp.minimum(kf, 30.0))
            ekv = ek * vf

            def step(carry, x):
                a, b = carry
                ekv_t, ek_t = x
                a = a * decay + ekv_t
                b = b * decay + ek_t
                return ((a, b), (a, b))
            ekv_t = jnp.swapaxes(ekv, 0, 1)
            ek_t = jnp.swapaxes(ek, 0, 1)
            init = (jnp.zeros_like(decay), jnp.zeros_like(decay))
            _, (nf, df) = lax.scan(step, init, (ekv_t, ek_t))
            _, (nb, db) = lax.scan(step, init, (ekv_t, ek_t), reverse=True)
            nf = jnp.swapaxes(nf, 0, 1)
            df = jnp.swapaxes(df, 0, 1)
            nb = jnp.swapaxes(nb, 0, 1)
            db = jnp.swapaxes(db, 0, 1)
            euk = jnp.exp(jnp.minimum(u.astype(jnp.float32)[None, None, :] + kf, 30.0))
            num = nf + nb - ekv + euk * vf
            den = df + db - ek + euk
            base = jax.nn.sigmoid(r.astype(jnp.float32)) * (num / jnp.maximum(den, 1e-08))
            out = base * (0.8 + 0.2 * tf)
            return out.astype(r.dtype)
        return _bi_wkv(r, k, v, w, u, time_emb)

    def _L0_ffn_ref(hidden_states, gate_w, w_gate, w_up, w_down, sw_gate, sw_up, sw_down):
        import jax, jax.numpy as jnp
        import numpy as np
        E, K, H, I = (64, 6, 512, 352)
        NS = 2
        IS = NS * I
        CAP = 64
        T_TOKENS = (1, 256)
        SCALE = 0.02

        def _moe_infer(x, gate_w, w_gate, w_up, w_down):
            T = x.shape[0]
            TK = T * K
            logits = x @ gate_w.T
            scores = jax.nn.softmax(logits, axis=-1)
            topk_w, topk_i = jax.lax.top_k(scores, K)
            flat_i = topk_i.reshape(-1)
            flat_w = topk_w.reshape(-1)
            token_ids = jnp.arange(TK, dtype=jnp.int32) // K
            order = jnp.argsort(flat_i)
            sorted_e = flat_i[order]
            counts = jnp.bincount(flat_i, length=E)
            starts = jnp.concatenate([jnp.zeros((1,), counts.dtype), jnp.cumsum(counts)[:-1]])
            pos_sorted = jnp.arange(TK) - starts[sorted_e]
            pos = jnp.zeros((TK,), jnp.int32).at[order].set(pos_sorted.astype(jnp.int32))
            valid = pos < CAP
            slot = jnp.where(valid, pos, CAP)
            buf = jnp.zeros((E, CAP + 1, H), x.dtype).at[flat_i, slot].set(x[token_ids])
            g = jnp.einsum('ech,ehi->eci', buf, w_gate)
            u = jnp.einsum('ech,ehi->eci', buf, w_up)
            y = jnp.einsum('eci,eih->ech', jax.nn.silu(g) * u, w_down)
            out_slots = y[flat_i, slot] * (flat_w * valid)[:, None]
            return out_slots.reshape(T, K, H).sum(axis=1)
        orig_shape = hidden_states.shape
        x = hidden_states.reshape(-1, orig_shape[-1])
        y = _moe_infer(x, gate_w, w_gate, w_up, w_down).reshape(orig_shape)
        shared = jax.nn.silu(hidden_states @ sw_gate) * (hidden_states @ sw_up) @ sw_down
        return y + shared

    def _L1_cond_ref(r, k, v, w, u, time_emb):
        import jax, jax.numpy as jnp
        from jax import lax
        import numpy as np
        B, T, C, TD = (8, 512, 512, 128)

        def _bi_wkv(r, k, v, w, u, time_emb):
            tf = jax.nn.sigmoid(jnp.sum(time_emb, axis=-1))[:, None, None]
            decay = jnp.exp(-jnp.exp(w.astype(jnp.float32)))[None, :] * (0.5 + 0.5 * tf[:, :, 0])
            kf = k.astype(jnp.float32)
            vf = v.astype(jnp.float32)
            ek = jnp.exp(jnp.minimum(kf, 30.0))
            ekv = ek * vf

            def step(carry, x):
                a, b = carry
                ekv_t, ek_t = x
                a = a * decay + ekv_t
                b = b * decay + ek_t
                return ((a, b), (a, b))
            ekv_t = jnp.swapaxes(ekv, 0, 1)
            ek_t = jnp.swapaxes(ek, 0, 1)
            init = (jnp.zeros_like(decay), jnp.zeros_like(decay))
            _, (nf, df) = lax.scan(step, init, (ekv_t, ek_t))
            _, (nb, db) = lax.scan(step, init, (ekv_t, ek_t), reverse=True)
            nf = jnp.swapaxes(nf, 0, 1)
            df = jnp.swapaxes(df, 0, 1)
            nb = jnp.swapaxes(nb, 0, 1)
            db = jnp.swapaxes(db, 0, 1)
            euk = jnp.exp(jnp.minimum(u.astype(jnp.float32)[None, None, :] + kf, 30.0))
            num = nf + nb - ekv + euk * vf
            den = df + db - ek + euk
            base = jax.nn.sigmoid(r.astype(jnp.float32)) * (num / jnp.maximum(den, 1e-08))
            out = base * (0.8 + 0.2 * tf)
            return out.astype(r.dtype)
        return _bi_wkv(r, k, v, w, u, time_emb)

    def _L1_ffn_ref(h_shard, w_gate_up, w_down):
        import jax, jax.numpy as jnp
        import numpy as np
        HIDDEN = 512
        INTER = 2048
        BATCH, LOCAL_SEQ = (2, 1024)
        batch, local_seq, hidden = h_shard.shape
        gate_up = jnp.einsum('bsh,oh->bso', h_shard, w_gate_up)
        gate, up = jnp.split(gate_up, 2, axis=-1)
        h = jax.nn.silu(gate) * up
        out = jnp.einsum('bsi,hi->bsh', h, w_down)
        return out
    x = x + _L0_ffn_ref(_L0_cond_ref(x, fside_BxSxS_0, fside_BxSxS_0, L0_cond_w, L0_cond_u, cond_512), L0_ffn_gate_w, L0_ffn_w_gate, L0_ffn_w_up, L0_ffn_w_down, L0_ffn_sw_gate, L0_ffn_sw_up, L0_ffn_sw_down)
    x = x + _L1_ffn_ref(_L1_cond_ref(x, fside_BxSxS_0, fside_BxSxS_0, L1_cond_w, L1_cond_u, cond_512), L1_ffn_w_gate_up, L1_ffn_w_down)
    return x

_drawn_inputs = setup_inputs


def setup_inputs(seed=0):
    import zlib

    import numpy as np

    out = dict(_drawn_inputs(seed))
    spreads = {}
    factors = {'fside_BxSxS_0': 2.667,
     'cond_512': 8.0,
     'L0_cond_w': 8.0,
     'L0_cond_u': 8.0,
     'L0_ffn_gate_w': 8.0,
     'L0_ffn_w_gate': 8.0,
     'L0_ffn_w_up': 8.0,
     'L0_ffn_w_down': 8.0,
     'L0_ffn_sw_gate': 4.896,
     'L0_ffn_sw_up': 4.919,
     'L0_ffn_sw_down': 4.875,
     'L1_cond_w': 4.892,
     'L1_cond_u': 8.0,
     'L1_ffn_w_gate_up': 2.783,
     'L1_ffn_w_down': 2.749}
    for name, (base, spread) in spreads.items():
        noise = np.random.default_rng([zlib.crc32(name.encode()), seed]).standard_normal(out[name].shape)
        drawn = base * np.exp(spread * noise) if base else spread * noise
        out[name] = jnp.asarray(drawn.astype(out[name].dtype))
    for name, factor in factors.items():
        out[name] = (out[name] * factor).astype(out[name].dtype)
    return out
```

```python
from contextlib import ExitStack

import concourse.bass as bass
from concourse import mybir

P = 128
ALU = mybir.AluOpType
ACT = mybir.ActivationFunctionType
AX_X = mybir.AxisListType.X
F32 = mybir.dt.float32
F32R = mybir.dt.float32r
U32 = mybir.dt.uint32

EXP_CAP = 30.0
DEN_FLOOR = 1e-8
TOPK = 6
CAP = 64
DMA = 16


class Expert:

    def __init__(self, i, off):
        self.i, self.off = i, off

    def __add__(self, d):
        return Expert(self.i, self.off + d)

    @property
    def n(self):
        return self.i * 4 + self.off

    @property
    def pair(self):
        return self.i * 2 + self.off // 2

    @property
    def slot2(self):
        return self.off % 2

    @property
    def slot4(self):
        return self.off % 4

    @property
    def fours(self):
        return self.i + self.off // 4


def adaln_ffn_kernel(nc, x_t, side_t, x_rows, cond, wkv_w, wkv_u, gate_w, moe_gu, moe_down,
                     shared_gu, shared_down, ffn_w, ident, expert_iota, pair_expert, token_key,
                     slot_col, out):
    B, _, BT = x_t.shape
    NJ = 4
    T = BT // NJ
    C = NJ * P
    NT = B * T
    TT = T // P
    E = gate_w.shape[2]
    XR = C + E
    I = moe_down.shape[1]
    GUW = NJ * 2 * I
    KT = [(k, min(P, I - k * P)) for k in range((I + P - 1) // P)]
    DNW = len(KT) * C
    SGW = shared_gu.shape[2]
    SM = shared_down.shape[0] // P + 1
    SLAST = shared_down.shape[0] - (SM - 1) * P
    NF = ffn_w.shape[0]
    FGU = NJ * 2 * P
    assert FGU + C == DNW and NF == 16 and E == 64 and B == 4 and TT == 4

    x0_rows = nc.dram_tensor("x0_rows", (NT, XR), F32, kind="Internal").ap()
    acc = nc.dram_tensor("acc_rows", (NT + CAP, C), F32, kind="Internal").ap()

    with ExitStack() as ctx:
        def sb(name, shape, dt=F32, stack=ctx):
            return stack.enter_context(nc.sbuf_tensor(name, shape, dt))

        bank = [ctx.enter_context(nc.psum_tensor(f"bank{n}", [P, 512], F32)) for n in range(8)]
        gate_bank, up_bank = (bank[4], bank[6]), (bank[5], bank[7])
        row_bank = (bank[3], bank[0])

        idt, iota_e, pair_e = sb("idt", [P, P]), sb("iota_e", [P, E]), sb("pair_e", [P, E // 2])
        key_col, scol = sb("key_col", [P, NT // P]), sb("scol", [CAP, 1])
        gate_sb = sb("gate_sb", [P, NJ * E])
        w_sb, u_sb = sb("w_sb", [P, 2 * NJ]), sb("u_sb", [P, 2 * NJ])
        cond_sb = sb("cond_sb", [P, B, P])
        tf, half_tf, out_scale = sb("tf", [P, B]), sb("half_tf", [P, B]), sb("out_scale", [P, B])
        dec0 = sb("dec0", [P, 2 * NJ])
        decay = sb("decay", [P, 2 * B * NJ])

        side_sb, x_sb = sb("side_sb", [P, 2, T]), sb("x_sb", [P, 2, T])
        ek, eu = sb("ek", [P, T]), sb("eu", [P, T])
        one_en = sb("one_en", [P, T])
        ekv, dv = sb("ekv", [P, T]), sb("dv", [P, T])
        den, den_b = sb("den", [P, T]), sb("den_b", [P, T])
        num, num_b = sb("num", [P, T]), sb("num_b", [P, T])
        wkv_out = sb("wkv_out", [P, NJ * T])

        gu_raw, dn_raw = sb("gu_raw", [P, 4 * GUW]), sb("dn_raw", [P, 4, DNW])
        gidx, sidx = sb("gidx", [P, E // 2], U32), sb("sidx", [CAP, E], U32)
        gidx_now, sidx_now = sb("gidx_now", [P, 2], U32), sb("sidx_now", [CAP, 2], U32)
        xg = sb("xg", [P, 2, XR])

        with ExitStack() as early:
            sgu = sb("sgu", [P, NJ, SGW], stack=early)
            x0 = sb("x0", [P, NJ * T], stack=early)
            xrow = sb("xrow", [P, TT, XR], stack=early)
            nmax, psums = sb("nmax", [P, TT], stack=early), sb("psums", [P, TT], stack=early)
            prec, pexp = sb("prec", [P, TT], stack=early), sb("pexp", [P, TT, E], stack=early)
            top8, top8_i = sb("top8", [P, TT, 8], stack=early), sb("top8_i", [P, TT, 8], U32, early)
            top8_f = sb("top8_f", [P, TT, 8], stack=early)
            onehot = sb("onehot", [P, TT, TOPK, E], stack=early)
            mkey = sb("mkey", [P, TT, E], stack=early)
            keys = sb("keys", [E, NT], stack=early)
            slot_key = sb("slot_key", [E, CAP], stack=early)
            tok_f, empty_f = sb("tok_f", [CAP, E], stack=early), sb("empty_f", [CAP, E], stack=early)
            sdn = sb("sdn", [P, SM, C], stack=early)
            h_sh, silu_sh = sb("h_sh", [P, SM, T], stack=early), sb("silu_sh", [P, T], stack=early)
            xres, y_sh = sb("xres", [P, 2, C], stack=early), sb("y_sh", [P, 2, C], stack=early)
        gu_hi, gu_lo = sb("gu_hi", [P, 2 * GUW], F32R), sb("gu_lo", [P, 2 * GUW], F32R)
        dn_hi, dn_lo = sb("dn_hi", [P, 2, DNW], F32R), sb("dn_lo", [P, 2, DNW], F32R)
        xs_hi, xs_lo = sb("xs_hi", [P, 4, NJ, CAP], F32R), sb("xs_lo", [P, 4, NJ, CAP], F32R)
        wsel, w_pair, w_odd = sb("wsel", [P, E]), sb("w_pair", [P, 2]), sb("w_odd", [CAP, 2])
        silu_e, h_e = sb("silu_e", [CAP, 2, I]), sb("h_e", [CAP, 2, I])
        hs_hi, hs_lo = sb("hs_hi", [P, 2, len(KT) * CAP], F32R), sb("hs_lo", [P, 2, len(KT) * CAP], F32R)
        y_e = sb("y_e", [CAP, 2, C])
        CH = NJ * T
        xa, sig, x1t, o_sb = (gu_raw[:, n * CH:(n + 1) * CH] for n in range(4))
        fh = [gu_raw[:, 4 * CH + n * T:4 * CH + (n + 1) * T] for n in range(2)]
        fsilu = [gu_raw[:, 4 * CH + (2 + n) * T:4 * CH + (3 + n) * T] for n in range(2)]
        x1_hi, x1_lo = gu_hi[:, 0:CH], gu_lo[:, 0:CH]
        fh_hi = [gu_hi[:, CH + n * T:CH + (n + 1) * T] for n in range(2)]
        fh_lo = [gu_lo[:, CH + n * T:CH + (n + 1) * T] for n in range(2)]

        S = {name: ctx.enter_context(nc.semaphore(name)) for name in ("cond_in const_in sgu_in sdn_in csum_done tf_ready exp_w_done dec0_ready fac_ready "
                     "k_ready e_ready en_done t_ready wkv_ready wkv_chain x0_ready logits_done "
                     "tok_t_done xrow_copied xrow_sent nmax_done nmax_ready pexp_ready p_ready route_chain "
                     "mask_ready mask_t_done keys_ready sh_gu_done sh_silu_ready sh_d_done dummy_in "
                     "round_chain slots_ready slots_t_done idx_chain idx_ready dn_pad bank_pad "
                     "gu_hi_ready gu_lo_ready dn_hi_ready dn_lo_ready xt_done xs_hi_ready xs_lo_ready "
                     "wsel_done wslot_ready gu_done e_silu_ready h_ready ht_done hs_hi_ready hs_lo_ready "
                     "d_done y_ready added gcol_first gcol_ready scol_ready top8_ready "
                     "side_e_in w_gu_hi_ready w_dn_hi_ready xa_in xa_t_done x1t_ready sig_ready x1_ready "
                     "x1_hi_ready x1_lo_ready out_ready out_sent").split()}

        def ring(name, n):
            return [ctx.enter_context(nc.semaphore(f"{name}{k}")) for k in range(n)]

        side_in, side_used, x_in, x_used = ring("side_in", 2), ring("side_used", 2), ring("x_in", 2), ring("x_used", 2)
        sh_h_ready, sh_y_ready, y_sent, xres_in = ring("sh_h_ready", 2), ring("sh_y_ready", 4), ring("y_sent", 4), ring("xres_in", 2)
        gu_in, dn_in, xg_in = ring("gu_in", 4), ring("dn_in", 4), ring("xg_in", 2)
        w_in, w_gu_lo, w_dn_lo = ring("w_in", 4), ring("w_gu_lo", 4), ring("w_dn_lo", 4)
        f_gu_done, f_silu, f_h, f_hi, f_lo, f_d_done = (
            ring(n, 2) for n in ("f_gu_done", "f_silu", "f_h", "f_hi", "f_lo", "f_d_done"))
        N_CONST = 8

        def cut(buf, start, size):
            return buf[:, start:start + size] if isinstance(start, int) else buf[:, bass.ds(start, size)]

        def gu_slot(buf, s):
            return buf[:, s * GUW:(s + 1) * GUW]

        block = ctx.enter_context(nc.Block())

        @block.sync
        def _(sp):
            sp.dma_start(cond_sb[:, :, :], cond.rearrange("(o b) t -> o b t", o=1).to_broadcast([P, B, P])).then_inc(S["cond_in"], DMA)
            for dst, src in ((w_sb[:, :], wkv_w), (u_sb[:, :], wkv_u), (idt[:, :], ident), (iota_e[:, :], expert_iota),
                             (pair_e[:, :], pair_expert), (key_col[:, :], token_key), (scol[:, :], slot_col),
                             (gate_sb[:, :], gate_w.rearrange("p j e -> p (j e)"))):
                sp.dma_start(dst, src).then_inc(S["const_in"], DMA)

            def load_side(b, j, slot, use):
                sp.wait_ge(side_used[slot], use)
                sp.dma_start(side_sb[:, slot, :], cut(side_t[b], j * T, T)).then_inc(side_in[slot], DMA)

            def load_batch(b):
                for j in range(NJ):
                    load_side(b, j, j % 2, b * 2 + j // 2)
                    sp.wait_ge(x_used[j % 2], b * 2 + j // 2)
                    sp.dma_start(x_sb[:, j % 2, :], cut(x_t[b], j * T, T)).then_inc(x_in[j % 2], DMA)

            load_batch(0)
            sp.dma_start(sgu[:, :, :], shared_gu).then_inc(S["sgu_in"], DMA)
            sp.dma_start(sdn[:, 0:SM - 1, :], shared_down[0:(SM - 1) * P, :].rearrange("(k p) c -> p k c", p=P)).then_inc(S["sdn_in"], DMA)
            sp.dma_start(sdn[0:SLAST, SM - 1, :], shared_down[(SM - 1) * P:, :]).then_inc(S["sdn_in"], DMA)
            with sp.Fori(1, B) as b:
                load_batch(b)

            def load_expert(e):
                s = e.slot4
                sp.dma_start(gu_slot(gu_raw, s), moe_gu[e.n]).then_inc(gu_in[s], DMA)
                sp.dma_start(dn_raw[:, s, 0:2 * C].rearrange("p (k c) -> p k c", k=2),
                             moe_down[e.n][0:2 * P, :].rearrange("(k p) c -> p k c", p=P)).then_inc(dn_in[s], DMA)
                sp.dma_start(dn_raw[0:I - 2 * P, s, 2 * C:3 * C], moe_down[e.n][2 * P:I, :]).then_inc(dn_in[s], DMA)

            sp.wait_ge(S["dn_pad"], 1)
            for off in range(4):
                load_expert(Expert(0, off))
            for j in range(NJ):
                load_side(0, j, 0, 2 * B + j)
            with sp.Fori(1, E // 4) as i:
                for off in range(4):
                    e = Expert(i, off)
                    sp.wait_ge(S["gu_lo_ready"], e.n - 3)
                    sp.wait_ge(S["dn_lo_ready"], e.n - 3)
                    load_expert(e)

            sp.wait_ge(S["dn_lo_ready"], E)
            sp.wait_ge(S["gu_lo_ready"], E)
            with sp.Fori(0, B) as c:
                with sp.Fori(0, NF // 4) as g:
                    for r in range(4):
                        sp.wait_ge(w_dn_lo[r], c * 4 + g)
                        sp.dma_start(dn_raw[:, r, :], ffn_w[g * 4 + r]).then_inc(w_in[r], DMA)

        @block.gpsimd
        def _(pool):
            pool.memset(dn_raw[96:P, :, 2 * C:3 * C], 0.0).then_inc(S["dn_pad"], 1)
            pool.dma_start(acc[NT:NT + CAP, :], x_rows[0:CAP, :]).then_inc(S["dummy_in"], DMA)

            def rows(t, b, tt):
                return t[bass.ds(b * T + tt * P, P), :]

            def load_residual(b, tt):
                s = tt % 2
                pool.wait_ge(S["dn_pad"], 1)
                pool.wait_ge(sh_y_ready[(tt + 2) % 4], b + tt // 2)
                pool.dma_start(xres[:, s, :], rows(x_rows, b, tt)).then_inc(xres_in[s], DMA)

            def store_rows(b, tt):
                s = tt % 2
                pool.wait_ge(S["dn_pad"], 1)
                pool.wait_ge(sh_y_ready[tt], b + 1)
                pool.dma_start(rows(acc, b, tt), y_sh[:, s, :]).then_inc(y_sent[tt], DMA)

            with pool.Fori(0, B) as b:
                load_residual(b, 0)
                load_residual(b, 1)
                pool.wait_ge(S["dn_pad"], 1)
                pool.wait_ge(S["xrow_copied"], b * TT + TT)
                pool.wait_ge(S["p_ready"], b + 1)
                pool.dma_start(x0_rows[bass.ds(b * T, T), :].rearrange("(t p) c -> p t c", p=P),
                               xrow[:, :, :]).then_inc(S["xrow_sent"], DMA)
                store_rows(b, 0)
                load_residual(b, 2)
                store_rows(b, 1)
                load_residual(b, 3)
                store_rows(b, 2)
                store_rows(b, 3)

            def gather(e, first=False):
                q, s = e.pair, (e.off // 2) % 2
                use = e.fours
                pool.wait_ge(S["idx_ready"], 1)
                if not first:
                    pool.wait_ge(S["xt_done"], q - 1)
                    pool.wait_ge(S["wslot_ready"], q - 1)
                    pool.wait_ge(xg_in[s], use * DMA)
                pool.tensor_copy(gidx_now[:, s:s + 1], cut(gidx, q, 1)).then_inc(S["gcol_first"] if first else S["gcol_ready"], 1)
                pool.wait_ge(S["xrow_sent"], B * DMA)
                pool.wait_ge(S["gcol_first"] if first else S["gcol_ready"], q + 1 if first else q - 1)
                pool.indirect_dma_start(xg[:, s, :], None, x0_rows,
                                        bass.IndirectOffsetOnAxis(ap=gidx_now[:, s:s + 1], axis=0)).then_inc(xg_in[s], DMA)

            def scatter(e, first=False):
                s = e.slot2
                pool.wait_ge(S["idx_ready"], 1)
                pool.wait_ge(S["y_ready"], e.n + 1)
                if not first:
                    pool.wait_ge(S["added"], e.n * DMA)
                pool.tensor_copy(sidx_now[:, s:s + 1], cut(sidx, e.n, 1)).then_inc(S["scol_ready"], 1)
                pool.wait_ge(S["idx_ready"], 1)
                pool.wait_ge(S["scol_ready"], e.n + 1)
                pool.indirect_dma_start(acc, bass.IndirectOffsetOnAxis(ap=sidx_now[:, s:s + 1], axis=0),
                                        y_e[:, s, :], None, compute_op=ALU.add).then_inc(S["added"], DMA)

            gather(Expert(0, 0), first=True)
            gather(Expert(0, 2), first=True)
            for tt in range(TT):
                pool.wait_ge(y_sent[tt], B * DMA)
            pool.wait_ge(S["dummy_in"], DMA)

            def step(e, gathers=True, scatters=True):
                if gathers and e.off % 2 == 0:
                    gather(e + 4)
                if scatters:
                    scatter(e + -2, first=isinstance(e.i, int) and e.off == 2)

            for off in range(4):
                step(Expert(0, off), scatters=off >= 2)
            with pool.Fori(1, E // 4 - 1) as i:
                for off in range(4):
                    step(Expert(i, off))
            for off in range(4):
                step(Expert(0, E - 4 + off), gathers=False)
            for off in range(2):
                step(Expert(0, E + off), gathers=False)

            def load_sums(c):
                pool.wait_ge(S["gu_lo_ready"], E)
                pool.wait_ge(S["added"], E * DMA)
                pool.wait_ge(S["xa_t_done"], c * NJ)
                pool.dma_start(xa.rearrange("p (t c) -> p t c", t=TT),
                               acc[bass.ds(c * T, T), :].rearrange("(t p) c -> p t c", p=P)).then_inc(S["xa_in"], DMA)

            def load_side_e(c, j):
                pool.wait_ge(S["dn_pad"], 1)
                pool.wait_ge(side_used[0], (c + 2) * NJ + j)
                pool.dma_start(side_sb[:, 0, :], cut(side_t[c], j * T, T)).then_inc(S["side_e_in"], DMA)

            def store_out(c):
                pool.wait_ge(S["dn_pad"], 1)
                pool.wait_ge(S["out_ready"], c * NJ + NJ)
                pool.dma_start(out[c], o_sb).then_inc(S["out_sent"], DMA)

            load_sums(0)
            with pool.Fori(0, B - 1) as c:
                for j in range(NJ):
                    load_side_e(c + 1, j)
                load_sums(c + 1)
                store_out(c)
            store_out(B - 1)
            pool.wait_ge(S["out_sent"], B * DMA)

        @block.scalar
        def _(act):
            act.wait_ge(S["csum_done"], 1)
            act.activation(tf[:, :], tf[:, :], ACT.Sigmoid).then_inc(S["tf_ready"], 1)
            act.wait_ge(S["const_in"], N_CONST * DMA)
            act.activation(w_sb[:, :], w_sb[:, :], ACT.Exp).then_inc(S["exp_w_done"], 1)
            act.wait_ge(S["exp_w_done"], 1)
            act.activation(dec0[:, :], w_sb[:, :], ACT.Exp, scale=-1.0).then_inc(S["dec0_ready"], 1)

            def exps(unit):
                act.wait_ge(S["k_ready"], unit + 1)
                act.activation(ek[:, :], ek[:, :], ACT.Exp)
                act.activation(eu[:, :], eu[:, :], ACT.Exp).then_inc(S["e_ready"], 1)

            def gate_r(b, j):
                unit = b * NJ + j
                act.wait_ge(x_in[j % 2], (b * 2 + j // 2 + 1) * DMA)
                act.wait_ge(S["wkv_ready"], unit)
                act.activation(one_en[:, :], x_sb[:, j % 2, :], ACT.Exp, scale=-1.0).then_inc(x_used[j % 2], 1)
                act.wait_ge(x_used[j % 2], b * 2 + j // 2 + 1)
                act.activation(one_en[:, :], one_en[:, :], ACT.Copy, bias=1.0).then_inc(S["t_ready"], 1)

            def softmax_exp(b):
                act.wait_ge(S["nmax_ready"], b + 1)
                act.wait_ge(S["p_ready"], b)
                for tt in range(TT):
                    ins = act.activation(pexp[:, tt, :], bank[0][:, tt * E:(tt + 1) * E], ACT.Exp,
                                         bias=nmax[:, tt:tt + 1], accum_out=psums[:, tt:tt + 1])
                ins.then_inc(S["pexp_ready"], 1)

            def copy_rows(b):
                act.wait_ge(S["xrow_sent"], b * DMA)
                for tt in range(TT):
                    act.wait_ge(S["tok_t_done"], b * TT + tt + 1)
                    act.activation(xrow[:, tt, 0:C], bank[1][:, :], ACT.Copy).then_inc(S["xrow_copied"], 1)

            def shared_silu(b, m):
                rows = P if m < SM - 1 else SLAST
                act.wait_ge(S["sh_gu_done"], b * SM + m + 1)
                act.wait_ge(sh_h_ready[(m + 1) % 2], b * (SM // 2) + (m + 1) // 2)
                act.activation(silu_sh[0:rows, :], gate_bank[m % 2][0:rows, :], ACT.Silu).then_inc(S["sh_silu_ready"], 1)

            def copy_keys(b):
                act.wait_ge(S["mask_t_done"], b + 1)
                act.activation(cut(keys, b * T, T), bank[2][0:E, :], ACT.Copy).then_inc(S["keys_ready"], 1)

            def hand_on_x0(b, first):
                act.wait_ge(S["wkv_ready"], b * NJ + NJ)
                if not first:
                    act.wait_ge(S["sh_gu_done"], b * SM)
                act.activation(x0[:, :], wkv_out[:, :], ACT.Copy).then_inc(S["x0_ready"], 1)

            def early_step(s, wkv, shared):
                if shared:
                    softmax_exp(s - 1)
                    copy_rows(s - 1)
                for j in range(NJ):
                    if wkv:
                        exps(s * NJ + j)
                        gate_r(s, j)
                    if shared and j < SM // 2:
                        shared_silu(s - 1, 2 * j)
                        shared_silu(s - 1, 2 * j + 1)
                    if shared and j == 0:
                        copy_keys(s - 1)
                if wkv:
                    hand_on_x0(s, not shared)

            early_step(0, True, False)
            with act.Fori(1, B) as s:
                early_step(s, True, True)
            early_step(B, False, True)

            for j in range(NJ):
                exps(B * NJ + j)

            def split_hi_gu(e):
                act.wait_ge(gu_in[e.slot4], (e.fours + 1) * DMA)
                act.activation(gu_slot(gu_hi, e.slot2), gu_slot(gu_raw, e.slot4), ACT.Copy).then_inc(S["gu_hi_ready"], 1)

            def split_hi_dn(e, first):
                act.wait_ge(dn_in[e.slot4], (e.fours + 1) * 2 * DMA)
                if not first:
                    act.wait_ge(S["d_done"], e.n - 1)
                act.activation(dn_hi[:, e.slot2, :], dn_raw[:, e.slot4, :], ACT.Copy).then_inc(S["dn_hi_ready"], 1)

            def tokens_hi(e):
                s = e.slot4
                act.wait_ge(S["xt_done"], e.pair + 1)
                act.activation(xs_hi[:, s:s + 2, :, :].rearrange("p s j t -> p j s t"),
                               bank[1][:, :].rearrange("p (j s t) -> p j s t", j=NJ, s=2), ACT.Copy).then_inc(S["xs_hi_ready"], 1)

            def step(e, silu=True, hs=True, xs=True, gu=True, dn=True, y=True, first=False):
                if silu:
                    act.wait_ge(S["gu_done"], e.n + 1)
                    if not first:
                        act.wait_ge(S["h_ready"], e.n - 1)
                    act.activation(silu_e[:, e.slot2, :], gate_bank[e.slot2][0:CAP, 0:I], ACT.Silu).then_inc(S["e_silu_ready"], 1)
                if hs:
                    d = e + -1
                    act.wait_ge(S["ht_done"], d.n + 1)
                    if not (isinstance(e.i, int) and d.off < 2):
                        act.wait_ge(S["d_done"], d.n - 1)
                    act.activation(hs_hi[:, d.slot2, :], bank[2][:, 0:len(KT) * CAP], ACT.Copy).then_inc(S["hs_hi_ready"], 1)
                if xs and e.off % 2 == 0:
                    tokens_hi(e + 2)
                if gu:
                    split_hi_gu(e + 2)
                if dn:
                    split_hi_dn(e, first)
                if y:
                    d = e + -2
                    act.wait_ge(S["d_done"], d.n + 1)
                    if not (isinstance(e.i, int) and d.off < 2):
                        act.wait_ge(S["added"], (d.n - 1) * DMA)
                    act.activation(y_e[:, d.slot2, :], row_bank[d.slot2][0:CAP, :], ACT.Copy).then_inc(S["y_ready"], 1)

            act.wait_ge(S["sh_d_done"], B * TT)
            act.wait_ge(S["xrow_sent"], B * DMA)
            act.wait_ge(S["idx_ready"], 1)
            for tt in range(TT):
                act.wait_ge(y_sent[tt], B * DMA)
            tokens_hi(Expert(0, 0))
            split_hi_gu(Expert(0, 0))
            split_hi_gu(Expert(0, 1))
            for off in range(4):
                step(Expert(0, off), hs=off >= 1, y=off >= 2, first=off < 2)
            with act.Fori(1, E // 4 - 1) as i:
                for off in range(4):
                    step(Expert(i, off))
            for off in range(4):
                step(Expert(0, E - 4 + off), xs=off < 2, gu=off < 2)
            step(Expert(0, E), silu=False, xs=False, gu=False, dn=False)
            step(Expert(0, E + 1), silu=False, hs=False, xs=False, gu=False, dn=False)

            def f_split_hi_gu(c, n):
                g, r = n
                act.wait_ge(w_in[r], (c * 4 + g + 1) * DMA)
                act.wait_ge(f_gu_done[r % 2], c * 8 + g * 2 + r // 2)
                act.activation(dn_hi[:, r % 2, 0:FGU], dn_raw[:, r, 0:FGU], ACT.Copy).then_inc(S["w_gu_hi_ready"], 1)

            def f_step(c, g, r, nxt):
                half = c * 8 + g * 2 + r // 2
                if nxt is not None:
                    f_split_hi_gu(*nxt)
                act.wait_ge(f_d_done[r % 2], half)
                act.activation(dn_hi[:, r % 2, FGU:], dn_raw[:, r, FGU:], ACT.Copy).then_inc(S["w_dn_hi_ready"], 1)
                act.wait_ge(f_gu_done[r % 2], half + 1)
                act.wait_ge(f_h[r % 2], half)
                act.activation(fsilu[r % 2], gate_bank[r % 2][:, :], ACT.Silu).then_inc(f_silu[r % 2], 1)
                act.wait_ge(f_h[r % 2], half + 1)
                act.activation(fh_hi[r % 2], fh[r % 2], ACT.Copy).then_inc(f_hi[r % 2], 1)

            def f_group(c, g, wkv, last=False):
                for r in range(4):
                    nxt = (c, (g, r + 1)) if r < 3 else (None if last else (c, (g + 1, 0)))
                    f_step(c, g, r, nxt)
                    if wkv and r == 0:
                        exps((B + 1 + c) * NJ + g)

            def f_chunk(c, wkv, last=False):
                for j in range(NJ):
                    act.wait_ge(S["xa_t_done"], c * NJ + j + 1)
                    act.activation(sig[:, j * T:(j + 1) * T], bank[4 + j][:, :], ACT.Sigmoid).then_inc(S["sig_ready"], 1)
                act.wait_ge(S["out_ready"], c * NJ)
                for j in range(NJ):
                    act.activation(x1t[:, j * T:(j + 1) * T], bank[4 + j][:, :], ACT.Copy).then_inc(S["x1t_ready"], 1)
                for j in range(NJ):
                    act.wait_ge(S["x1_ready"], c * NJ + j + 1)
                    act.activation(x1_hi[:, j * T:(j + 1) * T], sig[:, j * T:(j + 1) * T], ACT.Copy).then_inc(S["x1_hi_ready"], 1)
                f_group(c, 0, wkv)
                with act.Fori(1, NF // 4 - 1) as g:
                    f_group(c, g, wkv)
                f_group(c, NF // 4 - 1, wkv, last)

            act.wait_ge(S["d_done"], E)
            act.wait_ge(S["gu_done"], E)
            f_split_hi_gu(0, (0, 0))
            with act.Fori(0, B - 1) as c:
                f_chunk(c, True)
            f_chunk(B - 1, False, last=True)

        @block.vector
        def _(vec):
            V = nc.vector

            class Chain:

                def __init__(self, sem):
                    self.sem, self.base, self.n = sem, 0, 0

                def __call__(self, ins):
                    ins.then_inc(self.sem, 1)
                    self.n += 1

                def wait(self):
                    vec.wait_ge(self.sem, self.base + self.n)

            vec.wait_ge(S["cond_in"], DMA)
            V.tensor_reduce(tf[:, :], cond_sb[:, :, :], AX_X, ALU.add).then_inc(S["csum_done"], 1)
            vec.wait_ge(S["tf_ready"], 1)
            V.tensor_scalar(half_tf[:, :], tf[:, :], 0.5, 0.5, ALU.mult, ALU.add).then_inc(S["fac_ready"], 1)
            V.tensor_scalar(out_scale[:, :], tf[:, :], 0.2, 0.8, ALU.mult, ALU.add).then_inc(S["fac_ready"], 1)
            vec.wait_ge(S["dec0_ready"], 1)
            vec.wait_ge(S["fac_ready"], 2)
            for layer in range(2):
                for b in range(B):
                    V.tensor_scalar(decay[:, (layer * B + b) * NJ:(layer * B + b + 1) * NJ],
                                    dec0[:, layer * NJ:(layer + 1) * NJ], half_tf[:, b:b + 1], None,
                                    ALU.mult).then_inc(S["fac_ready"], 1)

            wkv = Chain(S["wkv_chain"])
            WKV_OPS = 11

            def wkv_clamp(layer, b, j, slot, arrived, use):
                wkv.wait()
                vec.wait_ge(S["wkv_ready"], (layer * B + b) * NJ + j)
                vec.wait_ge(arrived, (use + 1) * DMA)
                wkv(V.tensor_scalar(ek[:, :], side_sb[:, slot, :], EXP_CAP, None, ALU.min))
                V.tensor_scalar(eu[:, :], side_sb[:, slot, :], cut(u_sb, j + layer * NJ, 1), EXP_CAP,
                                ALU.add, ALU.min).then_inc(S["k_ready"], 1)

            def wkv_den(layer, b, j, slot):
                dec = cut(decay, (layer * B + b) * NJ + j, 1).to_broadcast([P, T])
                vec.wait_ge(S["e_ready"], (layer * B + b) * NJ + j + 1)
                wkv(V.tensor_tensor(ekv[:, :], ek[:, :], side_sb[:, slot, :], ALU.mult))
                wkv(V.tensor_tensor(eu[:, :], eu[:, :], ek[:, :], ALU.subtract))
                wkv(V.tensor_tensor_scan(den[:, :], dec, ek[:, :], 0.0, ALU.mult, ALU.add))
                wkv(V.tensor_tensor_scan(den_b[:, T - 1::-1], dec, ek[:, T - 1::-1], 0.0, ALU.mult, ALU.add))

            def wkv_num(layer, b, j, slot):
                dec = cut(decay, (layer * B + b) * NJ + j, 1).to_broadcast([P, T])
                wkv.wait()
                V.tensor_tensor(dv[:, :], eu[:, :], side_sb[:, slot, :], ALU.mult).then_inc(side_used[slot], 1)
                wkv(V.tensor_tensor_scan(num[:, :], dec, ekv[:, :], 0.0, ALU.mult, ALU.add))
                wkv(V.tensor_tensor_scan(num_b[:, T - 1::-1], dec, ekv[:, T - 1::-1], 0.0, ALU.mult, ALU.add))
                wkv(V.tensor_tensor(den[:, :], den[:, :], den_b[:, :], ALU.add))

            def wkv_ratio(layer, b, j):
                wkv.wait()
                V.tensor_tensor(num[:, :], num[:, :], num_b[:, :], ALU.add)
                wkv(V.tensor_tensor(den[:, :], den[:, :], eu[:, :], ALU.add))
                wkv.wait()
                V.tensor_tensor(num[:, :], num[:, :], dv[:, :], ALU.add)
                if layer == 0:
                    vec.wait_ge(S["t_ready"], b * NJ + j + 1)
                    wkv(V.scalar_tensor_tensor(out=den[:, :], in0=den[:, :], scalar=DEN_FLOOR, in1=one_en[:, :],
                                               op0=ALU.max, op1=ALU.mult))
                else:
                    wkv(V.tensor_scalar(den[:, :], den[:, :], DEN_FLOOR, None, ALU.max))
                wkv.wait()
                wkv(V.reciprocal(den_b[:, :], den[:, :]))
                wkv.wait()
                V.scalar_tensor_tensor(out=cut(wkv_out, j * T, T), in0=num[:, :], scalar=cut(out_scale, b, 1),
                                       in1=den_b[:, :], op0=ALU.mult, op1=ALU.mult).then_inc(S["wkv_ready"], 1)

            def route(b):
                vec.wait_ge(S["logits_done"], b + 1)
                V.tensor_reduce(nmax[:, :], bank[0][:, 0:TT * E].rearrange("p (t e) -> p t e", e=E), AX_X,
                                ALU.max).then_inc(S["nmax_done"], 1)
                vec.wait_ge(S["nmax_done"], b + 1)
                V.tensor_scalar(nmax[:, :], nmax[:, :], -1.0, None, ALU.mult).then_inc(S["nmax_ready"], 1)
                vec.wait_ge(S["pexp_ready"], b + 1)
                chain = S["route_chain"]
                OPS = 5
                V.reciprocal(prec[:, :], psums[:, :]).then_inc(chain, 1)
                vec.wait_ge(S["xrow_sent"], b * DMA)
                vec.wait_ge(chain, b * OPS + 1)
                for tt in range(TT):
                    ins = V.tensor_scalar(xrow[:, tt, C:XR], pexp[:, tt, :], prec[:, tt:tt + 1], None, ALU.mult)
                ins.then_inc(S["p_ready"], 1)
                vec.wait_ge(S["dec0_ready"], 1)
                vec.wait_ge(S["p_ready"], b + 1)
                for tt in range(TT):
                    ins = V.max(top8[:, tt, :], xrow[:, tt, C:XR])
                ins.then_inc(S["top8_ready"], 1)
                vec.wait_ge(S["dec0_ready"], 1)
                vec.wait_ge(S["top8_ready"], b + 1)
                for tt in range(TT):
                    ins = V.max_index(top8_i[:, tt, :], top8[:, tt, :], xrow[:, tt, C:XR])
                ins.then_inc(chain, 1)
                vec.wait_ge(chain, b * OPS + 2)
                V.tensor_copy(top8_f[:, :, :], top8_i[:, :, :]).then_inc(chain, 1)
                vec.wait_ge(chain, b * OPS + 3)
                V.tensor_tensor(onehot[:, :, :, :],
                                iota_e[:, :].rearrange("p (a b e) -> p a b e", a=1, b=1).to_broadcast([P, TT, TOPK, E]),
                                top8_f[:, :, 0:TOPK].rearrange("p t (k o) -> p t k o", o=1).to_broadcast([P, TT, TOPK, E]),
                                ALU.is_equal).then_inc(chain, 1)
                vec.wait_ge(chain, b * OPS + 4)
                vec.wait_ge(S["mask_t_done"], b)
                V.tensor_reduce(mkey[:, :, :], onehot[:, :, :, :].rearrange("p t k e -> p t e k"), AX_X,
                                ALU.add).then_inc(chain, 1)
                vec.wait_ge(chain, b * OPS + 5)
                for tt in range(TT):
                    ins = V.tensor_scalar(mkey[:, tt, :], mkey[:, tt, :], cut(key_col, b * TT + tt, 1), None, ALU.mult)
                ins.then_inc(S["mask_ready"], 1)

            def shared_h(b, m):
                rows = P if m < SM - 1 else SLAST
                up = up_bank[m % 2][:, :] if m < SM - 1 else gate_bank[m % 2][SLAST:2 * SLAST, :]
                vec.wait_ge(S["sh_silu_ready"], b * SM + m + 1)
                V.tensor_tensor(h_sh[0:rows, m, :], silu_sh[0:rows, :], up, ALU.mult).then_inc(sh_h_ready[m % 2], 1)

            def shared_y(b, tt):
                s = tt % 2
                vec.wait_ge(S["sh_d_done"], b * TT + tt + 1)
                vec.wait_ge(xres_in[s], (b * 2 + tt // 2 + 1) * DMA)
                vec.wait_ge(y_sent[(tt + 2) % 4], (b + tt // 2) * DMA)
                V.tensor_tensor(y_sh[:, s, :], row_bank[s][:, :], xres[:, s, :], ALU.add).then_inc(sh_y_ready[tt], 1)

            def early_step(s, shared):
                wkv.base, wkv.n = s * (NJ * WKV_OPS), 0
                if shared:
                    route(s - 1)
                for j in range(NJ):
                    wkv_clamp(0, s, j, j % 2, side_in[j % 2], s * 2 + j // 2)
                    wkv_den(0, s, j, j % 2)
                    if shared:
                        shared_h(s - 1, 2 * j) if j < 3 else [shared_y(s - 1, t) for t in (0, 1)]
                    wkv_num(0, s, j, j % 2)
                    wkv_ratio(0, s, j)
                    if shared:
                        shared_h(s - 1, 2 * j + 1) if j < 3 else [shared_y(s - 1, t) for t in (2, 3)]
                assert wkv.n == NJ * WKV_OPS

            vec.wait_ge(S["fac_ready"], 2 + 2 * B)
            vec.wait_ge(S["const_in"], N_CONST * DMA)
            early_step(0, False)
            with vec.Fori(1, B) as s:
                early_step(s, True)
            route(B - 1)

            def slot_round(r):
                vec.wait_ge(S["round_chain"], 2 * r)
                V.max(slot_key[:, 8 * r:8 * r + 8], keys[:, :]).then_inc(S["round_chain"], 1)
                vec.wait_ge(S["round_chain"], 2 * r + 1)
                V.match_replace(keys[:, :], slot_key[:, 8 * r:8 * r + 8], keys[:, :], 0.0).then_inc(S["round_chain"], 1)

            shared_h(B - 1, 0)
            shared_h(B - 1, 1)
            vec.wait_ge(S["keys_ready"], B)
            for r in range(8):
                slot_round(r)
                if r < 4:
                    shared_h(B - 1, r + 2)
                else:
                    shared_y(B - 1, r - 4)
            vec.wait_ge(S["round_chain"], 16)
            vec.engine_nop().then_inc(S["slots_ready"], 1)
            vec.wait_ge(S["slots_t_done"], 1)
            V.tensor_scalar(tok_f[:, :], bank[1][0:CAP, 0:E], -1.0, float(NT), ALU.mult, ALU.add).then_inc(S["idx_chain"], 1)
            vec.wait_ge(S["idx_chain"], 1)
            V.tensor_scalar(empty_f[:, :], tok_f[:, :], float(NT), None, ALU.is_equal).then_inc(S["idx_chain"], 1)
            halves = tok_f[:, :].rearrange("p (q o) -> p q o", o=2)
            V.tensor_scalar(gidx[0:CAP, :], halves[:, :, 0], float(NT - 1), None, ALU.min).then_inc(S["idx_chain"], 1)
            V.tensor_scalar(gidx[CAP:P, :], halves[:, :, 1], float(NT - 1), None, ALU.min).then_inc(S["idx_chain"], 1)
            vec.wait_ge(S["idx_chain"], 4)
            V.scalar_tensor_tensor(out=sidx[:, :], in0=empty_f[:, :], scalar=scol[:, 0:1], in1=tok_f[:, :],
                                   op0=ALU.mult, op1=ALU.add).then_inc(S["idx_ready"], 1)

            wkv.base, wkv.n = B * NJ * WKV_OPS, 0
            for j in range(NJ):
                wkv_clamp(1, 0, j, 0, side_in[0], 2 * B + j)
                wkv_den(1, 0, j, 0)
                wkv_num(1, 0, j, 0)
                wkv_ratio(1, 0, j)

            def split_lo_gu(e):
                vec.wait_ge(S["gu_hi_ready"], e.n + 1)
                V.tensor_tensor(gu_slot(gu_lo, e.slot2), gu_slot(gu_raw, e.slot4), gu_slot(gu_hi, e.slot2).bitcast(F32),
                                ALU.subtract).then_inc(S["gu_lo_ready"], 1)

            def split_lo_dn(e):
                vec.wait_ge(S["dn_hi_ready"], e.n + 1)
                V.tensor_tensor(dn_lo[:, e.slot2, :], dn_raw[:, e.slot4, :], dn_hi[:, e.slot2, :].bitcast(F32),
                                ALU.subtract).then_inc(S["dn_lo_ready"], 1)

            def tokens(e):
                s, q = e.slot4, e.pair
                half = (e.off // 2) % 2
                vec.wait_ge(xg_in[half], (e.fours + 1) * DMA)
                V.scalar_tensor_tensor(out=wsel[:, :], in0=iota_e[:, :], scalar=cut(pair_e, q, 1),
                                       in1=xg[:, half, C:XR], op0=ALU.is_equal, op1=ALU.mult,
                                       accum_out=w_pair[:, half:half + 1]).then_inc(S["wsel_done"], 1)
                vec.wait_ge(S["wsel_done"], q + 1)
                V.tensor_copy(w_odd[:, half:half + 1], w_pair[CAP:P, half:half + 1]).then_inc(S["wslot_ready"], 1)
                vec.wait_ge(S["xs_hi_ready"], q + 1)
                hi = xs_hi[:, s:s + 2, :, :].bitcast(F32).rearrange("p s j t -> p j s t")
                V.tensor_tensor(xs_lo[:, s:s + 2, :, :].rearrange("p s j t -> p j s t"),
                                bank[1][:, :].rearrange("p (j s t) -> p j s t", j=NJ, s=2), hi,
                                ALU.subtract).then_inc(S["xs_lo_ready"], 1)

            def step(e, h=True, hs=True, xs=True, gu=True, dn=True):
                half = (e.off // 2) % 2
                if h:
                    w = w_pair[0:CAP, half:half + 1] if e.slot2 == 0 else w_odd[:, half:half + 1]
                    vec.wait_ge(S["wslot_ready"], e.pair + 1)
                    vec.wait_ge(S["e_silu_ready"], e.n + 1)
                    if not (isinstance(e.i, int) and e.off < 2):
                        vec.wait_ge(S["ht_done"], e.n - 1)
                    V.scalar_tensor_tensor(out=h_e[:, e.slot2, :], in0=silu_e[:, e.slot2, :], scalar=w,
                                           in1=up_bank[e.slot2][0:CAP, 0:I], op0=ALU.mult, op1=ALU.mult).then_inc(S["h_ready"], 1)
                if hs:
                    d = e + -1
                    vec.wait_ge(S["hs_hi_ready"], d.n + 1)
                    V.tensor_tensor(hs_lo[:, d.slot2, :], bank[2][:, 0:len(KT) * CAP], hs_hi[:, d.slot2, :].bitcast(F32),
                                    ALU.subtract).then_inc(S["hs_lo_ready"], 1)
                if xs and e.off % 2 == 0:
                    tokens(e + 2)
                if gu:
                    split_lo_gu(e + 2)
                if dn:
                    split_lo_dn(e)

            vec.wait_ge(S["sh_d_done"], B * TT)
            for tt in range(TT):
                vec.wait_ge(y_sent[tt], B * DMA)
            V.memset(bank[2][96:P, 2 * CAP:3 * CAP], 0.0).then_inc(S["bank_pad"], 1)
            tokens(Expert(0, 0))
            split_lo_gu(Expert(0, 0))
            split_lo_gu(Expert(0, 1))
            for off in range(4):
                step(Expert(0, off), hs=off >= 1)
            with vec.Fori(1, E // 4 - 1) as i:
                for off in range(4):
                    step(Expert(i, off))
            for off in range(4):
                step(Expert(0, E - 4 + off), xs=off < 2, gu=off < 2)
            step(Expert(0, E), h=False, xs=False, gu=False, dn=False)

            def f_split_lo_gu(c, n):
                g, r = n
                vec.wait_ge(S["w_gu_hi_ready"], c * NF + g * 4 + r + 1)
                V.tensor_tensor(dn_lo[:, r % 2, 0:FGU], dn_raw[:, r, 0:FGU], dn_hi[:, r % 2, 0:FGU].bitcast(F32),
                                ALU.subtract).then_inc(w_gu_lo[r], 1)

            def f_step(c, g, r, nxt):
                half = c * 8 + g * 2 + r // 2
                if nxt is not None:
                    f_split_lo_gu(*nxt)
                vec.wait_ge(S["w_dn_hi_ready"], c * NF + g * 4 + r + 1)
                V.tensor_tensor(dn_lo[:, r % 2, FGU:], dn_raw[:, r, FGU:], dn_hi[:, r % 2, FGU:].bitcast(F32),
                                ALU.subtract).then_inc(w_dn_lo[r], 1)
                vec.wait_ge(f_lo[r % 2], half)
                vec.wait_ge(f_silu[r % 2], half + 1)
                V.tensor_tensor(fh[r % 2], fsilu[r % 2], up_bank[r % 2][:, :], ALU.mult).then_inc(f_h[r % 2], 1)
                vec.wait_ge(f_hi[r % 2], half + 1)
                V.tensor_tensor(fh_lo[r % 2], fh[r % 2], fh_hi[r % 2].bitcast(F32), ALU.subtract).then_inc(f_lo[r % 2], 1)

            def f_group(c, g, with_wkv, last=False):
                wkv.base, wkv.n = ((B + 1 + c) * NJ + g) * WKV_OPS, 0
                for r in range(4):
                    nxt = (c, (g, r + 1)) if r < 3 else (None if last else (c, (g + 1, 0)))
                    f_step(c, g, r, nxt)
                    if with_wkv:
                        if r == 0:
                            wkv_clamp(1, c + 1, g, 0, S["side_e_in"], c * NJ + g)
                        elif r == 1:
                            wkv_den(1, c + 1, g, 0)
                        elif r == 2:
                            wkv_num(1, c + 1, g, 0)
                        else:
                            wkv_ratio(1, c + 1, g)

            def f_chunk(c, with_wkv, last=False):
                vec.wait_ge(S["wkv_ready"], (B + 1 + c) * NJ)
                for j in range(NJ):
                    vec.wait_ge(S["sig_ready"], c * NJ + j + 1)
                    V.tensor_tensor(sig[:, j * T:(j + 1) * T], sig[:, j * T:(j + 1) * T],
                                    wkv_out[:, j * T:(j + 1) * T], ALU.mult).then_inc(S["x1_ready"], 1)
                for j in range(NJ):
                    vec.wait_ge(S["x1_hi_ready"], c * NJ + j + 1)
                    V.tensor_tensor(x1_lo[:, j * T:(j + 1) * T], sig[:, j * T:(j + 1) * T],
                                    x1_hi[:, j * T:(j + 1) * T].bitcast(F32), ALU.subtract).then_inc(S["x1_lo_ready"], 1)
                f_group(c, 0, with_wkv)
                with vec.Fori(1, NF // 4 - 1) as g:
                    f_group(c, g, with_wkv)
                f_group(c, NF // 4 - 1, with_wkv, last)
                vec.wait_ge(f_d_done[1], c * 8 + 8)
                vec.wait_ge(f_d_done[0], c * 8 + 8)
                vec.wait_ge(S["x1t_ready"], c * NJ + NJ)
                vec.wait_ge(S["out_sent"], c * DMA)
                for j in range(NJ):
                    V.tensor_tensor(o_sb[:, j * T:(j + 1) * T], bank[j][:, :], x1t[:, j * T:(j + 1) * T],
                                    ALU.add).then_inc(S["out_ready"], 1)

            f_split_lo_gu(0, (0, 0))
            with vec.Fori(0, B - 1) as c:
                f_chunk(c, True)
            f_chunk(B - 1, False, last=True)

        @block.tensor
        def _(pe):
            pe.wait_ge(S["const_in"], N_CONST * DMA)
            pe.wait_ge(S["sgu_in"], DMA)
            pe.wait_ge(S["sdn_in"], 2 * DMA)

            def batch(b):
                pe.wait_ge(S["x0_ready"], b + 1)
                pe.wait_ge(sh_y_ready[3], b)
                for tt in range(TT):
                    for j in range(NJ):
                        mm = pe.matmul(bank[0][:, tt * E:(tt + 1) * E], x0[:, j * T + tt * P:j * T + (tt + 1) * P],
                                       gate_sb[:, j * E:(j + 1) * E], start=j == 0, stop=j == NJ - 1)
                mm.then_inc(S["logits_done"], 1)
                for tt in range(TT):
                    pe.wait_ge(S["xrow_copied"], b * TT + tt)
                    for j in range(NJ):
                        mm = pe.transpose(bank[1][:, j * P:(j + 1) * P], x0[:, j * T + tt * P:j * T + (tt + 1) * P], idt[:, :])
                    mm.then_inc(S["tok_t_done"], 1)
                for m in range(SM):
                    pe.wait_ge(sh_h_ready[m % 2], b * (SM // 2) + m // 2)
                    for side, dst in enumerate((gate_bank[m % 2], up_bank[m % 2])[:2 if m < SM - 1 else 1]):
                        for j in range(NJ):
                            mm = pe.matmul(dst[:, :], sgu[:, j, (2 * m + side) * P:(2 * m + side + 1) * P],
                                           x0[:, j * T:(j + 1) * T], start=j == 0, stop=j == NJ - 1)
                    mm.then_inc(S["sh_gu_done"], 1)
                    if m == 1:
                        pe.wait_ge(S["sgu_in"], DMA)
                        pe.wait_ge(S["mask_ready"], b + 1)
                        pe.wait_ge(S["keys_ready"], b)
                        for tt in range(TT):
                            mm = pe.transpose(bank[2][0:E, tt * P:(tt + 1) * P], mkey[:, tt, :], idt[:, :])
                        mm.then_inc(S["mask_t_done"], 1)
                for s in range(2):
                    pe.wait_ge(sh_h_ready[s], b * (SM // 2) + SM // 2)
                pe.wait_ge(S["pexp_ready"], b + 1)
                for tt in range(TT):
                    pe.wait_ge(sh_y_ready[(tt + 2) % 4], b + tt // 2)
                    for k in range(SM):
                        rows = P if k < SM - 1 else SLAST
                        mm = pe.matmul(row_bank[tt % 2][:, :], h_sh[0:rows, k, tt * P:(tt + 1) * P], sdn[0:rows, k, :],
                                       start=k == 0, stop=k == SM - 1)
                    mm.then_inc(S["sh_d_done"], 1)

            with pe.Fori(0, B) as b:
                batch(b)
            pe.wait_ge(S["slots_ready"], 1)
            pe.transpose(bank[1][0:CAP, 0:E], slot_key[:, :], idt[0:E, 0:E]).then_inc(S["slots_t_done"], 1)

            def tokens(e, first=False):
                half = (e.off // 2) % 2
                pe.wait_ge(xg_in[half], (e.fours + 1) * DMA)
                if not first:
                    pe.wait_ge(S["xs_lo_ready"], e.pair)
                for j in range(NJ):
                    mm = pe.transpose(bank[1][:, j * P:(j + 1) * P], xg[:, half, j * P:(j + 1) * P], idt[:, :])
                mm.then_inc(S["xt_done"], 1)

            def gate_up(e):
                s, s4 = e.slot2, e.slot4
                pe.wait_ge(S["gu_lo_ready"], e.n + 1)
                pe.wait_ge(S["xs_lo_ready"], e.pair + 1)
                if not (isinstance(e.i, int) and e.off < 2):
                    pe.wait_ge(S["h_ready"], e.n - 1)
                for j in range(NJ):
                    for n, (x, w) in enumerate(((xs_hi, gu_hi), (xs_hi, gu_lo), (xs_lo, gu_hi))):
                        for side, dst in enumerate((gate_bank[s], up_bank[s])):
                            at = s * GUW + (2 * j + side) * I
                            mm = pe.matmul(dst[0:CAP, 0:I], x[:, s4, j, :], w[:, at:at + I],
                                           start=j == 0 and n == 0, stop=j == NJ - 1 and n == 2)
                mm.then_inc(S["gu_done"], 1)

            def turn_h(e):
                pe.wait_ge(S["bank_pad"], 1)
                pe.wait_ge(S["h_ready"], e.n + 1)
                if not (isinstance(e.i, int) and e.off < 1):
                    pe.wait_ge(S["hs_lo_ready"], e.n)
                for k, rows in KT:
                    mm = pe.transpose(bank[2][0:rows, k * CAP:(k + 1) * CAP], h_e[:, e.slot2, k * P:k * P + rows],
                                      idt[0:CAP, 0:CAP])
                mm.then_inc(S["ht_done"], 1)

            def down(e):
                s = e.slot2
                pe.wait_ge(S["hs_lo_ready"], e.n + 1)
                pe.wait_ge(S["dn_lo_ready"], e.n + 1)
                if not (isinstance(e.i, int) and e.off < 2):
                    pe.wait_ge(S["y_ready"], e.n - 1)
                for k, rows in KT:
                    for n, (h, w) in enumerate(((hs_hi, dn_hi), (hs_hi, dn_lo), (hs_lo, dn_hi))):
                        mm = pe.matmul(row_bank[s][0:CAP, :], h[0:rows, s, k * CAP:(k + 1) * CAP],
                                       w[0:rows, s, k * C:(k + 1) * C], start=k == 0 and n == 0,
                                       stop=k == len(KT) - 1 and n == 2)
                mm.then_inc(S["d_done"], 1)

            def step(e, gu=True, th=True, xt=True, dn=True):
                if gu:
                    gate_up(e)
                if th:
                    turn_h(e + -1)
                if xt and e.off % 2 == 0:
                    tokens(e + 2)
                if dn:
                    down(e + -2)

            pe.wait_ge(S["idx_ready"], 1)
            tokens(Expert(0, 0), first=True)
            for off in range(4):
                step(Expert(0, off), th=off >= 1, dn=off >= 2)
            with pe.Fori(1, E // 4 - 1) as i:
                for off in range(4):
                    step(Expert(i, off))
            for off in range(4):
                step(Expert(0, E - 4 + off), xt=off < 2)
            step(Expert(0, E), gu=False, xt=False)
            step(Expert(0, E + 1), gu=False, th=False, xt=False)

            def f_gate_up(c, g, r):
                s = r % 2
                pe.wait_ge(w_gu_lo[r], c * 4 + g + 1)
                pe.wait_ge(f_h[s], c * 8 + g * 2 + r // 2)
                for side, dst in enumerate((gate_bank[s], up_bank[s])):
                    for j in range(NJ):
                        at = (2 * j + side) * P
                        for n, (w, x) in enumerate(((dn_hi, x1_hi), (dn_hi, x1_lo), (dn_lo, x1_hi))):
                            mm = pe.matmul(dst[:, :], w[:, s, at:at + P], x[:, j * T:(j + 1) * T],
                                           start=j == 0 and n == 0, stop=j == NJ - 1 and n == 2)
                mm.then_inc(f_gu_done[s], 1)

            def f_down(c, g, r, first=False, last=False):
                s = r % 2
                pe.wait_ge(w_dn_lo[r], c * 4 + g + 1)
                pe.wait_ge(f_lo[s], c * 8 + g * 2 + r // 2 + 1)
                if first:
                    pe.wait_ge(S["out_ready"], c * NJ)
                for ct in range(NJ):
                    at = FGU + ct * P
                    for n, (w, h) in enumerate(((dn_hi, fh_hi), (dn_hi, fh_lo), (dn_lo, fh_hi))):
                        mm = pe.matmul(bank[ct][:, :], w[:, s, at:at + P], h[s], start=first and n == 0,
                                       stop=last and n == 2, skip_group_check=True)
                mm.then_inc(f_d_done[s], 1)

            def f_chunk(c):
                pe.wait_ge(S["xa_in"], (c + 1) * DMA)
                for s in range(2):
                    pe.wait_ge(f_h[s], c * 8)
                for j in range(NJ):
                    for tt in range(TT):
                        mm = pe.transpose(bank[4 + j][:, tt * P:(tt + 1) * P], xa[:, tt * C + j * P:tt * C + (j + 1) * P], idt[:, :])
                    mm.then_inc(S["xa_t_done"], 1)
                pe.wait_ge(S["x1_lo_ready"], c * NJ + NJ)
                pe.wait_ge(S["x1t_ready"], c * NJ + NJ)
                for r in range(4):
                    f_gate_up(c, 0, r)
                    if r:
                        f_down(c, 0, r - 1, first=r == 1)
                with pe.Fori(1, NF // 4) as g:
                    for r in range(4):
                        f_gate_up(c, g, r)
                        if r:
                            f_down(c, g, r - 1)
                        else:
                            f_down(c, g - 1, 3)
                f_down(c, NF // 4 - 1, 3, last=True)

            pe.wait_ge(S["h_ready"], E)
            pe.wait_ge(S["y_ready"], E)
            with pe.Fori(0, B) as c:
                f_chunk(c)


def channel_major(a, np):
    b, t, c = a.shape
    return np.ascontiguousarray(a.transpose(0, 2, 1).reshape(b, c // 128, 128, t).transpose(0, 2, 1, 3)).reshape(b, 128, -1)


def by_partition(w, np):
    return np.ascontiguousarray(w.reshape(-1, 128, w.shape[-1]).transpose(1, 0, 2))


def kernel(**inputs):
    import numpy as np
    from concourse import bacc
    from concourse.bass_utils import run_bass_kernel_spmd

    a = {k: np.asarray(v) for k, v in inputs.items()}
    B, T, C = a["x"].shape
    E, _, I = a["L0_ffn_w_gate"].shape
    IS = a["L0_ffn_sw_gate"].shape[1]
    F = a["L1_ffn_w_down"].shape[1]

    def layers(name):
        return np.concatenate([a[f"L{n}_cond_{name}"].reshape(4, 128).T for n in range(2)], axis=1)

    moe = np.concatenate([a["L0_ffn_w_gate"].reshape(E, 4, 128, I), a["L0_ffn_w_up"].reshape(E, 4, 128, I)], axis=3)
    moe = np.ascontiguousarray(moe.transpose(0, 2, 1, 3)).reshape(E, 128, -1)
    full = IS // 128
    tiles = []
    for m in range(full):
        tiles += [a["L0_ffn_sw_gate"][:, m * 128:(m + 1) * 128], a["L0_ffn_sw_up"][:, m * 128:(m + 1) * 128]]
    tiles += [a["L0_ffn_sw_gate"][:, full * 128:], a["L0_ffn_sw_up"][:, full * 128:]]
    shared_gu = by_partition(np.concatenate(tiles, axis=1), np)
    w = a["L1_ffn_w_gate_up"].T.reshape(4, 128, 2, F // 128, 128)
    w = w.transpose(3, 1, 0, 2, 4).reshape(F // 128, 128, -1)
    ffn = np.ascontiguousarray(np.concatenate([w, a["L1_ffn_w_down"].T.reshape(F // 128, 128, C)], axis=2))

    part = np.arange(128)
    arrays = {
        "x_t": channel_major(a["x"], np),
        "side_t": channel_major(a["fside_BxSxS_0"], np),
        "x_rows": np.ascontiguousarray(a["x"].reshape(B * T, C)),
        "cond": np.ascontiguousarray(a["cond_512"]),
        "wkv_w": np.ascontiguousarray(layers("w")),
        "wkv_u": np.ascontiguousarray(layers("u")),
        "gate_w": by_partition(np.ascontiguousarray(a["L0_ffn_gate_w"].T), np),
        "moe_gu": moe,
        "moe_down": np.ascontiguousarray(a["L0_ffn_w_down"]),
        "shared_gu": shared_gu,
        "shared_down": np.ascontiguousarray(a["L0_ffn_sw_down"]),
        "ffn_w": ffn,
        "ident": np.eye(128, dtype=np.float32),
        "expert_iota": np.tile(np.arange(E, dtype=np.float32), (128, 1)),
        "pair_expert": (2 * np.arange(E // 2)[None, :] + (part >= 64)[:, None]).astype(np.float32),
        "token_key": (B * T - (np.arange(B * T // 128)[None, :] * 128 + part[:, None])).astype(np.float32),
        "slot_col": np.arange(64, dtype=np.float32).reshape(64, 1),
    }
    nc = bacc.Bacc("TRN2", target_bir_lowering=False, num_devices=1)
    args = [nc.dram_tensor(f"in_{k}", v.shape, mybir.dt.from_np(v.dtype), kind="ExternalInput").ap() for k, v in arrays.items()]
    out = nc.dram_tensor("out_t", (B, 128, 4 * T), F32, kind="ExternalOutput").ap()
    adaln_ffn_kernel(nc, *args, out)
    r = run_bass_kernel_spmd(nc, [{f"in_{k}": v for k, v in arrays.items()}], core_ids=[0])
    y = r.results[0]["out_t"].reshape(B, 128, 4, T)
    return np.ascontiguousarray(y.transpose(0, 3, 2, 1)).reshape(B, T, C)
```

```python
from contextlib import ExitStack

import concourse.bass as bass
from concourse import mybir

P = 128
ALU = mybir.AluOpType
ACT = mybir.ActivationFunctionType
AX_X = mybir.AxisListType.X
F32 = mybir.dt.float32
F32R = mybir.dt.float32r
U32 = mybir.dt.uint32

EXP_CAP = 30.0
DEN_FLOOR = 1e-8
TOPK = 6
CAP = 64
DMA = 16


class Expert:

    def __init__(self, i, off):
        self.i, self.off = i, off

    def __add__(self, d):
        return Expert(self.i, self.off + d)

    @property
    def n(self):
        return self.i * 4 + self.off

    @property
    def pair(self):
        return self.i * 2 + self.off // 2

    @property
    def slot2(self):
        return self.off % 2

    @property
    def slot4(self):
        return self.off % 4

    @property
    def fours(self):
        return self.i + self.off // 4


def adaln_ffn_kernel(nc, x_t, side_t, x_rows, cond, wkv_w, wkv_u, gate_w, moe_gu, moe_down,
                     shared_gu, shared_down, ffn_w, ident, expert_iota, pair_expert, token_key,
                     slot_col, out):
    B, _, BT = x_t.shape
    NJ = 4
    T = BT // NJ
    C = NJ * P
    NT = B * T
    TT = T // P
    E = gate_w.shape[2]
    XR = C + E
    I = moe_down.shape[1]
    GUW = NJ * 2 * I
    KT = [(k, min(P, I - k * P)) for k in range((I + P - 1) // P)]
    DNW = len(KT) * C
    SGW = shared_gu.shape[2]
    SM = shared_down.shape[0] // P + 1
    SLAST = shared_down.shape[0] - (SM - 1) * P
    NF = ffn_w.shape[0]
    FGU = NJ * 2 * P
    assert FGU + C == DNW and NF == 16 and E == 64 and B == 4 and TT == 4

    x0_rows = nc.dram_tensor("x0_rows", (NT, XR), F32, kind="Internal").ap()
    acc = nc.dram_tensor("acc_rows", (NT + CAP, C), F32, kind="Internal").ap()

    with ExitStack() as ctx:
        def sb(name, shape, dt=F32, stack=ctx):
            return stack.enter_context(nc.sbuf_tensor(name, shape, dt))

        bank = [ctx.enter_context(nc.psum_tensor(f"bank{n}", [P, 512], F32)) for n in range(8)]
        gate_bank, up_bank = (bank[4], bank[6]), (bank[5], bank[7])
        turn_bank = (bank[6], bank[7], bank[4], bank[5])
        row_bank = (bank[3], bank[0])

        idt, iota_e, pair_e = sb("idt", [P, P]), sb("iota_e", [P, E]), sb("pair_e", [P, E // 2])
        key_col, scol = sb("key_col", [P, NT // P]), sb("scol", [CAP, 1])
        gate_sb = sb("gate_sb", [P, NJ * E])
        w_sb, u_sb = sb("w_sb", [P, 2 * NJ]), sb("u_sb", [P, 2 * NJ])
        cond_sb = sb("cond_sb", [P, B, P])
        tf, half_tf, out_scale = sb("tf", [P, B]), sb("half_tf", [P, B]), sb("out_scale", [P, B])
        dec0 = sb("dec0", [P, 2 * NJ])
        decay = sb("decay", [P, 2 * B * NJ])

        side_sb, x_sb = sb("side_sb", [P, 2, T]), sb("x_sb", [P, 2, T])
        ek, eu = sb("ek", [P, T]), sb("eu", [P, T])
        one_en = sb("one_en", [P, T])
        ekv, dv = sb("ekv", [P, T]), sb("dv", [P, T])
        den, den_b = sb("den", [P, T]), sb("den_b", [P, T])
        num, num_b = sb("num", [P, T]), sb("num_b", [P, T])
        wkv_out = sb("wkv_out", [P, NJ * T])

        gu_raw, dn_raw = sb("gu_raw", [P, 4 * GUW]), sb("dn_raw", [P, 4, DNW])
        gidx, sidx = sb("gidx", [P, E // 2], U32), sb("sidx", [CAP, E], U32)
        gidx_now, sidx_now = sb("gidx_now", [P, 2], U32), sb("sidx_now", [CAP, 2], U32)
        xg = sb("xg", [P, 2, XR])

        with ExitStack() as early:
            sgu = sb("sgu", [P, NJ, SGW], stack=early)
            x0 = sb("x0", [P, NJ * T], stack=early)
            xrow = sb("xrow", [P, TT, XR], stack=early)
            nmax, psums = sb("nmax", [P, TT], stack=early), sb("psums", [P, TT], stack=early)
            prec, pexp = sb("prec", [P, TT], stack=early), sb("pexp", [P, TT, E], stack=early)
            top8, top8_i = sb("top8", [P, TT, 8], stack=early), sb("top8_i", [P, TT, 8], U32, early)
            top8_f = sb("top8_f", [P, TT, 8], stack=early)
            onehot = sb("onehot", [P, TT, TOPK, E], stack=early)
            mkey = sb("mkey", [P, TT, E], stack=early)
            keys = sb("keys", [E, CAP + T], stack=early)
            slot_key = sb("slot_key", [E, CAP], stack=early)
            tok_f, empty_f = sb("tok_f", [CAP, E], stack=early), sb("empty_f", [CAP, E], stack=early)
            sdn = sb("sdn", [P, SM, C], stack=early)
            h_sh, silu_sh = sb("h_sh", [P, SM, T], stack=early), sb("silu_sh", [P, T], stack=early)
            xres, y_sh = sb("xres", [P, 2, C], stack=early), sb("y_sh", [P, 2, C], stack=early)
        gu_hi, gu_lo = sb("gu_hi", [P, 2 * GUW], F32R), sb("gu_lo", [P, 2 * GUW], F32R)
        dn_hi, dn_lo = sb("dn_hi", [P, 2, DNW], F32R), sb("dn_lo", [P, 2, DNW], F32R)
        xs_hi, xs_lo = sb("xs_hi", [P, 4, NJ, CAP], F32R), sb("xs_lo", [P, 4, NJ, CAP], F32R)
        wsel, w_pair, w_odd = sb("wsel", [P, E]), sb("w_pair", [P, 2]), sb("w_odd", [CAP, 2])
        silu_e, h_e = sb("silu_e", [CAP, 2, I]), sb("h_e", [CAP, 2, I])
        hs_hi, hs_lo = sb("hs_hi", [P, 2, len(KT) * CAP], F32R), sb("hs_lo", [P, 2, len(KT) * CAP], F32R)
        y_e = sb("y_e", [CAP, 2, C])
        CH = NJ * T
        xa, sig = gu_raw[:, 0:CH], gu_raw[:, CH:2 * CH]
        x1t = [gu_raw[:, n * CH:(n + 1) * CH] for n in (2, 3)]
        fh = [gu_raw[:, 4 * CH + n * T:4 * CH + (n + 1) * T] for n in range(2)]
        fsilu = [gu_raw[:, 4 * CH + (2 + n) * T:4 * CH + (3 + n) * T] for n in range(2)]
        x1_hi, x1_lo = ([t[:, n * CH:(n + 1) * CH] for n in range(2)] for t in (gu_hi, gu_lo))
        fh_hi, fh_lo = ([t[:, 2 * CH + n * T:2 * CH + (n + 1) * T] for n in range(2)] for t in (gu_hi, gu_lo))

        S = {name: ctx.enter_context(nc.semaphore(name)) for name in ("cond_in const_in sgu_in sdn_in csum_done tf_ready exp_w_done dec0_ready fac_ready "
                     "k_ready e_ready ekv_ready dv_ready scans_done num_added numer_ready edges_zero t_ready wkv_ready wkv_chain x0_ready logits_done "
                     "tok_t_done xrow_copied xrow_sent nmax_done nmax_ready pexp_ready p_ready route_chain "
                     "mask_ready mask_t_done keys_ready sh_gu_done sh_silu_ready sh_d_done dummy_in "
                     "best_ready slots_ready slots_t_done idx_chain idx_ready dn_pad bank_pad "
                     "gu_hi_ready gu_lo_ready dn_hi_ready dn_lo_ready xt_done xs_hi_ready xs_lo_ready "
                     "wsel_done wslot_ready gu_done e_silu_ready h_ready ht_done hs_hi_ready hs_lo_ready "
                     "d_done y_ready added gcol_first gcol_ready scol_ready top8_ready "
                     "w_gu_hi_ready w_dn_hi_ready xa_in xa_t_done x1t_ready sig_ready x1_ready "
                     "x1_hi_ready x1_lo_ready out_ready out_sent").split()}

        def ring(name, n):
            return [ctx.enter_context(nc.semaphore(f"{name}{k}")) for k in range(n)]

        side_in, x_in, x_used = ring("side_in", 2), ring("x_in", 2), ring("x_used", 2)
        sh_h_ready, sh_y_ready, y_sent, xres_in = ring("sh_h_ready", 2), ring("sh_y_ready", 4), ring("y_sent", 4), ring("xres_in", 2)
        gu_in, dn_in, xg_in = ring("gu_in", 4), ring("dn_in", 4), ring("xg_in", 2)
        w_in, w_gu_lo, w_dn_lo = ring("w_in", 4), ring("w_gu_lo", 4), ring("w_dn_lo", 4)
        f_gu_done, f_silu, f_h, f_hi, f_lo, f_d_done = (
            ring(n, 2) for n in ("f_gu_done", "f_silu", "f_h", "f_hi", "f_lo", "f_d_done"))
        round_max, round_cut = ring("round_max", CAP // 8), ring("round_cut", CAP // 8)
        N_CONST = 8

        def cut(buf, start, size):
            return buf[:, start:start + size] if isinstance(start, int) else buf[:, bass.ds(start, size)]

        def gu_slot(buf, s):
            return buf[:, s * GUW:(s + 1) * GUW]

        block = ctx.enter_context(nc.Block())

        @block.sync
        def _(sp):
            sp.dma_start(cond_sb[:, :, :], cond.rearrange("(o b) t -> o b t", o=1).to_broadcast([P, B, P])).then_inc(S["cond_in"], DMA)
            for dst, src in ((w_sb[:, :], wkv_w), (u_sb[:, :], wkv_u), (idt[:, :], ident), (iota_e[:, :], expert_iota),
                             (pair_e[:, :], pair_expert), (key_col[:, :], token_key), (scol[:, :], slot_col),
                             (gate_sb[:, :], gate_w.rearrange("p j e -> p (j e)"))):
                sp.dma_start(dst, src).then_inc(S["const_in"], DMA)

            def load_side(b, j, slot, read):
                if read is not None:
                    sp.wait_ge(S["dv_ready"], read)
                sp.dma_start(side_sb[:, slot, :], cut(side_t[b], j * T, T)).then_inc(side_in[slot], DMA)

            def load_unit(b, j):
                load_side(b, j, j % 2, b * NJ + j - 1 if not isinstance(b, int) or b or j > 1 else None)
                sp.wait_ge(x_used[j % 2], b * 2 + j // 2)
                sp.dma_start(x_sb[:, j % 2, :], cut(x_t[b], j * T, T)).then_inc(x_in[j % 2], DMA)

            def rows(t, b, tt):
                return t[bass.ds(b * T + tt * P, P), :]

            def load_residual(b, tt):
                sp.wait_ge(sh_y_ready[(tt + 2) % 4], b + tt // 2)
                sp.dma_start(xres[:, tt % 2, :], rows(x_rows, b, tt)).then_inc(xres_in[tt % 2], DMA)

            def store_x0(b):
                sp.wait_ge(S["xrow_copied"], b * TT + TT)
                sp.wait_ge(S["p_ready"], b + 1)
                sp.dma_start(x0_rows[bass.ds(b * T, T), :].rearrange("(t p) c -> p t c", p=P),
                             xrow[:, :, :]).then_inc(S["xrow_sent"], DMA)

            def store_rows(b, tt):
                sp.wait_ge(sh_y_ready[tt], b + 1)
                sp.dma_start(rows(acc, b, tt), y_sh[:, tt % 2, :]).then_inc(y_sent[tt], DMA)

            def store_batch(b):
                store_rows(b, 0)
                load_residual(b, 2)
                store_rows(b, 1)
                load_residual(b, 3)
                store_rows(b, 2)
                store_rows(b, 3)

            def early_step(s, ahead):
                load_residual(s - 1, 0)
                load_residual(s - 1, 1)
                load_unit(s, 2)
                load_unit(s, 3)
                store_x0(s - 1)
                ahead()
                store_batch(s - 1)

            def load_expert(e):
                s = e.slot4
                sp.dma_start(gu_slot(gu_raw, s), moe_gu[e.n]).then_inc(gu_in[s], DMA)
                sp.dma_start(dn_raw[:, s, 0:2 * C].rearrange("p (k c) -> p k c", k=2),
                             moe_down[e.n][0:2 * P, :].rearrange("(k p) c -> p k c", p=P)).then_inc(dn_in[s], DMA)
                sp.dma_start(dn_raw[0:I - 2 * P, s, 2 * C:3 * C], moe_down[e.n][2 * P:I, :]).then_inc(dn_in[s], DMA)

            for j in range(NJ):
                load_unit(0, j)
            sp.dma_start(sgu[:, :, :], shared_gu).then_inc(S["sgu_in"], DMA)
            sp.dma_start(sdn[:, 0:SM - 1, :], shared_down[0:(SM - 1) * P, :].rearrange("(k p) c -> p k c", p=P)).then_inc(S["sdn_in"], DMA)
            sp.dma_start(sdn[0:SLAST, SM - 1, :], shared_down[(SM - 1) * P:, :]).then_inc(S["sdn_in"], DMA)
            load_unit(1, 0)
            load_unit(1, 1)
            with sp.Fori(1, B - 1) as s:
                early_step(s, lambda: (load_unit(s + 1, 0), load_unit(s + 1, 1)))
            early_step(B - 1, lambda: (load_side(0, 0, 0, B * NJ - 1), load_side(0, 1, 1, B * NJ)))
            load_residual(B - 1, 0)
            load_residual(B - 1, 1)
            store_x0(B - 1)
            load_side(0, 2, 0, B * NJ + 1)
            load_side(0, 3, 1, B * NJ + 2)
            sp.wait_ge(S["dn_pad"], 1)
            for off in range(4):
                load_expert(Expert(0, off))
            load_side(1, 0, 0, B * NJ + 3)
            store_batch(B - 1)

            with sp.Fori(1, E // 4) as i:
                for off in range(4):
                    e = Expert(i, off)
                    sp.wait_ge(S["gu_lo_ready"], e.n - 3)
                    sp.wait_ge(S["dn_lo_ready"], e.n - 3)
                    load_expert(e)

            def load_tiles(c, g, unit=None):
                if unit is not None:
                    load_side(unit[0], unit[1], 0, (B + c + 1) * NJ + g + 1)
                for r in range(4):
                    sp.wait_ge(w_dn_lo[r], c * 4 + g)
                    sp.dma_start(dn_raw[:, r, :], ffn_w[g * 4 + r]).then_inc(w_in[r], DMA)

            def load_sums(c):
                sp.wait_ge(S["added"], E * DMA)
                sp.wait_ge(S["xa_t_done"], c * NJ)
                sp.dma_start(xa.rearrange("p (t c) -> p t c", t=TT),
                             acc[c * T:(c + 1) * T, :].rearrange("(t p) c -> p t c", p=P)).then_inc(S["xa_in"], DMA)

            def store_out(c):
                sp.wait_ge(S["out_ready"], c * NJ + NJ)
                sp.dma_start(out[c], x1t[c % 2]).then_inc(S["out_sent"], DMA)

            sp.wait_ge(S["dn_lo_ready"], E)
            sp.wait_ge(S["gu_lo_ready"], E)
            for c in range(B):
                load_tiles(c, 0, (c + 1, 1) if c < B - 1 else None)
                if c == 0:
                    load_sums(0)
                else:
                    store_out(c - 1)
                if c < B - 1:
                    load_sums(c + 1)
                with sp.Fori(1, NF // 4 - 1) as g:
                    load_tiles(c, g, (c + 1, g + 1) if c < B - 1 else None)
                load_tiles(c, NF // 4 - 1, (c + 2, 0) if c < B - 2 else None)
            store_out(B - 1)
            for tt in range(TT):
                sp.wait_ge(y_sent[tt], B * DMA)
            sp.wait_ge(S["xrow_sent"], B * DMA)
            sp.wait_ge(S["out_sent"], B * DMA)

        @block.gpsimd
        def _(pool):
            pool.memset(dn_raw[96:P, :, 2 * C:3 * C], 0.0).then_inc(S["dn_pad"], 1)
            pool.dma_start(acc[NT:NT + CAP, :], x_rows[0:CAP, :]).then_inc(S["dummy_in"], DMA)

            def numerator(unit, slot):
                pool.wait_ge(S["ekv_ready"], unit + 1)
                pool.wait_ge(S["wkv_ready"], unit)
                pool.tensor_tensor(dv[:, :], eu[:, :], side_sb[:, slot, :], ALU.mult).then_inc(S["dv_ready"], 1)
                pool.wait_ge(S["scans_done"], unit + 1)
                pool.tensor_tensor(num[:, :], num[:, :], num_b[:, :], ALU.add).then_inc(S["num_added"], 1)
                pool.wait_ge(S["dv_ready"], unit + 1)
                pool.wait_ge(S["num_added"], unit + 1)
                pool.tensor_tensor(num[:, :], num[:, :], dv[:, :], ALU.add).then_inc(S["numer_ready"], 1)

            pool.wait_ge(S["dn_pad"], 1)
            with pool.Fori(0, B) as b:
                for j in range(NJ):
                    numerator(b * NJ + j, j % 2)
            numerator(B * NJ, 0)

            def gather(e, first=False):
                q, s = e.pair, (e.off // 2) % 2
                use = e.fours
                pool.wait_ge(S["idx_ready"], 1)
                if not first:
                    pool.wait_ge(S["xt_done"], q - 1)
                    pool.wait_ge(S["wslot_ready"], q - 1)
                    pool.wait_ge(xg_in[s], use * DMA)
                pool.tensor_copy(gidx_now[:, s:s + 1], cut(gidx, q, 1)).then_inc(S["gcol_first"] if first else S["gcol_ready"], 1)
                pool.wait_ge(S["xrow_sent"], B * DMA)
                pool.wait_ge(S["gcol_first"] if first else S["gcol_ready"], q + 1 if first else q - 1)
                pool.indirect_dma_start(xg[:, s, :], None, x0_rows,
                                        bass.IndirectOffsetOnAxis(ap=gidx_now[:, s:s + 1], axis=0)).then_inc(xg_in[s], DMA)

            def scatter(e, first=False):
                s = e.slot2
                pool.wait_ge(S["idx_ready"], 1)
                pool.wait_ge(S["y_ready"], e.n + 1)
                if not first:
                    pool.wait_ge(S["added"], e.n * DMA)
                pool.tensor_copy(sidx_now[:, s:s + 1], cut(sidx, e.n, 1)).then_inc(S["scol_ready"], 1)
                pool.wait_ge(S["idx_ready"], 1)
                pool.wait_ge(S["scol_ready"], e.n + 1)
                pool.indirect_dma_start(acc, bass.IndirectOffsetOnAxis(ap=sidx_now[:, s:s + 1], axis=0),
                                        y_e[:, s, :], None, compute_op=ALU.add).then_inc(S["added"], DMA)

            gather(Expert(0, 0), first=True)
            gather(Expert(0, 2), first=True)
            for n in range(1, NJ + 1):
                numerator(B * NJ + n, n % 2)
            for tt in range(TT):
                pool.wait_ge(y_sent[tt], B * DMA)
            pool.wait_ge(S["dummy_in"], DMA)

            def step(e, gathers=True, scatters=True):
                if gathers and e.off % 2 == 0:
                    gather(e + 4)
                if scatters:
                    scatter(e + -2, first=isinstance(e.i, int) and e.off == 2)

            for off in range(4):
                step(Expert(0, off), scatters=off >= 2)
            with pool.Fori(1, E // 4 - 1) as i:
                for off in range(4):
                    step(Expert(i, off))
            for off in range(4):
                step(Expert(0, E - 4 + off), gathers=False)
            for off in range(2):
                step(Expert(0, E + off), gathers=False)

            with pool.Fori(0, (B - 1) * NJ - 1) as n:
                numerator((B + 1) * NJ + 1 + n, 0)
            pool.wait_ge(S["added"], E * DMA)

        @block.scalar
        def _(act):
            act.wait_ge(S["csum_done"], 1)
            act.activation(tf[:, :], tf[:, :], ACT.Sigmoid).then_inc(S["tf_ready"], 1)
            act.wait_ge(S["const_in"], N_CONST * DMA)
            act.activation(w_sb[:, :], w_sb[:, :], ACT.Exp).then_inc(S["exp_w_done"], 1)
            act.wait_ge(S["exp_w_done"], 1)
            act.activation(dec0[:, :], w_sb[:, :], ACT.Exp, scale=-1.0).then_inc(S["dec0_ready"], 1)

            def exps(unit):
                act.wait_ge(S["k_ready"], unit + 1)
                act.activation(ek[:, :], ek[:, :], ACT.Exp)
                act.activation(eu[:, :], eu[:, :], ACT.Exp).then_inc(S["e_ready"], 1)

            def gate_r(b, j):
                unit = b * NJ + j
                act.wait_ge(x_in[j % 2], (b * 2 + j // 2 + 1) * DMA)
                act.wait_ge(S["wkv_ready"], unit)
                act.activation(one_en[:, :], x_sb[:, j % 2, :], ACT.Exp, scale=-1.0).then_inc(x_used[j % 2], 1)
                act.wait_ge(x_used[j % 2], b * 2 + j // 2 + 1)
                act.activation(one_en[:, :], one_en[:, :], ACT.Copy, bias=1.0).then_inc(S["t_ready"], 1)

            def softmax_exp(b):
                act.wait_ge(S["nmax_ready"], b + 1)
                act.wait_ge(S["p_ready"], b)
                for tt in range(TT):
                    ins = act.activation(pexp[:, tt, :], bank[0][:, tt * E:(tt + 1) * E], ACT.Exp,
                                         bias=nmax[:, tt:tt + 1], accum_out=psums[:, tt:tt + 1])
                ins.then_inc(S["pexp_ready"], 1)

            def copy_rows(b):
                act.wait_ge(S["xrow_sent"], b * DMA)
                for tt in range(TT):
                    act.wait_ge(S["tok_t_done"], b * TT + tt + 1)
                    act.activation(xrow[:, tt, 0:C], bank[1][:, :], ACT.Copy).then_inc(S["xrow_copied"], 1)

            def shared_silu(b, m):
                rows = P if m < SM - 1 else SLAST
                act.wait_ge(S["sh_gu_done"], b * SM + m + 1)
                act.wait_ge(sh_h_ready[(m + 1) % 2], b * (SM // 2) + (m + 1) // 2)
                act.activation(silu_sh[0:rows, :], gate_bank[m % 2][0:rows, :], ACT.Silu).then_inc(S["sh_silu_ready"], 1)

            def copy_keys(b):
                act.wait_ge(S["mask_t_done"], b + 1)
                act.wait_ge(S["best_ready"], b + 1)
                act.activation(keys[:, CAP:CAP + T], bank[2][0:E, :], ACT.Copy).then_inc(S["keys_ready"], 1)

            def hand_on_x0(b, first):
                act.wait_ge(S["wkv_ready"], b * NJ + NJ)
                if not first:
                    act.wait_ge(S["sh_gu_done"], b * SM)
                act.activation(x0[:, :], wkv_out[:, :], ACT.Copy).then_inc(S["x0_ready"], 1)

            def early_step(s, wkv, shared, late=False):
                exps(s * NJ)
                if wkv:
                    gate_r(s, 0)
                if shared:
                    softmax_exp(s - 1)
                    copy_rows(s - 1)
                for j in range(NJ):
                    if j < NJ - 1 or late:
                        exps(s * NJ + j + 1)
                    if shared and j < SM // 2:
                        shared_silu(s - 1, 2 * j)
                        shared_silu(s - 1, 2 * j + 1)
                    if shared and j == 0:
                        copy_keys(s - 1)
                    if wkv and j < NJ - 1:
                        gate_r(s, j + 1)
                if wkv:
                    hand_on_x0(s, not shared)

            early_step(0, True, False)
            with act.Fori(1, B) as s:
                early_step(s, True, True)
            early_step(B, False, True, late=True)

            def split_hi_gu(e):
                act.wait_ge(gu_in[e.slot4], (e.fours + 1) * DMA)
                act.activation(gu_slot(gu_hi, e.slot2), gu_slot(gu_raw, e.slot4), ACT.Copy).then_inc(S["gu_hi_ready"], 1)

            def split_hi_dn(e, first):
                act.wait_ge(dn_in[e.slot4], (e.fours + 1) * 2 * DMA)
                if not first:
                    act.wait_ge(S["d_done"], e.n - 1)
                act.activation(dn_hi[:, e.slot2, :], dn_raw[:, e.slot4, :], ACT.Copy).then_inc(S["dn_hi_ready"], 1)

            def tokens_hi(e):
                s = e.slot4
                act.wait_ge(S["xt_done"], e.pair + 1)
                act.activation(xs_hi[:, s:s + 2, :, :].rearrange("p s j t -> p j s t"),
                               bank[1][:, :].rearrange("p (j s t) -> p j s t", j=NJ, s=2), ACT.Copy).then_inc(S["xs_hi_ready"], 1)

            def step(e, silu=True, hs=True, xs=True, gu=True, dn=True, y=True, first=False):
                if silu:
                    act.wait_ge(S["gu_done"], e.n + 1)
                    if not first:
                        act.wait_ge(S["h_ready"], e.n - 1)
                    act.activation(silu_e[:, e.slot2, :], gate_bank[e.slot2][0:CAP, 0:I], ACT.Silu).then_inc(S["e_silu_ready"], 1)
                if hs:
                    d = e + -1
                    act.wait_ge(S["ht_done"], d.n + 1)
                    if not (isinstance(e.i, int) and d.off < 2):
                        act.wait_ge(S["d_done"], d.n - 1)
                    act.activation(hs_hi[:, d.slot2, :], bank[2][:, 0:len(KT) * CAP], ACT.Copy).then_inc(S["hs_hi_ready"], 1)
                if xs and e.off % 2 == 0:
                    tokens_hi(e + 2)
                if gu:
                    split_hi_gu(e + 2)
                if dn:
                    split_hi_dn(e, first)
                if y:
                    d = e + -2
                    act.wait_ge(S["d_done"], d.n + 1)
                    if not (isinstance(e.i, int) and d.off < 2):
                        act.wait_ge(S["added"], (d.n - 1) * DMA)
                    act.activation(y_e[:, d.slot2, :], row_bank[d.slot2][0:CAP, :], ACT.Copy).then_inc(S["y_ready"], 1)

            act.wait_ge(S["sh_d_done"], B * TT)
            act.wait_ge(S["xrow_sent"], B * DMA)
            act.wait_ge(S["idx_ready"], 1)
            for tt in range(TT):
                act.wait_ge(y_sent[tt], B * DMA)
            tokens_hi(Expert(0, 0))
            split_hi_gu(Expert(0, 0))
            split_hi_gu(Expert(0, 1))
            for off in range(4):
                step(Expert(0, off), hs=off >= 1, y=off >= 2, first=off < 2)
            with act.Fori(1, E // 4 - 1) as i:
                for off in range(4):
                    step(Expert(i, off))
            for off in range(4):
                step(Expert(0, E - 4 + off), xs=off < 2, gu=off < 2)
            step(Expert(0, E), silu=False, xs=False, gu=False, dn=False)
            step(Expert(0, E + 1), silu=False, hs=False, xs=False, gu=False, dn=False)

            def f_split_hi_gu(c, n):
                g, r = n
                act.wait_ge(w_in[r], (c * 4 + g + 1) * DMA)
                act.wait_ge(f_gu_done[r % 2], c * 8 + g * 2 + r // 2)
                act.activation(dn_hi[:, r % 2, 0:FGU], dn_raw[:, r, 0:FGU], ACT.Copy).then_inc(S["w_gu_hi_ready"], 1)

            def turned(c, j):
                act.wait_ge(S["xa_t_done"], c * NJ + j + 1)
                act.wait_ge(S["x1_lo_ready"], c * NJ)
                act.activation(sig[:, j * T:(j + 1) * T], turn_bank[j][:, :], ACT.Sigmoid)
                if c >= 2:
                    act.wait_ge(S["out_sent"], (c - 1) * DMA)
                act.activation(x1t[c % 2][:, j * T:(j + 1) * T], turn_bank[j][:, :],
                               ACT.Copy).then_inc(S["x1t_ready"], 1)

            def x1_high(c, j):
                act.wait_ge(S["x1_ready"], c * NJ + j + 1)
                if c >= 2:
                    act.wait_ge(f_gu_done[1], (c - 1) * 8)
                act.activation(x1_hi[c % 2][:, j * T:(j + 1) * T], sig[:, j * T:(j + 1) * T], ACT.Copy).then_inc(S["x1_hi_ready"], 1)

            def f_step(c, g, r, nxt, turn=None):
                half = c * 8 + g * 2 + r // 2
                if nxt is not None:
                    f_split_hi_gu(*nxt)
                act.wait_ge(f_d_done[r % 2], half)
                act.activation(dn_hi[:, r % 2, FGU:], dn_raw[:, r, FGU:], ACT.Copy).then_inc(S["w_dn_hi_ready"], 1)
                act.wait_ge(f_gu_done[r % 2], half + 1)
                act.wait_ge(f_h[r % 2], half)
                act.activation(fsilu[r % 2], gate_bank[r % 2][:, :], ACT.Silu).then_inc(f_silu[r % 2], 1)
                if turn is not None:
                    turned(turn, 2 * r)
                    turned(turn, 2 * r + 1)
                act.wait_ge(f_h[r % 2], half + 1)
                act.activation(fh_hi[r % 2], fh[r % 2], ACT.Copy).then_inc(f_hi[r % 2], 1)

            def f_group(c, g, wkv):
                for r in range(4):
                    f_step(c, g, r, (c, (g, r + 1)) if r < 3 else (c, (g + 1, 0)))
                    if wkv and r == 0:
                        exps((B + 1 + c) * NJ + g + 1)

            def f_last_group(c, wkv, prepare):
                g = NF // 4 - 1
                for r in range(4):
                    nxt = (c, (g, r + 1)) if r < 3 else ((c + 1, (0, 0)) if prepare else None)
                    if prepare and r >= 2:
                        x1_high(c + 1, 2 * (r - 2))
                        x1_high(c + 1, 2 * (r - 2) + 1)
                    f_step(c, g, r, nxt, c + 1 if prepare and r < 2 else None)
                    if wkv and r == 0:
                        exps((B + 1 + c) * NJ + g + 1)

            act.wait_ge(S["d_done"], E)
            act.wait_ge(S["gu_done"], E)
            act.wait_ge(S["gu_lo_ready"], E)
            act.wait_ge(S["dn_lo_ready"], E)
            f_split_hi_gu(0, (0, 0))
            for j in range(NJ):
                turned(0, j)
            for j in range(NJ):
                x1_high(0, j)
            for c in range(B):
                f_group(c, 0, c < B - 1)
                with act.Fori(1, NF // 4 - 1) as g:
                    f_group(c, g, c < B - 1)
                f_last_group(c, c < B - 2, c < B - 1)

        @block.vector
        def _(vec):
            V = nc.vector

            class Chain:

                def __init__(self, sem):
                    self.sem, self.base, self.n = sem, 0, 0

                def __call__(self, ins):
                    ins.then_inc(self.sem, 1)
                    self.n += 1

                def wait(self):
                    vec.wait_ge(self.sem, self.base + self.n)

            vec.wait_ge(S["cond_in"], DMA)
            V.tensor_reduce(tf[:, :], cond_sb[:, :, :], AX_X, ALU.add).then_inc(S["csum_done"], 1)
            vec.wait_ge(S["tf_ready"], 1)
            V.tensor_scalar(half_tf[:, :], tf[:, :], 0.5, 0.5, ALU.mult, ALU.add).then_inc(S["fac_ready"], 1)
            V.tensor_scalar(out_scale[:, :], tf[:, :], 0.2, 0.8, ALU.mult, ALU.add).then_inc(S["fac_ready"], 1)
            vec.wait_ge(S["dec0_ready"], 1)
            vec.wait_ge(S["fac_ready"], 2)
            for layer in range(2):
                for b in range(B):
                    V.tensor_scalar(decay[:, (layer * B + b) * NJ:(layer * B + b + 1) * NJ],
                                    dec0[:, layer * NJ:(layer + 1) * NJ], half_tf[:, b:b + 1], None,
                                    ALU.mult).then_inc(S["fac_ready"], 1)

            wkv = Chain(S["wkv_chain"])
            WKV_OPS = 6
            for t in (den_b, num_b):
                V.memset(t[:, T - 1:T], 0.0).then_inc(S["edges_zero"], 1)

            def wkv_clamp(layer, b, j, slot, use):
                wkv.wait()
                vec.wait_ge(S["dv_ready"], (layer * B + b) * NJ + j)
                vec.wait_ge(side_in[slot], (use + 1) * DMA)
                wkv(V.tensor_scalar(ek[:, :], side_sb[:, slot, :], EXP_CAP, None, ALU.min))
                V.tensor_scalar(eu[:, :], side_sb[:, slot, :], cut(u_sb, j + layer * NJ, 1), EXP_CAP,
                                ALU.add, ALU.min).then_inc(S["k_ready"], 1)

            def wkv_scans(layer, b, j, slot):
                dec = cut(decay, (layer * B + b) * NJ + j, 1).to_broadcast([P, T])
                vec.wait_ge(S["e_ready"], (layer * B + b) * NJ + j + 1)
                vec.wait_ge(S["wkv_ready"], (layer * B + b) * NJ + j)
                V.tensor_tensor(ekv[:, :], ek[:, :], side_sb[:, slot, :], ALU.mult).then_inc(S["ekv_ready"], 1)
                V.tensor_tensor_scan(den[:, :], dec, ek[:, :], 0.0, ALU.mult, ALU.add)
                wkv(V.tensor_tensor_scan(den_b[:, T - 2::-1], ek[:, T - 1:0:-1], dec[:, 0:T - 1], 0.0, ALU.add, ALU.mult))
                wkv.wait()
                V.tensor_tensor_scan(num[:, :], dec, ekv[:, :], 0.0, ALU.mult, ALU.add)
                V.tensor_tensor_scan(num_b[:, T - 2::-1], ekv[:, T - 1:0:-1], dec[:, 0:T - 1], 0.0, ALU.add,
                                     ALU.mult).then_inc(S["scans_done"], 1)
                wkv(V.tensor_tensor(den[:, :], den[:, :], den_b[:, :], ALU.add))
                wkv.wait()
                wkv(V.tensor_tensor(den[:, :], den[:, :], eu[:, :], ALU.add))

            def wkv_recip(layer, b, j):
                unit = (layer * B + b) * NJ + j
                wkv.wait()
                if layer == 0:
                    vec.wait_ge(S["t_ready"], unit + 1)
                    wkv(V.scalar_tensor_tensor(out=den[:, :], in0=den[:, :], scalar=DEN_FLOOR, in1=one_en[:, :],
                                               op0=ALU.max, op1=ALU.mult))
                else:
                    wkv(V.tensor_scalar(den[:, :], den[:, :], DEN_FLOOR, None, ALU.max))
                wkv.wait()
                wkv(V.reciprocal(den[:, :], den[:, :]))

            def wkv_scale(layer, b, j):
                wkv.wait()
                vec.wait_ge(S["numer_ready"], (layer * B + b) * NJ + j + 1)
                V.scalar_tensor_tensor(out=cut(wkv_out, j * T, T), in0=num[:, :], scalar=cut(out_scale, b, 1),
                                       in1=den[:, :], op0=ALU.mult, op1=ALU.mult).then_inc(S["wkv_ready"], 1)

            def wkv_ratio(layer, b, j):
                wkv_recip(layer, b, j)
                wkv_scale(layer, b, j)

            def route(b):
                vec.wait_ge(S["logits_done"], b + 1)
                V.tensor_reduce(nmax[:, :], bank[0][:, 0:TT * E].rearrange("p (t e) -> p t e", e=E), AX_X,
                                ALU.max).then_inc(S["nmax_done"], 1)
                vec.wait_ge(S["nmax_done"], b + 1)
                V.tensor_scalar(nmax[:, :], nmax[:, :], -1.0, None, ALU.mult).then_inc(S["nmax_ready"], 1)
                vec.wait_ge(S["pexp_ready"], b + 1)
                chain = S["route_chain"]
                OPS = 5
                V.reciprocal(prec[:, :], psums[:, :]).then_inc(chain, 1)
                vec.wait_ge(S["xrow_sent"], b * DMA)
                vec.wait_ge(chain, b * OPS + 1)
                for tt in range(TT):
                    ins = V.tensor_scalar(xrow[:, tt, C:XR], pexp[:, tt, :], prec[:, tt:tt + 1], None, ALU.mult)
                ins.then_inc(S["p_ready"], 1)
                vec.wait_ge(S["dec0_ready"], 1)
                vec.wait_ge(S["p_ready"], b + 1)
                for tt in range(TT):
                    ins = V.max(top8[:, tt, :], xrow[:, tt, C:XR])
                ins.then_inc(S["top8_ready"], 1)
                vec.wait_ge(S["dec0_ready"], 1)
                vec.wait_ge(S["top8_ready"], b + 1)
                for tt in range(TT):
                    ins = V.max_index(top8_i[:, tt, :], top8[:, tt, :], xrow[:, tt, C:XR])
                ins.then_inc(chain, 1)
                vec.wait_ge(chain, b * OPS + 2)
                V.tensor_copy(top8_f[:, :, :], top8_i[:, :, :]).then_inc(chain, 1)
                vec.wait_ge(chain, b * OPS + 3)
                V.tensor_tensor(onehot[:, :, :, :],
                                iota_e[:, :].rearrange("p (a b e) -> p a b e", a=1, b=1).to_broadcast([P, TT, TOPK, E]),
                                top8_f[:, :, 0:TOPK].rearrange("p t (k o) -> p t k o", o=1).to_broadcast([P, TT, TOPK, E]),
                                ALU.is_equal).then_inc(chain, 1)
                vec.wait_ge(chain, b * OPS + 4)
                vec.wait_ge(S["mask_t_done"], b)
                V.tensor_reduce(mkey[:, :, :], onehot[:, :, :, :].rearrange("p t k e -> p t e k"), AX_X,
                                ALU.add).then_inc(chain, 1)
                vec.wait_ge(chain, b * OPS + 5)
                for tt in range(TT):
                    ins = V.tensor_scalar(mkey[:, tt, :], mkey[:, tt, :], cut(key_col, b * TT + tt, 1), None, ALU.mult)
                ins.then_inc(S["mask_ready"], 1)

            def shared_h(b, m):
                rows = P if m < SM - 1 else SLAST
                up = up_bank[m % 2][:, :] if m < SM - 1 else gate_bank[m % 2][SLAST:2 * SLAST, :]
                vec.wait_ge(S["sh_silu_ready"], b * SM + m + 1)
                V.tensor_tensor(h_sh[0:rows, m, :], silu_sh[0:rows, :], up, ALU.mult).then_inc(sh_h_ready[m % 2], 1)

            def shared_y(b, tt):
                s = tt % 2
                vec.wait_ge(S["sh_d_done"], b * TT + tt + 1)
                vec.wait_ge(xres_in[s], (b * 2 + tt // 2 + 1) * DMA)
                vec.wait_ge(y_sent[(tt + 2) % 4], (b + tt // 2) * DMA)
                V.tensor_tensor(y_sh[:, s, :], row_bank[s][:, :], xres[:, s, :], ALU.add).then_inc(sh_y_ready[tt], 1)

            def slot_rounds(b, first, last):
                for r in range(first, last):
                    got = slot_key[:, 8 * r:8 * r + 8]
                    vec.wait_ge(S["dec0_ready"], 1)
                    vec.wait_ge(S["keys_ready"], b + 1)
                    if r:
                        vec.wait_ge(round_cut[r - 1], b + 1)
                    else:
                        vec.wait_ge(S["best_ready"], b + 1)
                    V.max(got, keys[:, :]).then_inc(round_max[r], 1)
                    vec.wait_ge(S["dec0_ready"], 1)
                    vec.wait_ge(round_max[r], b + 1)
                    V.match_replace(keys[:, :], got, keys[:, :], 0.0).then_inc(round_cut[r], 1)

            def keep_best(b):
                vec.wait_ge(round_cut[CAP // 8 - 1], b + 1)
                V.tensor_copy(keys[:, 0:CAP], slot_key[:, :]).then_inc(S["best_ready"], 1)

            def early_step(s, shared):
                wkv.base, wkv.n = s * (NJ * WKV_OPS), 0
                wkv_clamp(0, s, 0, 0, s * 2)
                wkv_scans(0, s, 0, 0)
                if shared:
                    route(s - 1)
                for j in range(NJ):
                    if j:
                        wkv_scans(0, s, j, j % 2)
                    if j < NJ - 1:
                        wkv_clamp(0, s, j + 1, (j + 1) % 2, s * 2 + (j + 1) // 2)
                    wkv_ratio(0, s, j)
                    if shared and j < NJ - 1:
                        shared_h(s - 1, 2 * j)
                        shared_h(s - 1, 2 * j + 1)
                if shared:
                    shared_y(s - 1, 0)
                    slot_rounds(s - 1, 0, 4)
                    shared_y(s - 1, 1)
                    slot_rounds(s - 1, 4, 8)
                    keep_best(s - 1)
                    shared_y(s - 1, 2)
                    shared_y(s - 1, 3)
                assert wkv.n == NJ * WKV_OPS

            vec.wait_ge(S["fac_ready"], 2 + 2 * B)
            vec.wait_ge(S["const_in"], N_CONST * DMA)
            vec.wait_ge(S["edges_zero"], 2)
            V.memset(keys[:, 0:CAP], 0.0).then_inc(S["best_ready"], 1)
            early_step(0, False)
            with vec.Fori(1, B) as s:
                early_step(s, True)

            wkv.base, wkv.n = B * NJ * WKV_OPS, 0
            wkv_clamp(1, 0, 0, 0, 2 * B)
            wkv_scans(1, 0, 0, 0)
            route(B - 1)
            wkv_clamp(1, 0, 1, 1, 2 * B)
            wkv_ratio(1, 0, 0)
            shared_h(B - 1, 0)
            shared_h(B - 1, 1)
            slot_rounds(B - 1, 0, 8)
            vec.wait_ge(round_cut[CAP // 8 - 1], B)
            vec.engine_nop().then_inc(S["slots_ready"], 1)
            vec.wait_ge(S["slots_t_done"], 1)
            V.tensor_scalar(tok_f[:, :], bank[1][0:CAP, 0:E], -1.0, float(NT), ALU.mult, ALU.add).then_inc(S["idx_chain"], 1)
            vec.wait_ge(S["idx_chain"], 1)
            V.tensor_scalar(empty_f[:, :], tok_f[:, :], float(NT), None, ALU.is_equal).then_inc(S["idx_chain"], 1)
            halves = tok_f[:, :].rearrange("p (q o) -> p q o", o=2)
            V.tensor_scalar(gidx[0:CAP, :], halves[:, :, 0], float(NT - 1), None, ALU.min).then_inc(S["idx_chain"], 1)
            V.tensor_scalar(gidx[CAP:P, :], halves[:, :, 1], float(NT - 1), None, ALU.min).then_inc(S["idx_chain"], 1)
            vec.wait_ge(S["idx_chain"], 4)
            V.scalar_tensor_tensor(out=sidx[:, :], in0=empty_f[:, :], scalar=scol[:, 0:1], in1=tok_f[:, :],
                                   op0=ALU.mult, op1=ALU.add).then_inc(S["idx_ready"], 1)

            for j in range(1, NJ):
                wkv_scans(1, 0, j, j % 2)
                if j < NJ - 1:
                    wkv_clamp(1, 0, j + 1, (j + 1) % 2, 2 * B + (j + 1) // 2)
                else:
                    wkv_clamp(1, 1, 0, 0, 2 * B + 2)
                wkv_ratio(1, 0, j)
                if j < NJ - 1:
                    shared_h(B - 1, 2 * j)
                    shared_h(B - 1, 2 * j + 1)
            shared_y(B - 1, 0)
            shared_y(B - 1, 1)
            wkv_scans(1, 1, 0, 0)
            wkv_recip(1, 1, 0)
            shared_y(B - 1, 2)
            shared_y(B - 1, 3)

            def split_lo_gu(e):
                vec.wait_ge(S["gu_hi_ready"], e.n + 1)
                V.tensor_tensor(gu_slot(gu_lo, e.slot2), gu_slot(gu_raw, e.slot4), gu_slot(gu_hi, e.slot2).bitcast(F32),
                                ALU.subtract).then_inc(S["gu_lo_ready"], 1)

            def split_lo_dn(e):
                vec.wait_ge(S["dn_hi_ready"], e.n + 1)
                V.tensor_tensor(dn_lo[:, e.slot2, :], dn_raw[:, e.slot4, :], dn_hi[:, e.slot2, :].bitcast(F32),
                                ALU.subtract).then_inc(S["dn_lo_ready"], 1)

            def tokens(e):
                s, q = e.slot4, e.pair
                half = (e.off // 2) % 2
                vec.wait_ge(xg_in[half], (e.fours + 1) * DMA)
                V.scalar_tensor_tensor(out=wsel[:, :], in0=iota_e[:, :], scalar=cut(pair_e, q, 1),
                                       in1=xg[:, half, C:XR], op0=ALU.is_equal, op1=ALU.mult,
                                       accum_out=w_pair[:, half:half + 1]).then_inc(S["wsel_done"], 1)
                vec.wait_ge(S["wsel_done"], q + 1)
                V.tensor_copy(w_odd[:, half:half + 1], w_pair[CAP:P, half:half + 1]).then_inc(S["wslot_ready"], 1)
                vec.wait_ge(S["xs_hi_ready"], q + 1)
                hi = xs_hi[:, s:s + 2, :, :].bitcast(F32).rearrange("p s j t -> p j s t")
                V.tensor_tensor(xs_lo[:, s:s + 2, :, :].rearrange("p s j t -> p j s t"),
                                bank[1][:, :].rearrange("p (j s t) -> p j s t", j=NJ, s=2), hi,
                                ALU.subtract).then_inc(S["xs_lo_ready"], 1)

            def step(e, h=True, hs=True, xs=True, gu=True, dn=True):
                half = (e.off // 2) % 2
                if h:
                    w = w_pair[0:CAP, half:half + 1] if e.slot2 == 0 else w_odd[:, half:half + 1]
                    vec.wait_ge(S["wslot_ready"], e.pair + 1)
                    vec.wait_ge(S["e_silu_ready"], e.n + 1)
                    if not (isinstance(e.i, int) and e.off < 2):
                        vec.wait_ge(S["ht_done"], e.n - 1)
                    V.scalar_tensor_tensor(out=h_e[:, e.slot2, :], in0=silu_e[:, e.slot2, :], scalar=w,
                                           in1=up_bank[e.slot2][0:CAP, 0:I], op0=ALU.mult, op1=ALU.mult).then_inc(S["h_ready"], 1)
                if hs:
                    d = e + -1
                    vec.wait_ge(S["hs_hi_ready"], d.n + 1)
                    V.tensor_tensor(hs_lo[:, d.slot2, :], bank[2][:, 0:len(KT) * CAP], hs_hi[:, d.slot2, :].bitcast(F32),
                                    ALU.subtract).then_inc(S["hs_lo_ready"], 1)
                if xs and e.off % 2 == 0:
                    tokens(e + 2)
                if gu:
                    split_lo_gu(e + 2)
                if dn:
                    split_lo_dn(e)

            vec.wait_ge(S["sh_d_done"], B * TT)
            for tt in range(TT):
                vec.wait_ge(y_sent[tt], B * DMA)
            V.memset(bank[2][96:P, 2 * CAP:3 * CAP], 0.0).then_inc(S["bank_pad"], 1)
            tokens(Expert(0, 0))
            split_lo_gu(Expert(0, 0))
            split_lo_gu(Expert(0, 1))
            for off in range(4):
                step(Expert(0, off), hs=off >= 1)
            with vec.Fori(1, E // 4 - 1) as i:
                for off in range(4):
                    step(Expert(i, off))
            for off in range(4):
                step(Expert(0, E - 4 + off), xs=off < 2, gu=off < 2)
            step(Expert(0, E), h=False, xs=False, gu=False, dn=False)

            def f_split_lo_gu(c, n):
                g, r = n
                vec.wait_ge(S["w_gu_hi_ready"], c * NF + g * 4 + r + 1)
                V.tensor_tensor(dn_lo[:, r % 2, 0:FGU], dn_raw[:, r, 0:FGU], dn_hi[:, r % 2, 0:FGU].bitcast(F32),
                                ALU.subtract).then_inc(w_gu_lo[r], 1)

            def f_step(c, g, r, nxt):
                half = c * 8 + g * 2 + r // 2
                if nxt is not None:
                    f_split_lo_gu(*nxt)
                vec.wait_ge(S["w_dn_hi_ready"], c * NF + g * 4 + r + 1)
                V.tensor_tensor(dn_lo[:, r % 2, FGU:], dn_raw[:, r, FGU:], dn_hi[:, r % 2, FGU:].bitcast(F32),
                                ALU.subtract).then_inc(w_dn_lo[r], 1)
                vec.wait_ge(f_lo[r % 2], half)
                vec.wait_ge(f_silu[r % 2], half + 1)
                V.tensor_tensor(fh[r % 2], fsilu[r % 2], up_bank[r % 2][:, :], ALU.mult).then_inc(f_h[r % 2], 1)
                vec.wait_ge(f_hi[r % 2], half + 1)
                V.tensor_tensor(fh_lo[r % 2], fh[r % 2], fh_hi[r % 2].bitcast(F32), ALU.subtract).then_inc(f_lo[r % 2], 1)

            def x1_part(c, j):
                vec.wait_ge(S["x1t_ready"], c * NJ + j + 1)
                V.tensor_tensor(sig[:, j * T:(j + 1) * T], sig[:, j * T:(j + 1) * T],
                                wkv_out[:, j * T:(j + 1) * T], ALU.mult).then_inc(S["x1_ready"], 1)

            def x1_low(c, j):
                vec.wait_ge(S["x1_hi_ready"], c * NJ + j + 1)
                V.tensor_tensor(x1_lo[c % 2][:, j * T:(j + 1) * T], sig[:, j * T:(j + 1) * T],
                                x1_hi[c % 2][:, j * T:(j + 1) * T].bitcast(F32), ALU.subtract).then_inc(S["x1_lo_ready"], 1)
            def f_out(c):
                vec.wait_ge(f_d_done[1], c * 8 + 8)
                vec.wait_ge(f_d_done[0], c * 8 + 8)
                for j in range(NJ):
                    V.tensor_tensor(x1t[c % 2][:, j * T:(j + 1) * T], bank[j][:, :], x1t[c % 2][:, j * T:(j + 1) * T],
                                    ALU.add).then_inc(S["out_ready"], 1)

            def f_group(c, g, unit, out=False, prepare=False, nxt_chunk=True):
                wkv.base, wkv.n = ((B + c + 1) * NJ + g + 1) * WKV_OPS, 0
                for r in range(4):
                    nxt = (c, (g, r + 1)) if r < 3 else ((c, (g + 1, 0)) if nxt_chunk else None)
                    f_step(c, g, r, nxt)
                    if out and r == 0:
                        f_out(c - 1)
                    if prepare and r in (1, 2):
                        x1_part(c + 1, 2 * (r - 1))
                        x1_part(c + 1, 2 * (r - 1) + 1)
                    if prepare and r in (2, 3):
                        x1_low(c + 1, 2 * (r - 2))
                        x1_low(c + 1, 2 * (r - 2) + 1)
                    if unit is not None:
                        if r == 0:
                            wkv_clamp(1, unit[0], unit[1], 0, 2 * B + 3 + c * 4 + g)
                        elif r == 1:
                            wkv_scans(1, unit[0], unit[1], 0)
                        elif r == 2:
                            wkv_recip(1, unit[0], unit[1])
                        else:
                            wkv_scale(1, unit[0], unit[1])

            LAST = NF // 4 - 1
            f_split_lo_gu(0, (0, 0))
            for j in range(NJ):
                x1_part(0, j)
            for j in range(NJ):
                x1_low(0, j)
            wkv.base, wkv.n = ((B + 1) * NJ + 1) * WKV_OPS, 0
            wkv_scale(1, 1, 0)
            for c in range(B):
                f_group(c, 0, (c + 1, 1) if c < B - 1 else None, out=c > 0)
                with vec.Fori(1, LAST) as g:
                    f_group(c, g, (c + 1, g + 1) if c < B - 1 else None)
                f_group(c, LAST, (c + 2, 0) if c < B - 2 else None, prepare=c < B - 1, nxt_chunk=c < B - 1)
            f_out(B - 1)

        @block.tensor
        def _(pe):
            pe.wait_ge(S["const_in"], N_CONST * DMA)
            pe.wait_ge(S["sgu_in"], DMA)
            pe.wait_ge(S["sdn_in"], 2 * DMA)

            def turn_slots():
                pe.wait_ge(S["xrow_copied"], B * TT)
                pe.wait_ge(S["slots_ready"], 1)
                pe.transpose(bank[1][0:CAP, 0:E], slot_key[:, :], idt[0:E, 0:E]).then_inc(S["slots_t_done"], 1)

            def batch(b, last=False):
                pe.wait_ge(S["x0_ready"], b + 1)
                pe.wait_ge(sh_y_ready[3], b)
                for tt in range(TT):
                    for j in range(NJ):
                        mm = pe.matmul(bank[0][:, tt * E:(tt + 1) * E], x0[:, j * T + tt * P:j * T + (tt + 1) * P],
                                       gate_sb[:, j * E:(j + 1) * E], start=j == 0, stop=j == NJ - 1)
                mm.then_inc(S["logits_done"], 1)
                for tt in range(TT):
                    pe.wait_ge(S["xrow_copied"], b * TT + tt)
                    for j in range(NJ):
                        mm = pe.transpose(bank[1][:, j * P:(j + 1) * P], x0[:, j * T + tt * P:j * T + (tt + 1) * P], idt[:, :])
                    mm.then_inc(S["tok_t_done"], 1)
                for m in range(SM):
                    pe.wait_ge(sh_h_ready[m % 2], b * (SM // 2) + m // 2)
                    for side, dst in enumerate((gate_bank[m % 2], up_bank[m % 2])[:2 if m < SM - 1 else 1]):
                        for j in range(NJ):
                            mm = pe.matmul(dst[:, :], sgu[:, j, (2 * m + side) * P:(2 * m + side + 1) * P],
                                           x0[:, j * T:(j + 1) * T], start=j == 0, stop=j == NJ - 1)
                    mm.then_inc(S["sh_gu_done"], 1)
                    if last and m == 3:
                        turn_slots()
                    if m == 1:
                        pe.wait_ge(S["sgu_in"], DMA)
                        pe.wait_ge(S["mask_ready"], b + 1)
                        pe.wait_ge(S["keys_ready"], b)
                        for tt in range(TT):
                            mm = pe.transpose(bank[2][0:E, tt * P:(tt + 1) * P], mkey[:, tt, :], idt[:, :])
                        mm.then_inc(S["mask_t_done"], 1)
                for s in range(2):
                    pe.wait_ge(sh_h_ready[s], b * (SM // 2) + SM // 2)
                pe.wait_ge(S["pexp_ready"], b + 1)
                for tt in range(TT):
                    pe.wait_ge(sh_y_ready[(tt + 2) % 4], b + tt // 2)
                    for k in range(SM):
                        rows = P if k < SM - 1 else SLAST
                        mm = pe.matmul(row_bank[tt % 2][:, :], h_sh[0:rows, k, tt * P:(tt + 1) * P], sdn[0:rows, k, :],
                                       start=k == 0, stop=k == SM - 1)
                    mm.then_inc(S["sh_d_done"], 1)

            with pe.Fori(0, B - 1) as b:
                batch(b)
            batch(B - 1, last=True)

            def tokens(e, first=False):
                half = (e.off // 2) % 2
                pe.wait_ge(xg_in[half], (e.fours + 1) * DMA)
                if not first:
                    pe.wait_ge(S["xs_lo_ready"], e.pair)
                for j in range(NJ):
                    mm = pe.transpose(bank[1][:, j * P:(j + 1) * P], xg[:, half, j * P:(j + 1) * P], idt[:, :])
                mm.then_inc(S["xt_done"], 1)

            def gate_up(e):
                s, s4 = e.slot2, e.slot4
                pe.wait_ge(S["gu_lo_ready"], e.n + 1)
                pe.wait_ge(S["xs_lo_ready"], e.pair + 1)
                if not (isinstance(e.i, int) and e.off < 2):
                    pe.wait_ge(S["h_ready"], e.n - 1)
                for j in range(NJ):
                    for n, (x, w) in enumerate(((xs_hi, gu_hi), (xs_hi, gu_lo), (xs_lo, gu_hi))):
                        for side, dst in enumerate((gate_bank[s], up_bank[s])):
                            at = s * GUW + (2 * j + side) * I
                            mm = pe.matmul(dst[0:CAP, 0:I], x[:, s4, j, :], w[:, at:at + I],
                                           start=j == 0 and n == 0, stop=j == NJ - 1 and n == 2)
                mm.then_inc(S["gu_done"], 1)

            def turn_h(e):
                pe.wait_ge(S["bank_pad"], 1)
                pe.wait_ge(S["h_ready"], e.n + 1)
                if not (isinstance(e.i, int) and e.off < 1):
                    pe.wait_ge(S["hs_lo_ready"], e.n)
                for k, rows in KT:
                    mm = pe.transpose(bank[2][0:rows, k * CAP:(k + 1) * CAP], h_e[:, e.slot2, k * P:k * P + rows],
                                      idt[0:CAP, 0:CAP])
                mm.then_inc(S["ht_done"], 1)

            def down(e):
                s = e.slot2
                pe.wait_ge(S["hs_lo_ready"], e.n + 1)
                pe.wait_ge(S["dn_lo_ready"], e.n + 1)
                if not (isinstance(e.i, int) and e.off < 2):
                    pe.wait_ge(S["y_ready"], e.n - 1)
                for k, rows in KT:
                    for n, (h, w) in enumerate(((hs_hi, dn_hi), (hs_hi, dn_lo), (hs_lo, dn_hi))):
                        mm = pe.matmul(row_bank[s][0:CAP, :], h[0:rows, s, k * CAP:(k + 1) * CAP],
                                       w[0:rows, s, k * C:(k + 1) * C], start=k == 0 and n == 0,
                                       stop=k == len(KT) - 1 and n == 2)
                mm.then_inc(S["d_done"], 1)

            def step(e, gu=True, th=True, xt=True, dn=True):
                if gu:
                    gate_up(e)
                if th:
                    turn_h(e + -1)
                if xt and e.off % 2 == 0:
                    tokens(e + 2)
                if dn:
                    down(e + -2)

            pe.wait_ge(S["idx_ready"], 1)
            tokens(Expert(0, 0), first=True)
            for off in range(4):
                step(Expert(0, off), th=off >= 1, dn=off >= 2)
            with pe.Fori(1, E // 4 - 1) as i:
                for off in range(4):
                    step(Expert(i, off))
            for off in range(4):
                step(Expert(0, E - 4 + off), xt=off < 2)
            step(Expert(0, E), gu=False, xt=False)
            step(Expert(0, E + 1), gu=False, th=False, xt=False)

            def turn_tokens(c, j):
                for tt in range(TT):
                    mm = pe.transpose(turn_bank[j][:, tt * P:(tt + 1) * P], xa[:, tt * C + j * P:tt * C + (j + 1) * P], idt[:, :])
                mm.then_inc(S["xa_t_done"], 1)

            def f_gate_up(c, g, r):
                s = r % 2
                pe.wait_ge(w_gu_lo[r], c * 4 + g + 1)
                pe.wait_ge(f_h[s], c * 8 + g * 2 + r // 2)
                for side, dst in enumerate((gate_bank[s], up_bank[s])):
                    for j in range(NJ):
                        at = (2 * j + side) * P
                        for n, (w, x) in enumerate(((dn_hi, x1_hi), (dn_hi, x1_lo), (dn_lo, x1_hi))):
                            mm = pe.matmul(dst[:, :], w[:, s, at:at + P], x[c % 2][:, j * T:(j + 1) * T],
                                           start=j == 0 and n == 0, stop=j == NJ - 1 and n == 2)
                mm.then_inc(f_gu_done[s], 1)

            def f_down(c, g, r, first=False, last=False):
                s = r % 2
                pe.wait_ge(w_dn_lo[r], c * 4 + g + 1)
                pe.wait_ge(f_lo[s], c * 8 + g * 2 + r // 2 + 1)
                if first:
                    pe.wait_ge(S["out_ready"], c * NJ)
                for ct in range(NJ):
                    at = FGU + ct * P
                    for n, (w, h) in enumerate(((dn_hi, fh_hi), (dn_hi, fh_lo), (dn_lo, fh_hi))):
                        mm = pe.matmul(bank[ct][:, :], w[:, s, at:at + P], h[s], start=first and n == 0,
                                       stop=last and n == 2, skip_group_check=True)
                mm.then_inc(f_d_done[s], 1)

            def f_group(c, g, prepare=False):
                first_group = isinstance(g, int) and g == 0
                for r in range(4):
                    if prepare and r in (1, 2):
                        pe.wait_ge(S["x1t_ready"], (c + 1) * NJ + 2 * r)
                    if first_group and r == 0:
                        pe.wait_ge(S["x1_lo_ready"], (c + 1) * NJ)
                    f_gate_up(c, g, r)
                    if prepare and r < 2:
                        pe.wait_ge(S["xa_in"], (c + 2) * DMA)
                        pe.wait_ge(f_h[1 - r], c * 8 + g * 2 + r)
                        turn_tokens(c + 1, 2 * r)
                        turn_tokens(c + 1, 2 * r + 1)
                    if r:
                        f_down(c, g, r - 1, first=first_group and r == 1)
                    elif not first_group:
                        f_down(c, g - 1, 3)
                    elif c:
                        f_down(c - 1, LAST, 3, last=True)

            LAST = NF // 4 - 1
            pe.wait_ge(S["h_ready"], E)
            pe.wait_ge(S["y_ready"], E)
            pe.wait_ge(S["xa_in"], DMA)
            for j in range(NJ):
                turn_tokens(0, j)
            for c in range(B):
                f_group(c, 0)
                with pe.Fori(1, LAST) as g:
                    f_group(c, g)
                f_group(c, LAST, prepare=c < B - 1)
            f_down(B - 1, LAST, 3, last=True)


def channel_major(a, np):
    b, t, c = a.shape
    return np.ascontiguousarray(a.transpose(0, 2, 1).reshape(b, c // 128, 128, t).transpose(0, 2, 1, 3)).reshape(b, 128, -1)


def by_partition(w, np):
    return np.ascontiguousarray(w.reshape(-1, 128, w.shape[-1]).transpose(1, 0, 2))


def kernel(**inputs):
    import numpy as np
    from concourse import bacc
    from concourse.bass_utils import run_bass_kernel_spmd

    a = {k: np.asarray(v) for k, v in inputs.items()}
    B, T, C = a["x"].shape
    E, _, I = a["L0_ffn_w_gate"].shape
    IS = a["L0_ffn_sw_gate"].shape[1]
    F = a["L1_ffn_w_down"].shape[1]

    def layers(name):
        return np.concatenate([a[f"L{n}_cond_{name}"].reshape(4, 128).T for n in range(2)], axis=1)

    moe = np.concatenate([a["L0_ffn_w_gate"].reshape(E, 4, 128, I), a["L0_ffn_w_up"].reshape(E, 4, 128, I)], axis=3)
    moe = np.ascontiguousarray(moe.transpose(0, 2, 1, 3)).reshape(E, 128, -1)
    full = IS // 128
    tiles = []
    for m in range(full):
        tiles += [a["L0_ffn_sw_gate"][:, m * 128:(m + 1) * 128], a["L0_ffn_sw_up"][:, m * 128:(m + 1) * 128]]
    tiles += [a["L0_ffn_sw_gate"][:, full * 128:], a["L0_ffn_sw_up"][:, full * 128:]]
    shared_gu = by_partition(np.concatenate(tiles, axis=1), np)
    w = a["L1_ffn_w_gate_up"].T.reshape(4, 128, 2, F // 128, 128)
    w = w.transpose(3, 1, 0, 2, 4).reshape(F // 128, 128, -1)
    ffn = np.ascontiguousarray(np.concatenate([w, a["L1_ffn_w_down"].T.reshape(F // 128, 128, C)], axis=2))

    part = np.arange(128)
    arrays = {
        "x_t": channel_major(a["x"], np),
        "side_t": channel_major(a["fside_BxSxS_0"], np),
        "x_rows": np.ascontiguousarray(a["x"].reshape(B * T, C)),
        "cond": np.ascontiguousarray(a["cond_512"]),
        "wkv_w": np.ascontiguousarray(layers("w")),
        "wkv_u": np.ascontiguousarray(layers("u")),
        "gate_w": by_partition(np.ascontiguousarray(a["L0_ffn_gate_w"].T), np),
        "moe_gu": moe,
        "moe_down": np.ascontiguousarray(a["L0_ffn_w_down"]),
        "shared_gu": shared_gu,
        "shared_down": np.ascontiguousarray(a["L0_ffn_sw_down"]),
        "ffn_w": ffn,
        "ident": np.eye(128, dtype=np.float32),
        "expert_iota": np.tile(np.arange(E, dtype=np.float32), (128, 1)),
        "pair_expert": (2 * np.arange(E // 2)[None, :] + (part >= 64)[:, None]).astype(np.float32),
        "token_key": (B * T - (np.arange(B * T // 128)[None, :] * 128 + part[:, None])).astype(np.float32),
        "slot_col": np.arange(64, dtype=np.float32).reshape(64, 1),
    }
    nc = bacc.Bacc("TRN2", target_bir_lowering=False, num_devices=1)
    args = [nc.dram_tensor(f"in_{k}", v.shape, mybir.dt.from_np(v.dtype), kind="ExternalInput").ap() for k, v in arrays.items()]
    out = nc.dram_tensor("out_t", (B, 128, 4 * T), F32, kind="ExternalOutput").ap()
    adaln_ffn_kernel(nc, *args, out)
    r = run_bass_kernel_spmd(nc, [{f"in_{k}": v for k, v in arrays.items()}], core_ids=[0])
    y = r.results[0]["out_t"].reshape(B, 128, 4, T)
    return np.ascontiguousarray(y.transpose(0, 3, 2, 1)).reshape(B, T, C)
```

```python
from contextlib import ExitStack

import concourse.bass as bass
from concourse import mybir

P = 128
ALU = mybir.AluOpType
ACT = mybir.ActivationFunctionType
AX_X = mybir.AxisListType.X
F32 = mybir.dt.float32
F32R = mybir.dt.float32r
U32 = mybir.dt.uint32

EXP_CAP = 30.0
DEN_FLOOR = 1e-8
TOPK = 6
CAP = 64
DMA = 16


class Expert:

    def __init__(self, i, off):
        self.i, self.off = i, off

    def __add__(self, d):
        return Expert(self.i, self.off + d)

    @property
    def n(self):
        return self.i * 4 + self.off

    @property
    def pair(self):
        return self.i * 2 + self.off // 2

    @property
    def slot2(self):
        return self.off % 2

    @property
    def slot4(self):
        return self.off % 4

    @property
    def fours(self):
        return self.i + self.off // 4


def adaln_ffn_kernel(nc, x_t, side_t, x_rows, cond, wkv_w, wkv_u, gate_w, moe_gu, moe_down,
                     shared_gu, shared_down, ffn_w, ident, expert_iota, pair_expert, token_key,
                     slot_col, out):
    B, _, BT = x_t.shape
    NJ = 4
    T = BT // NJ
    C = NJ * P
    NT = B * T
    TT = T // P
    E = gate_w.shape[2]
    XR = C + E
    I = moe_down.shape[1]
    GUW = NJ * 2 * I
    KT = [(k, min(P, I - k * P)) for k in range((I + P - 1) // P)]
    DNW = len(KT) * C
    SGW = shared_gu.shape[2]
    SM = shared_down.shape[0] // P + 1
    SLAST = shared_down.shape[0] - (SM - 1) * P
    NF = ffn_w.shape[0]
    FGU = NJ * 2 * P
    assert FGU + C == DNW and NF == 16 and E == 64 and B == 4 and TT == 4

    x0_rows = nc.dram_tensor("x0_rows", (NT, XR), F32, kind="Internal").ap()
    acc = nc.dram_tensor("acc_rows", (NT + CAP, C), F32, kind="Internal").ap()

    with ExitStack() as ctx:
        def sb(name, shape, dt=F32, stack=ctx):
            return stack.enter_context(nc.sbuf_tensor(name, shape, dt))

        bank = [ctx.enter_context(nc.psum_tensor(f"bank{n}", [P, 512], F32)) for n in range(8)]
        gate_bank, up_bank = (bank[4], bank[6]), (bank[5], bank[7])
        turn_bank = (bank[6], bank[7], bank[4], bank[5])
        sh_bank = (bank[3], bank[4], bank[6], bank[7])
        row_bank = (bank[3], bank[0])

        idt, iota_e, pair_e = sb("idt", [P, P]), sb("iota_e", [P, E]), sb("pair_e", [P, E // 2])
        key_col, scol = sb("key_col", [P, NT // P]), sb("scol", [CAP, 1])
        gate_sb = sb("gate_sb", [P, NJ * E])
        w_sb, u_sb = sb("w_sb", [P, 2 * NJ]), sb("u_sb", [P, 2 * NJ])
        cond_sb = sb("cond_sb", [P, B, P])
        tf, half_tf, out_scale = sb("tf", [P, B]), sb("half_tf", [P, B]), sb("out_scale", [P, B])
        dec0 = sb("dec0", [P, 2 * NJ])
        decay = sb("decay", [P, 2 * B * NJ])

        side_sb, x_sb = sb("side_sb", [P, 2, T]), sb("x_sb", [P, 2, T])
        ek, eu = sb("ek", [P, T]), sb("eu", [P, T])
        one_en = sb("one_en", [P, T])
        ekv, dv = sb("ekv", [P, T]), sb("dv", [P, T])
        den, den_b = sb("den", [P, T]), sb("den_b", [P, T])
        num, num_b = sb("num", [P, T]), sb("num_b", [P, T])
        wkv_out = sb("wkv_out", [P, NJ * T])

        gu_raw, dn_raw = sb("gu_raw", [P, 4 * GUW]), sb("dn_raw", [P, 4, DNW])
        gidx, sidx = sb("gidx", [P, E // 2], U32), sb("sidx", [CAP, E], U32)
        gidx_now, sidx_now = sb("gidx_now", [P, 2], U32), sb("sidx_now", [CAP, 2], U32)
        xg = sb("xg", [P, 2, XR])

        with ExitStack() as early:
            sgu = sb("sgu", [P, NJ, SGW], stack=early)
            x0 = sb("x0", [P, NJ * T], stack=early)
            xrow = sb("xrow", [P, TT, XR], stack=early)
            nmax, psums = sb("nmax", [P, TT], stack=early), sb("psums", [P, TT], stack=early)
            prec, pexp = sb("prec", [P, TT], stack=early), sb("pexp", [P, TT, E], stack=early)
            top8, top8_i = sb("top8", [P, TT, 8], stack=early), sb("top8_i", [P, TT, 8], U32, early)
            top8_f = sb("top8_f", [P, TT, 8], stack=early)
            onehot = sb("onehot", [P, TT, TOPK, E], stack=early)
            mkey = sb("mkey", [P, TT, E], stack=early)
            keys = sb("keys", [E, CAP + T], stack=early)
            slot_key = sb("slot_key", [E, CAP], stack=early)
            tok_f, empty_f = sb("tok_f", [CAP, E], stack=early), sb("empty_f", [CAP, E], stack=early)
            silu_sh = sb("silu_sh", [P, T], stack=early)
            sdn, h_sh = sb("sdn", [P, SM, C], stack=early), sb("h_sh", [P, SM, T], stack=early)
            xres, y_sh = sb("xres", [P, 2, C], stack=early), sb("y_sh", [P, 2, C], stack=early)
        gu_hi, gu_lo = sb("gu_hi", [P, 2 * GUW], F32R), sb("gu_lo", [P, 2 * GUW], F32R)
        xs_hi, xs_lo = sb("xs_hi", [P, 4, NJ, CAP], F32R), sb("xs_lo", [P, 4, NJ, CAP], F32R)
        wsel, w_pair, w_odd = sb("wsel", [P, E]), sb("w_pair", [P, 2]), sb("w_odd", [CAP, 2])
        dn_hi, dn_lo = sb("dn_hi", [P, 2, DNW], F32R), sb("dn_lo", [P, 2, DNW], F32R)
        silu_e, h_e = sb("silu_e", [CAP, 2, I]), sb("h_e", [CAP, 2, I])
        hs_hi, hs_lo = sb("hs_hi", [P, 2, len(KT) * CAP], F32R), sb("hs_lo", [P, 2, len(KT) * CAP], F32R)
        y_e = sb("y_e", [CAP, 2, C])
        CH = NJ * T
        xa, sig = gu_raw[:, 0:CH], gu_raw[:, CH:2 * CH]
        x1t = [gu_raw[:, n * CH:(n + 1) * CH] for n in (2, 3)]
        fh = [gu_raw[:, 4 * CH + n * T:4 * CH + (n + 1) * T] for n in range(2)]
        fsilu = [gu_raw[:, 4 * CH + (2 + n) * T:4 * CH + (3 + n) * T] for n in range(2)]
        x1_hi, x1_lo = ([t[:, n * CH:(n + 1) * CH] for n in range(2)] for t in (gu_hi, gu_lo))
        fh_hi, fh_lo = ([t[:, 2 * CH + n * T:2 * CH + (n + 1) * T] for n in range(2)] for t in (gu_hi, gu_lo))

        S = {name: ctx.enter_context(nc.semaphore(name)) for name in ("cond_in wu_in const_in sgu_in sdn_in csum_done tf_ready exp_w_done dec0_ready fac_ready "
                     "k_ready e_ready ekv_ready dv_ready den_scanned den_added scans_done num_added numer_ready edges_zero t_ready wkv_ready wkv_chain x0_ready logits_done "
                     "tok_t_done xrow_sent nmax_done nmax_ready pexp_ready p_ready route_chain "
                     "mask_ready mask_t_done keys_ready sh_gu_done sh_silu_ready sh_d_done dummy_in "
                     "best_ready slots_ready slots_t_done idx_chain idx_ready dn_pad bank_pad "
                     "gu_hi_ready gu_lo_ready dn_hi_ready dn_lo_ready xt_done xs_hi_ready xs_lo_ready "
                     "wsel_done wslot_ready gu_done e_silu_ready h_ready ht_done hs_hi_ready hs_lo_ready "
                     "d_done y_ready added gcol_first gcol_ready scol_ready top8_ready "
                     "w_gu_hi_ready w_dn_hi_ready xa_t_done x1t_ready sig_ready x1_ready "
                     "x1_hi_ready x1_lo_ready out_ready out_sent").split()}

        def ring(name, n):
            return [ctx.enter_context(nc.semaphore(f"{name}{k}")) for k in range(n)]

        side_in, x_in, x_used = ring("side_in", 2), ring("x_in", 2), ring("x_used", 2)
        sh_h_ready, sh_y_ready, y_sent, xres_in = ring("sh_h_ready", 2), ring("sh_y_ready", 4), ring("y_sent", 4), ring("xres_in", 2)
        gu_in, dn_in, xg_in, xa_in = ring("gu_in", 4), ring("dn_in", 4), ring("xg_in", 2), ring("xa_in", 2)
        w_in, w_gu_lo, w_dn_lo = ring("w_in", 4), ring("w_gu_lo", 4), ring("w_dn_lo", 4)
        f_gu_done, f_silu, f_h, f_hi, f_lo, f_d_done = (
            ring(n, 2) for n in ("f_gu_done", "f_silu", "f_h", "f_hi", "f_lo", "f_d_done"))
        xrow_copied = ring("xrow_copied", TT)
        round_max, round_cut = ring("round_max", CAP // 8), ring("round_cut", CAP // 8 - 1)
        N_CONST = 6

        late_units = ((0, 1, side_sb[:, 1, :], side_in[1], 2 * B), (0, 2, x_sb[:, 0, :], x_in[0], 2 * B),
                      (0, 3, x_sb[:, 1, :], x_in[1], 2 * B), (1, 0, side_sb[:, 0, :], side_in[0], 2 * B + 1))
        parts = ((1, 4), (5, 8), (9, 12), (13, E // 4 - 1))

        def cut(buf, start, size):
            return buf[:, start:start + size] if isinstance(start, int) else buf[:, bass.ds(start, size)]

        def gu_slot(buf, s):
            return buf[:, s * GUW:(s + 1) * GUW]

        block = ctx.enter_context(nc.Block())

        @block.sync
        def _(sp):
            sp.dma_start(cond_sb[:, :, :], cond.rearrange("(o b) t -> o b t", o=1).to_broadcast([P, B, P])).then_inc(S["cond_in"], DMA)
            sp.dma_start(w_sb[:, :], wkv_w).then_inc(S["wu_in"], DMA)
            sp.dma_start(u_sb[:, :], wkv_u).then_inc(S["wu_in"], DMA)

            def load_side(b, j, slot, read):
                if read is not None:
                    sp.wait_ge(S["dv_ready"], read)
                sp.dma_start(side_sb[:, slot, :], cut(side_t[b], j * T, T)).then_inc(side_in[slot], DMA)

            def load_unit(b, j):
                load_side(b, j, j % 2, b * NJ + j - 1 if not isinstance(b, int) or b or j > 1 else None)
                sp.wait_ge(x_used[j % 2], b * 2 + j // 2)
                sp.dma_start(x_sb[:, j % 2, :], cut(x_t[b], j * T, T)).then_inc(x_in[j % 2], DMA)

            def rows(t, b, tt):
                return t[bass.ds(b * T + tt * P, P), :]

            def load_residual(b, tt):
                sp.wait_ge(sh_y_ready[(tt + 2) % 4], b + tt // 2)
                sp.dma_start(xres[:, tt % 2, :], rows(x_rows, b, tt)).then_inc(xres_in[tt % 2], DMA)

            def store_x0(b):
                sp.wait_ge(xrow_copied[TT - 1], b + 1)
                sp.wait_ge(S["p_ready"], b + 1)
                sp.dma_start(x0_rows[bass.ds(b * T, T), :].rearrange("(t p) c -> p t c", p=P),
                             xrow[:, :, :]).then_inc(S["xrow_sent"], DMA)

            def store_rows(b, tt):
                sp.wait_ge(sh_y_ready[tt], b + 1)
                sp.dma_start(rows(acc, b, tt), y_sh[:, tt % 2, :]).then_inc(y_sent[tt], DMA)

            def store_batch(b):
                store_rows(b, 0)
                load_residual(b, 2)
                store_rows(b, 1)
                load_residual(b, 3)
                store_rows(b, 2)
                store_rows(b, 3)

            def early_step(s, ahead):
                load_residual(s - 1, 0)
                load_residual(s - 1, 1)
                load_unit(s, 2)
                load_unit(s, 3)
                store_x0(s - 1)
                ahead()
                store_batch(s - 1)

            def load_gu(e, first=False):
                s = e.slot4
                if not first:
                    sp.wait_ge(S["gu_lo_ready"], e.n - 3)
                sp.dma_start(gu_slot(gu_raw, s), moe_gu[e.n]).then_inc(gu_in[s], DMA)

            def load_dn(e, first=False):
                s = e.slot4
                if not first:
                    sp.wait_ge(S["dn_lo_ready"], e.n - 3)
                sp.dma_start(dn_raw[:, s, 0:2 * C].rearrange("p (k c) -> p k c", k=2),
                             moe_down[e.n][0:2 * P, :].rearrange("(k p) c -> p k c", p=P)).then_inc(dn_in[s], DMA)
                sp.dma_start(dn_raw[0:I - 2 * P, s, 2 * C:3 * C], moe_down[e.n][2 * P:I, :]).then_inc(dn_in[s], DMA)

            load_unit(0, 0)
            for dst, src in ((idt[:, :], ident), (iota_e[:, :], expert_iota), (pair_e[:, :], pair_expert),
                             (key_col[:, :], token_key), (scol[:, :], slot_col),
                             (gate_sb[:, :], gate_w.rearrange("p j e -> p (j e)"))):
                sp.dma_start(dst, src).then_inc(S["const_in"], DMA)
            for j in range(1, NJ):
                load_unit(0, j)
            sp.dma_start(sgu[:, :, :], shared_gu).then_inc(S["sgu_in"], DMA)
            sp.dma_start(sdn[:, 0:SM - 1, :], shared_down[0:(SM - 1) * P, :].rearrange("(k p) c -> p k c", p=P)).then_inc(S["sdn_in"], DMA)
            sp.dma_start(sdn[0:SLAST, SM - 1, :], shared_down[(SM - 1) * P:, :]).then_inc(S["sdn_in"], DMA)
            load_unit(1, 0)
            load_unit(1, 1)
            with sp.Fori(1, B - 1) as s:
                early_step(s, lambda: (load_unit(s + 1, 0), load_unit(s + 1, 1)))
            early_step(B - 1, lambda: load_side(0, 0, 0, B * NJ - 1))
            load_residual(B - 1, 0)
            load_residual(B - 1, 1)
            store_x0(B - 1)
            load_side(0, 1, 1, B * NJ)
            for j in (2, 3):
                sp.wait_ge(x_used[j - 2], 2 * B)
                sp.dma_start(x_sb[:, j - 2, :], side_t[0][:, j * T:(j + 1) * T]).then_inc(x_in[j - 2], DMA)
            sp.wait_ge(S["dn_pad"], 1)
            for off in range(4):
                load_gu(Expert(0, off), first=True)
                load_dn(Expert(0, off), first=True)
            load_side(1, 0, 0, B * NJ + 1)
            store_rows(B - 1, 0)
            load_residual(B - 1, 2)
            store_rows(B - 1, 1)
            load_residual(B - 1, 3)
            load_gu(Expert(0, 4))
            store_rows(B - 1, 2)
            store_rows(B - 1, 3)
            load_gu(Expert(0, 5))
            load_dn(Expert(0, 4))
            load_dn(Expert(0, 5))
            for off in (6, 7):
                load_gu(Expert(0, off))
                load_dn(Expert(0, off))
            with sp.Fori(2, E // 4) as i:
                for off in range(4):
                    load_gu(Expert(i, off))
                    load_dn(Expert(i, off))

            def load_tiles(c, g, unit=None):
                if unit is not None:
                    load_side(unit[0], unit[1], 0, (B + c + 1) * NJ + g + 1)
                for r in range(4):
                    if c == 0 and isinstance(g, int) and g == 0:
                        sp.wait_ge(S["dn_lo_ready"], E - 3 + r)
                    else:
                        sp.wait_ge(w_dn_lo[r], c * 4 + g)
                    sp.dma_start(dn_raw[:, r, :], ffn_w[g * 4 + r]).then_inc(w_in[r], DMA)

            def load_sums(c):
                sp.wait_ge(S["gu_lo_ready"], E)
                sp.wait_ge(S["added"], E * DMA)
                sp.wait_ge(S["xa_t_done"], c * NJ)
                for half in range(2):
                    sp.dma_start(xa[:, half * CH // 2:(half + 1) * CH // 2].rearrange("p (t c) -> p t c", c=C),
                                 acc[(2 * c + half) * T // 2:(2 * c + half + 1) * T // 2, :].rearrange(
                                     "(t p) c -> p t c", p=P)).then_inc(xa_in[half], DMA)

            def store_out(c):
                sp.wait_ge(S["out_ready"], c * NJ + NJ)
                sp.dma_start(out[c], x1t[c % 2]).then_inc(S["out_sent"], DMA)

            for c in range(B):
                load_tiles(c, 0, (c + 1, 1) if 0 < c < B - 1 else None)
                if c == 0:
                    load_sums(0)
                    load_side(1, 1, 0, (B + 1) * NJ + 1)
                else:
                    store_out(c - 1)
                if c < B - 1:
                    load_sums(c + 1)
                with sp.Fori(1, NF // 4 - 1) as g:
                    load_tiles(c, g, (c + 1, g + 1) if c < B - 1 else None)
                load_tiles(c, NF // 4 - 1, (c + 2, 0) if c < B - 2 else None)
            store_out(B - 1)
            for tt in range(TT):
                sp.wait_ge(y_sent[tt], B * DMA)
            sp.wait_ge(S["xrow_sent"], B * DMA)
            sp.wait_ge(S["out_sent"], B * DMA)

        @block.gpsimd
        def _(pool):
            pool.memset(dn_raw[96:P, :, 2 * C:3 * C], 0.0).then_inc(S["dn_pad"], 1)
            pool.dma_start(acc[NT:NT + CAP, :], x_rows[0:CAP, :]).then_inc(S["dummy_in"], DMA)

            def products(unit, v):
                pool.wait_ge(S["e_ready"], unit + 1)
                pool.wait_ge(S["scans_done"], unit)
                pool.tensor_tensor(ekv[:, :], ek[:, :], v, ALU.mult).then_inc(S["ekv_ready"], 1)
                pool.wait_ge(S["wkv_ready"], unit)
                pool.tensor_tensor(dv[:, :], eu[:, :], v, ALU.mult).then_inc(S["dv_ready"], 1)

            def sums(unit):
                pool.wait_ge(S["den_scanned"], unit + 1)
                pool.tensor_tensor(den[:, :], den[:, :], den_b[:, :], ALU.add).then_inc(S["den_added"], 1)
                pool.wait_ge(S["scans_done"], unit + 1)
                pool.tensor_tensor(num[:, :], num[:, :], num_b[:, :], ALU.add).then_inc(S["num_added"], 1)
                pool.wait_ge(S["dv_ready"], unit + 1)
                pool.wait_ge(S["num_added"], unit + 1)
                pool.tensor_tensor(num[:, :], num[:, :], dv[:, :], ALU.add).then_inc(S["numer_ready"], 1)

            def numerator(unit, v):
                products(unit, v)
                sums(unit)

            pool.wait_ge(S["dn_pad"], 1)
            with pool.Fori(0, B) as b:
                for j in range(NJ):
                    numerator(b * NJ + j, side_sb[:, j % 2, :])
            numerator(B * NJ, side_sb[:, 0, :])

            def gather(e, first=False):
                q, s = e.pair, (e.off // 2) % 2
                use = e.fours
                pool.wait_ge(S["idx_ready"], 1)
                if not first:
                    pool.wait_ge(S["xt_done"], q - 1)
                    pool.wait_ge(S["wslot_ready"], q - 1)
                    pool.wait_ge(xg_in[s], use * DMA)
                pool.tensor_copy(gidx_now[:, s:s + 1], cut(gidx, q, 1)).then_inc(S["gcol_first"] if first else S["gcol_ready"], 1)
                pool.wait_ge(S["xrow_sent"], B * DMA)
                pool.wait_ge(S["gcol_first"] if first else S["gcol_ready"], q + 1 if first else q - 1)
                pool.indirect_dma_start(xg[:, s, :], None, x0_rows,
                                        bass.IndirectOffsetOnAxis(ap=gidx_now[:, s:s + 1], axis=0)).then_inc(xg_in[s], DMA)

            def scatter(e, first=False):
                s = e.slot2
                pool.wait_ge(S["idx_ready"], 1)
                pool.wait_ge(S["y_ready"], e.n + 1)
                if not first:
                    pool.wait_ge(S["added"], e.n * DMA)
                pool.tensor_copy(sidx_now[:, s:s + 1], cut(sidx, e.n, 1)).then_inc(S["scol_ready"], 1)
                pool.wait_ge(S["idx_ready"], 1)
                pool.wait_ge(S["scol_ready"], e.n + 1)
                pool.indirect_dma_start(acc, bass.IndirectOffsetOnAxis(ap=sidx_now[:, s:s + 1], axis=0),
                                        y_e[:, s, :], None, compute_op=ALU.add).then_inc(S["added"], DMA)

            gather(Expert(0, 0), first=True)
            gather(Expert(0, 2), first=True)
            for tt in range(TT):
                pool.wait_ge(y_sent[tt], B * DMA)
            pool.wait_ge(S["dummy_in"], DMA)

            def split_lo_dn(e):
                pool.wait_ge(S["dn_hi_ready"], e.n + 1)
                pool.tensor_tensor(dn_lo[:, e.slot2, :], dn_raw[:, e.slot4, :], dn_hi[:, e.slot2, :].bitcast(F32),
                                   ALU.subtract).then_inc(S["dn_lo_ready"], 1)

            def step(e, gathers=True, splits=True, scatters=True):
                if gathers and e.off % 2 == 1:
                    gather(e + 5)
                if splits:
                    split_lo_dn(e)
                if scatters:
                    scatter(e + -2, first=isinstance(e.i, int) and e.n == 2)

            pool.wait_ge(S["sh_d_done"], B * TT)
            gather(Expert(0, 4))
            for off in range(4):
                step(Expert(0, off), scatters=off >= 2)
            for n, (lo, hi) in enumerate(parts):
                with pool.Fori(lo, hi if n < 3 else hi - 1) as i:
                    for off in range(4):
                        step(Expert(i, off))
                if n < 3:
                    for off in range(4):
                        step(Expert(0, 4 * hi + off))
                        if off == 0:
                            products(B * NJ + 1 + n, late_units[n][2])
                        elif off == 1:
                            sums(B * NJ + 1 + n)
            for off in range(8):
                step(Expert(0, E - 8 + off), gathers=off == 1, splits=off < 4)
            for off in range(2):
                step(Expert(0, E + off), gathers=False, splits=False)
            numerator((B + 1) * NJ, late_units[3][2])

            with pool.Fori(0, (B - 1) * NJ - 1) as n:
                numerator((B + 1) * NJ + 1 + n, side_sb[:, 0, :])
            pool.wait_ge(S["added"], E * DMA)

        @block.scalar
        def _(act):
            act.wait_ge(S["csum_done"], 1)
            act.activation(tf[:, :], tf[:, :], ACT.Sigmoid).then_inc(S["tf_ready"], 1)
            act.wait_ge(S["wu_in"], 2 * DMA)
            act.activation(w_sb[:, :], w_sb[:, :], ACT.Exp).then_inc(S["exp_w_done"], 1)
            act.wait_ge(S["exp_w_done"], 1)
            act.activation(dec0[:, :], w_sb[:, :], ACT.Exp, scale=-1.0).then_inc(S["dec0_ready"], 1)

            def exps(unit):
                act.wait_ge(S["k_ready"], unit + 1)
                act.activation(ek[:, :], ek[:, :], ACT.Exp)
                act.activation(eu[:, :], eu[:, :], ACT.Exp).then_inc(S["e_ready"], 1)

            def gate_r(b, j):
                unit = b * NJ + j
                act.wait_ge(x_in[j % 2], (b * 2 + j // 2 + 1) * DMA)
                act.wait_ge(S["wkv_ready"], unit)
                act.activation(one_en[:, :], x_sb[:, j % 2, :], ACT.Exp, scale=-1.0).then_inc(x_used[j % 2], 1)
                act.wait_ge(x_used[j % 2], b * 2 + j // 2 + 1)
                act.activation(one_en[:, :], one_en[:, :], ACT.Copy, bias=1.0).then_inc(S["t_ready"], 1)

            def softmax_exp(b):
                act.wait_ge(S["nmax_ready"], b + 1)
                act.wait_ge(S["p_ready"], b)
                for tt in range(TT):
                    ins = act.activation(pexp[:, tt, :], bank[0][:, tt * E:(tt + 1) * E], ACT.Exp,
                                         bias=nmax[:, tt:tt + 1], accum_out=psums[:, tt:tt + 1])
                ins.then_inc(S["pexp_ready"], 1)

            def copy_rows(b):
                act.wait_ge(S["xrow_sent"], b * DMA)
                for tt in range(TT):
                    act.wait_ge(S["tok_t_done"], b * TT + tt + 1)
                    act.activation(xrow[:, tt, 0:C], bank[1 + tt % 2][:, :], ACT.Copy).then_inc(xrow_copied[tt], 1)

            def shared_silu(b, m):
                rows = P if m < SM - 1 else SLAST
                act.wait_ge(S["sh_gu_done"], b * SM + m + 1)
                act.wait_ge(sh_h_ready[(m + 1) % 2], b * (SM // 2) + (m + 1) // 2)
                act.activation(silu_sh[0:rows, :], gate_bank[m % 2][0:rows, :], ACT.Silu).then_inc(S["sh_silu_ready"], 1)

            def copy_keys(b):
                act.wait_ge(S["mask_t_done"], b + 1)
                act.wait_ge(S["best_ready"], b + 1)
                act.activation(keys[:, CAP:CAP + T], bank[2][0:E, :], ACT.Copy).then_inc(S["keys_ready"], 1)

            def hand_on_x0(b, j, first):
                act.wait_ge(S["wkv_ready"], b * NJ + j + 1)
                if not first:
                    act.wait_ge(S["sh_gu_done"], b * SM)
                act.activation(x0[:, j * T:(j + 1) * T], wkv_out[:, j * T:(j + 1) * T], ACT.Copy).then_inc(S["x0_ready"], 1)

            def early_step(s, shared):
                exps(s * NJ)
                gate_r(s, 0)
                if shared:
                    softmax_exp(s - 1)
                    copy_rows(s - 1)
                for j in range(NJ):
                    if shared and j < SM // 2:
                        shared_silu(s - 1, 2 * j)
                    if j < NJ - 1:
                        exps(s * NJ + j + 1)
                    if shared and j < SM // 2:
                        shared_silu(s - 1, 2 * j + 1)
                    if shared and j == 0:
                        copy_keys(s - 1)
                    if j < NJ - 1:
                        gate_r(s, j + 1)
                    if not shared:
                        hand_on_x0(s, j, True)
                if shared:
                    for j in range(NJ):
                        hand_on_x0(s, j, False)

            early_step(0, False)
            with act.Fori(1, B) as s:
                early_step(s, True)
            exps(B * NJ)
            softmax_exp(B - 1)
            copy_rows(B - 1)
            shared_silu(B - 1, 0)
            shared_silu(B - 1, 1)
            copy_keys(B - 1)
            for m in range(2, SM):
                shared_silu(B - 1, m)

            def split_hi_gu(e):
                act.wait_ge(gu_in[e.slot4], (e.fours + 1) * DMA)
                act.activation(gu_slot(gu_hi, e.slot2), gu_slot(gu_raw, e.slot4), ACT.Copy).then_inc(S["gu_hi_ready"], 1)

            def split_hi_dn(e, first):
                act.wait_ge(dn_in[e.slot4], (e.fours + 1) * 2 * DMA)
                if not first:
                    act.wait_ge(S["d_done"], e.n - 1)
                act.activation(dn_hi[:, e.slot2, :], dn_raw[:, e.slot4, :], ACT.Copy).then_inc(S["dn_hi_ready"], 1)

            def tokens_hi(e):
                s = e.slot4
                act.wait_ge(S["xt_done"], e.pair + 1)
                act.activation(xs_hi[:, s:s + 2, :, :].rearrange("p s j t -> p j s t"),
                               bank[1][:, :].rearrange("p (j s t) -> p j s t", j=NJ, s=2), ACT.Copy).then_inc(S["xs_hi_ready"], 1)

            def step(e, silu=True, hs=True, xs=True, gu=True, dn=True, y=True, first=False):
                if silu:
                    act.wait_ge(S["gu_done"], e.n + 1)
                    if not first:
                        act.wait_ge(S["h_ready"], e.n - 1)
                    act.activation(silu_e[:, e.slot2, :], gate_bank[e.slot2][0:CAP, 0:I], ACT.Silu).then_inc(S["e_silu_ready"], 1)
                if hs:
                    d = e + -1
                    act.wait_ge(S["ht_done"], d.n + 1)
                    if not (isinstance(e.i, int) and d.off < 2):
                        act.wait_ge(S["d_done"], d.n - 1)
                    act.activation(hs_hi[:, d.slot2, :], bank[2][:, 0:len(KT) * CAP], ACT.Copy).then_inc(S["hs_hi_ready"], 1)
                if xs and e.off % 2 == 0:
                    tokens_hi(e + 2)
                if gu:
                    split_hi_gu(e + 2)
                if dn:
                    split_hi_dn(e, first)
                if y:
                    d = e + -2
                    act.wait_ge(S["d_done"], d.n + 1)
                    if not (isinstance(e.i, int) and d.off < 2):
                        act.wait_ge(S["added"], (d.n - 1) * DMA)
                    act.activation(y_e[:, d.slot2, :], row_bank[d.slot2][0:CAP, :], ACT.Copy).then_inc(S["y_ready"], 1)

            act.wait_ge(S["sh_gu_done"], B * SM)
            for s in range(2):
                act.wait_ge(sh_h_ready[s], B * (SM // 2))
            act.wait_ge(S["xrow_sent"], B * DMA)
            act.wait_ge(S["idx_ready"], 1)
            split_hi_gu(Expert(0, 0))
            tokens_hi(Expert(0, 0))
            split_hi_gu(Expert(0, 1))
            act.wait_ge(S["sh_d_done"], B * TT)
            for tt in range(TT):
                act.wait_ge(y_sent[tt], B * DMA)
            for off in range(4):
                step(Expert(0, off), hs=off >= 1, y=off >= 2, first=off < 2)
            for n, (lo, hi) in enumerate(parts):
                with act.Fori(lo, hi) as i:
                    for off in range(4):
                        step(Expert(i, off))
                if n < 3:
                    for off in range(4):
                        step(Expert(0, 4 * hi + off))
                        if off == 0:
                            exps(B * NJ + 1 + n)
            exps((B + 1) * NJ)
            for off in range(4):
                step(Expert(0, E - 4 + off), xs=off < 2, gu=off < 2)
            step(Expert(0, E), silu=False, xs=False, gu=False, dn=False)
            step(Expert(0, E + 1), silu=False, hs=False, xs=False, gu=False, dn=False)

            def f_split_hi_gu(c, n):
                g, r = n
                act.wait_ge(w_in[r], (c * 4 + g + 1) * DMA)
                act.wait_ge(f_gu_done[r % 2], c * 8 + g * 2 + r // 2)
                act.activation(dn_hi[:, r % 2, 0:FGU], dn_raw[:, r, 0:FGU], ACT.Copy).then_inc(S["w_gu_hi_ready"], 1)

            def turned_sigmoid(c, j):
                act.wait_ge(S["xa_t_done"], c * NJ + j + 1)
                act.wait_ge(S["x1_lo_ready"], c * NJ)
                act.activation(sig[:, j * T:(j + 1) * T], turn_bank[j][:, :], ACT.Sigmoid).then_inc(S["sig_ready"], 1)

            def turned_copy(c, j):
                if c >= 2:
                    act.wait_ge(S["out_sent"], (c - 1) * DMA)
                act.activation(x1t[c % 2][:, j * T:(j + 1) * T], turn_bank[j][:, :],
                               ACT.Copy).then_inc(S["x1t_ready"], 1)

            def x1_high(c, j):
                act.wait_ge(S["x1_ready"], c * NJ + j + 1)
                if c >= 2:
                    act.wait_ge(f_gu_done[1], (c - 1) * 8)
                act.activation(x1_hi[c % 2][:, j * T:(j + 1) * T], sig[:, j * T:(j + 1) * T], ACT.Copy).then_inc(S["x1_hi_ready"], 1)

            def f_step(c, g, r, nxt, turn=None):
                half = c * 8 + g * 2 + r // 2
                if nxt is not None:
                    f_split_hi_gu(*nxt)
                act.wait_ge(f_d_done[r % 2], half)
                act.activation(dn_hi[:, r % 2, FGU:], dn_raw[:, r, FGU:], ACT.Copy).then_inc(S["w_dn_hi_ready"], 1)
                act.wait_ge(f_gu_done[r % 2], half + 1)
                act.wait_ge(f_h[r % 2], half)
                act.activation(fsilu[r % 2], gate_bank[r % 2][:, :], ACT.Silu).then_inc(f_silu[r % 2], 1)
                if turn is not None:
                    for j in (2 * r, 2 * r + 1):
                        turned_sigmoid(turn, j)
                        turned_copy(turn, j)
                act.wait_ge(f_h[r % 2], half + 1)
                act.activation(fh_hi[r % 2], fh[r % 2], ACT.Copy).then_inc(f_hi[r % 2], 1)

            def f_group(c, g, wkv):
                for r in range(4):
                    f_step(c, g, r, (c, (g, r + 1)) if r < 3 else (c, (g + 1, 0)))
                    if wkv and r == 0:
                        exps((B + 1 + c) * NJ + g + 1)

            def f_last_group(c, wkv, prepare):
                g = NF // 4 - 1
                for r in range(4):
                    nxt = (c, (g, r + 1)) if r < 3 else ((c + 1, (0, 0)) if prepare else None)
                    if prepare and r >= 2:
                        x1_high(c + 1, 2 * (r - 2))
                        x1_high(c + 1, 2 * (r - 2) + 1)
                    f_step(c, g, r, nxt, c + 1 if prepare and r < 2 else None)
                    if wkv and r == 0:
                        exps((B + 1 + c) * NJ + g + 1)

            act.wait_ge(S["d_done"], E)
            act.wait_ge(S["gu_done"], E)
            act.wait_ge(S["gu_lo_ready"], E)
            act.wait_ge(S["dn_lo_ready"], E)
            f_split_hi_gu(0, (0, 0))
            for j in range(NJ):
                turned_sigmoid(0, j)
            for j in (2, 3):
                turned_copy(0, j)
            for j in range(NJ):
                x1_high(0, j)
            for j in (0, 1):
                turned_copy(0, j)
            for c in range(B):
                f_group(c, 0, c < B - 1)
                with act.Fori(1, NF // 4 - 1) as g:
                    f_group(c, g, c < B - 1)
                f_last_group(c, c < B - 2, c < B - 1)

        @block.vector
        def _(vec):
            V = nc.vector

            class Chain:

                def __init__(self, sem):
                    self.sem, self.base, self.n = sem, 0, 0

                def __call__(self, ins):
                    ins.then_inc(self.sem, 1)
                    self.n += 1

                def wait(self):
                    vec.wait_ge(self.sem, self.base + self.n)

            vec.wait_ge(S["cond_in"], DMA)
            V.tensor_reduce(tf[:, :], cond_sb[:, :, :], AX_X, ALU.add).then_inc(S["csum_done"], 1)
            vec.wait_ge(S["tf_ready"], 1)
            V.tensor_scalar(half_tf[:, :], tf[:, :], 0.5, 0.5, ALU.mult, ALU.add).then_inc(S["fac_ready"], 1)
            V.tensor_scalar(out_scale[:, :], tf[:, :], 0.2, 0.8, ALU.mult, ALU.add).then_inc(S["fac_ready"], 1)
            def decays():
                vec.wait_ge(S["dec0_ready"], 1)
                vec.wait_ge(S["fac_ready"], 2)
                for layer in range(2):
                    for b in range(B):
                        V.tensor_scalar(decay[:, (layer * B + b) * NJ:(layer * B + b + 1) * NJ],
                                        dec0[:, layer * NJ:(layer + 1) * NJ], half_tf[:, b:b + 1], None,
                                        ALU.mult).then_inc(S["fac_ready"], 1)
                vec.wait_ge(S["fac_ready"], 2 + 2 * B)

            wkv = Chain(S["wkv_chain"])
            WKV_OPS = 4
            for t in (den_b, num_b):
                V.memset(t[:, T - 1:T], 0.0).then_inc(S["edges_zero"], 1)

            def wkv_clamp(layer, b, j, v, arrived, use):
                wkv.wait()
                vec.wait_ge(S["dv_ready"], (layer * B + b) * NJ + j)
                vec.wait_ge(arrived, (use + 1) * DMA)
                wkv(V.tensor_scalar(ek[:, :], v, EXP_CAP, None, ALU.min))
                V.tensor_scalar(eu[:, :], v, cut(u_sb, j + layer * NJ, 1), EXP_CAP,
                                ALU.add, ALU.min).then_inc(S["k_ready"], 1)

            def wkv_scans(layer, b, j):
                dec = cut(decay, (layer * B + b) * NJ + j, 1).to_broadcast([P, T])
                vec.wait_ge(S["e_ready"], (layer * B + b) * NJ + j + 1)
                vec.wait_ge(S["wkv_ready"], (layer * B + b) * NJ + j)
                V.tensor_tensor_scan(den[:, :], dec, ek[:, :], 0.0, ALU.mult, ALU.add)
                V.tensor_tensor_scan(den_b[:, T - 2::-1], ek[:, T - 1:0:-1], dec[:, 0:T - 1], 0.0, ALU.add,
                                     ALU.mult).then_inc(S["den_scanned"], 1)
                vec.wait_ge(S["ekv_ready"], (layer * B + b) * NJ + j + 1)
                V.tensor_tensor_scan(num[:, :], dec, ekv[:, :], 0.0, ALU.mult, ALU.add)
                V.tensor_tensor_scan(num_b[:, T - 2::-1], ekv[:, T - 1:0:-1], dec[:, 0:T - 1], 0.0, ALU.add,
                                     ALU.mult).then_inc(S["scans_done"], 1)

            def wkv_total(layer, b, j):
                vec.wait_ge(S["den_added"], (layer * B + b) * NJ + j + 1)
                wkv(V.tensor_tensor(den[:, :], den[:, :], eu[:, :], ALU.add))

            def wkv_recip(layer, b, j):
                unit = (layer * B + b) * NJ + j
                wkv.wait()
                if layer == 0:
                    vec.wait_ge(S["t_ready"], unit + 1)
                    wkv(V.scalar_tensor_tensor(out=den[:, :], in0=den[:, :], scalar=DEN_FLOOR, in1=one_en[:, :],
                                               op0=ALU.max, op1=ALU.mult))
                else:
                    wkv(V.tensor_scalar(den[:, :], den[:, :], DEN_FLOOR, None, ALU.max))
                wkv.wait()
                wkv(V.reciprocal(den[:, :], den[:, :]))

            def wkv_scale(layer, b, j):
                wkv.wait()
                vec.wait_ge(S["numer_ready"], (layer * B + b) * NJ + j + 1)
                V.scalar_tensor_tensor(out=cut(wkv_out, j * T, T), in0=num[:, :], scalar=cut(out_scale, b, 1),
                                       in1=den[:, :], op0=ALU.mult, op1=ALU.mult).then_inc(S["wkv_ready"], 1)

            def wkv_ratio(layer, b, j):
                wkv_recip(layer, b, j)
                wkv_scale(layer, b, j)

            def route(b):
                vec.wait_ge(S["logits_done"], b + 1)
                V.tensor_reduce(nmax[:, :], bank[0][:, 0:TT * E].rearrange("p (t e) -> p t e", e=E), AX_X,
                                ALU.max).then_inc(S["nmax_done"], 1)
                vec.wait_ge(S["nmax_done"], b + 1)
                V.tensor_scalar(nmax[:, :], nmax[:, :], -1.0, None, ALU.mult).then_inc(S["nmax_ready"], 1)
                vec.wait_ge(S["pexp_ready"], b + 1)
                chain = S["route_chain"]
                OPS = 5
                V.reciprocal(prec[:, :], psums[:, :]).then_inc(chain, 1)
                vec.wait_ge(S["xrow_sent"], b * DMA)
                vec.wait_ge(chain, b * OPS + 1)
                for tt in range(TT):
                    ins = V.tensor_scalar(xrow[:, tt, C:XR], pexp[:, tt, :], prec[:, tt:tt + 1], None, ALU.mult)
                ins.then_inc(S["p_ready"], 1)
                vec.wait_ge(S["dec0_ready"], 1)
                vec.wait_ge(S["p_ready"], b + 1)
                for tt in range(TT):
                    ins = V.max(top8[:, tt, :], xrow[:, tt, C:XR])
                ins.then_inc(S["top8_ready"], 1)
                vec.wait_ge(S["dec0_ready"], 1)
                vec.wait_ge(S["top8_ready"], b + 1)
                for tt in range(TT):
                    ins = V.max_index(top8_i[:, tt, :], top8[:, tt, :], xrow[:, tt, C:XR])
                ins.then_inc(chain, 1)
                vec.wait_ge(chain, b * OPS + 2)
                V.tensor_copy(top8_f[:, :, :], top8_i[:, :, :]).then_inc(chain, 1)
                vec.wait_ge(chain, b * OPS + 3)
                V.tensor_tensor(onehot[:, :, :, :],
                                iota_e[:, :].rearrange("p (a b e) -> p a b e", a=1, b=1).to_broadcast([P, TT, TOPK, E]),
                                top8_f[:, :, 0:TOPK].rearrange("p t (k o) -> p t k o", o=1).to_broadcast([P, TT, TOPK, E]),
                                ALU.is_equal).then_inc(chain, 1)
                vec.wait_ge(chain, b * OPS + 4)
                vec.wait_ge(S["mask_t_done"], b)
                V.tensor_reduce(mkey[:, :, :], onehot[:, :, :, :].rearrange("p t k e -> p t e k"), AX_X,
                                ALU.add).then_inc(chain, 1)
                vec.wait_ge(chain, b * OPS + 5)
                for tt in range(TT):
                    ins = V.tensor_scalar(mkey[:, tt, :], mkey[:, tt, :], cut(key_col, b * TT + tt, 1), None, ALU.mult)
                ins.then_inc(S["mask_ready"], 1)

            def shared_h(b, m):
                rows = P if m < SM - 1 else SLAST
                up = up_bank[m % 2][:, :] if m < SM - 1 else gate_bank[m % 2][SLAST:2 * SLAST, :]
                vec.wait_ge(S["sh_silu_ready"], b * SM + m + 1)
                V.tensor_tensor(h_sh[0:rows, m, :], silu_sh[0:rows, :], up, ALU.mult).then_inc(sh_h_ready[m % 2], 1)

            def shared_y(b, tt):
                s = tt % 2
                vec.wait_ge(S["sh_d_done"], b * TT + tt + 1)
                vec.wait_ge(xres_in[s], (b * 2 + tt // 2 + 1) * DMA)
                vec.wait_ge(y_sent[(tt + 2) % 4], (b + tt // 2) * DMA)
                V.tensor_tensor(y_sh[:, s, :], sh_bank[tt][:, :], xres[:, s, :], ALU.add).then_inc(sh_y_ready[tt], 1)

            def slot_rounds(b, first, last):
                for r in range(first, last):
                    got = slot_key[:, 8 * r:8 * r + 8]
                    vec.wait_ge(S["dec0_ready"], 1)
                    vec.wait_ge(S["keys_ready"], b + 1)
                    if r:
                        vec.wait_ge(round_cut[r - 1], b + 1)
                    else:
                        vec.wait_ge(S["best_ready"], b + 1)
                    V.max(got, keys[:, :]).then_inc(round_max[r], 1)
                    if r < CAP // 8 - 1:
                        vec.wait_ge(S["dec0_ready"], 1)
                        vec.wait_ge(round_max[r], b + 1)
                        V.match_replace(keys[:, :], got, keys[:, :], 0.0).then_inc(round_cut[r], 1)

            def keep_best(b):
                vec.wait_ge(round_max[CAP // 8 - 1], b + 1)
                V.tensor_copy(keys[:, 0:CAP], slot_key[:, :]).then_inc(S["best_ready"], 1)

            def early_step(s, shared):
                wkv.base, wkv.n = s * (NJ * WKV_OPS), 0
                wkv_clamp(0, s, 0, side_sb[:, 0, :], side_in[0], s * 2)
                if not shared:
                    decays()
                wkv_scans(0, s, 0)
                if shared:
                    route(s - 1)
                for j in range(NJ):
                    if j:
                        wkv_scans(0, s, j)
                    if shared and j < SM // 2:
                        slot_rounds(s - 1, *((0, 0), (0, 3), (3, 4))[j])
                        shared_h(s - 1, 2 * j)
                    wkv_total(0, s, j)
                    if j < NJ - 1:
                        wkv_clamp(0, s, j + 1, side_sb[:, (j + 1) % 2, :], side_in[(j + 1) % 2], s * 2 + (j + 1) // 2)
                    if shared and j == 2:
                        slot_rounds(s - 1, 4, 5)
                        shared_h(s - 1, 5)
                    wkv_ratio(0, s, j)
                    if shared and j in (0, 1):
                        shared_h(s - 1, 2 * j + 1)
                if shared:
                    shared_y(s - 1, 0)
                    shared_y(s - 1, 1)
                    slot_rounds(s - 1, 5, 8)
                    keep_best(s - 1)
                    shared_y(s - 1, 2)
                    shared_y(s - 1, 3)
                assert wkv.n == NJ * WKV_OPS

            def tokens_low(e):
                s, q = e.slot4, e.pair
                vec.wait_ge(S["xs_hi_ready"], q + 1)
                hi = xs_hi[:, s:s + 2, :, :].bitcast(F32).rearrange("p s j t -> p j s t")
                V.tensor_tensor(xs_lo[:, s:s + 2, :, :].rearrange("p s j t -> p j s t"),
                                bank[1][:, :].rearrange("p (j s t) -> p j s t", j=NJ, s=2), hi,
                                ALU.subtract).then_inc(S["xs_lo_ready"], 1)

            def split_lo_gu(e):
                vec.wait_ge(S["gu_hi_ready"], e.n + 1)
                V.tensor_tensor(gu_slot(gu_lo, e.slot2), gu_slot(gu_raw, e.slot4), gu_slot(gu_hi, e.slot2).bitcast(F32),
                                ALU.subtract).then_inc(S["gu_lo_ready"], 1)

            vec.wait_ge(S["wu_in"], 2 * DMA)
            vec.wait_ge(S["edges_zero"], 2)
            V.memset(keys[:, 0:CAP], 0.0).then_inc(S["best_ready"], 1)
            early_step(0, False)
            vec.wait_ge(S["const_in"], N_CONST * DMA)
            with vec.Fori(1, B) as s:
                early_step(s, True)

            wkv.base, wkv.n = B * NJ * WKV_OPS, 0
            wkv_clamp(1, 0, 0, side_sb[:, 0, :], side_in[0], 2 * B)
            wkv_scans(1, 0, 0)
            route(B - 1)
            wkv_total(1, 0, 0)
            wkv_ratio(1, 0, 0)
            shared_h(B - 1, 0)
            shared_h(B - 1, 1)
            slot_rounds(B - 1, 0, 8)
            vec.wait_ge(round_max[CAP // 8 - 1], B)
            vec.engine_nop().then_inc(S["slots_ready"], 1)
            shared_h(B - 1, 2)
            vec.wait_ge(S["slots_t_done"], 1)
            V.tensor_scalar(tok_f[:, :], bank[1][0:CAP, 0:E], -1.0, float(NT), ALU.mult, ALU.add).then_inc(S["idx_chain"], 1)
            vec.wait_ge(S["idx_chain"], 1)
            V.tensor_scalar(empty_f[:, :], tok_f[:, :], float(NT), None, ALU.is_equal).then_inc(S["idx_chain"], 1)
            halves = tok_f[:, :].rearrange("p (q o) -> p q o", o=2)
            V.tensor_scalar(gidx[0:CAP, :], halves[:, :, 0], float(NT - 1), None, ALU.min).then_inc(S["idx_chain"], 1)
            V.tensor_scalar(gidx[CAP:P, :], halves[:, :, 1], float(NT - 1), None, ALU.min).then_inc(S["idx_chain"], 1)
            vec.wait_ge(S["idx_chain"], 4)
            V.scalar_tensor_tensor(out=sidx[:, :], in0=empty_f[:, :], scalar=scol[:, 0:1], in1=tok_f[:, :],
                                   op0=ALU.mult, op1=ALU.add).then_inc(S["idx_ready"], 1)

            for m in range(3, SM):
                shared_h(B - 1, m)
            shared_y(B - 1, 0)
            split_lo_gu(Expert(0, 0))
            split_lo_gu(Expert(0, 1))
            tokens_low(Expert(0, 0))
            for tt in range(1, TT):
                shared_y(B - 1, tt)

            def last_lo_dn(e):
                vec.wait_ge(S["dn_lo_ready"], e.n)
                vec.wait_ge(S["dn_hi_ready"], e.n + 1)
                V.tensor_tensor(dn_lo[:, e.slot2, :], dn_raw[:, e.slot4, :], dn_hi[:, e.slot2, :].bitcast(F32),
                                ALU.subtract).then_inc(S["dn_lo_ready"], 1)

            def slot_weights(e):
                q = e.pair
                half = (e.off // 2) % 2
                vec.wait_ge(xg_in[half], (e.fours + 1) * DMA)
                V.scalar_tensor_tensor(out=wsel[:, :], in0=iota_e[:, :], scalar=cut(pair_e, q, 1),
                                       in1=xg[:, half, C:XR], op0=ALU.is_equal, op1=ALU.mult,
                                       accum_out=w_pair[:, half:half + 1]).then_inc(S["wsel_done"], 1)
                vec.wait_ge(S["wsel_done"], q + 1)
                V.tensor_copy(w_odd[:, half:half + 1], w_pair[CAP:P, half:half + 1]).then_inc(S["wslot_ready"], 1)
            def step(e, h=True, hs=True, xs=True, gu=True):
                half = (e.off // 2) % 2
                if h:
                    w = w_pair[0:CAP, half:half + 1] if e.slot2 == 0 else w_odd[:, half:half + 1]
                    vec.wait_ge(S["wslot_ready"], e.pair + 1)
                    vec.wait_ge(S["e_silu_ready"], e.n + 1)
                    if not (isinstance(e.i, int) and e.off < 2):
                        vec.wait_ge(S["ht_done"], e.n - 1)
                    V.scalar_tensor_tensor(out=h_e[:, e.slot2, :], in0=silu_e[:, e.slot2, :], scalar=w,
                                           in1=up_bank[e.slot2][0:CAP, 0:I], op0=ALU.mult, op1=ALU.mult).then_inc(S["h_ready"], 1)
                if hs:
                    d = e + -1
                    vec.wait_ge(S["hs_hi_ready"], d.n + 1)
                    V.tensor_tensor(hs_lo[:, d.slot2, :], bank[2][:, 0:len(KT) * CAP], hs_hi[:, d.slot2, :].bitcast(F32),
                                    ALU.subtract).then_inc(S["hs_lo_ready"], 1)
                if xs and e.off % 2 == 0:
                    slot_weights(e + 2)
                    tokens_low(e + 2)
                if gu:
                    split_lo_gu(e + 2)

            vec.wait_ge(S["sh_d_done"], B * TT)
            for tt in range(TT):
                vec.wait_ge(y_sent[tt], B * DMA)
            V.memset(bank[2][96:P, 2 * CAP:3 * CAP], 0.0).then_inc(S["bank_pad"], 1)
            slot_weights(Expert(0, 0))
            for off in range(4):
                step(Expert(0, off), hs=off >= 1)
            for n, (lo, hi) in enumerate(parts):
                with vec.Fori(lo, hi) as i:
                    for off in range(4):
                        step(Expert(i, off))
                b, j, v, arrived, use = late_units[n]
                wkv.base, wkv.n = (B * NJ + 1 + n) * WKV_OPS, 0
                if n == 3:
                    wkv_clamp(1, b, j, v, arrived, use)
                else:
                    for off in range(4):
                        step(Expert(0, 4 * hi + off))
                        if off == 0:
                            wkv_clamp(1, b, j, v, arrived, use)
                        elif off == 1:
                            wkv_scans(1, b, j)
                        elif off == 2:
                            wkv_total(1, b, j)
                        else:
                            wkv_ratio(1, b, j)
            for off in range(4):
                step(Expert(0, E - 4 + off), xs=off < 2, gu=off < 2)
                last_lo_dn(Expert(0, E - 4 + off))
            step(Expert(0, E), h=False, xs=False, gu=False)

            def f_split_lo_gu(c, n):
                g, r = n
                vec.wait_ge(S["w_gu_hi_ready"], c * NF + g * 4 + r + 1)
                V.tensor_tensor(dn_lo[:, r % 2, 0:FGU], dn_raw[:, r, 0:FGU], dn_hi[:, r % 2, 0:FGU].bitcast(F32),
                                ALU.subtract).then_inc(w_gu_lo[r], 1)

            def f_step(c, g, r, nxt):
                half = c * 8 + g * 2 + r // 2
                if nxt is not None:
                    f_split_lo_gu(*nxt)
                vec.wait_ge(S["w_dn_hi_ready"], c * NF + g * 4 + r + 1)
                V.tensor_tensor(dn_lo[:, r % 2, FGU:], dn_raw[:, r, FGU:], dn_hi[:, r % 2, FGU:].bitcast(F32),
                                ALU.subtract).then_inc(w_dn_lo[r], 1)
                vec.wait_ge(f_lo[r % 2], half)
                vec.wait_ge(f_silu[r % 2], half + 1)
                V.tensor_tensor(fh[r % 2], fsilu[r % 2], up_bank[r % 2][:, :], ALU.mult).then_inc(f_h[r % 2], 1)
                vec.wait_ge(f_hi[r % 2], half + 1)
                V.tensor_tensor(fh_lo[r % 2], fh[r % 2], fh_hi[r % 2].bitcast(F32), ALU.subtract).then_inc(f_lo[r % 2], 1)

            def x1_part(c, j):
                vec.wait_ge(S["sig_ready"], c * NJ + j + 1)
                V.tensor_tensor(sig[:, j * T:(j + 1) * T], sig[:, j * T:(j + 1) * T],
                                wkv_out[:, j * T:(j + 1) * T], ALU.mult).then_inc(S["x1_ready"], 1)

            def x1_low(c, j):
                vec.wait_ge(S["x1_hi_ready"], c * NJ + j + 1)
                V.tensor_tensor(x1_lo[c % 2][:, j * T:(j + 1) * T], sig[:, j * T:(j + 1) * T],
                                x1_hi[c % 2][:, j * T:(j + 1) * T].bitcast(F32), ALU.subtract).then_inc(S["x1_lo_ready"], 1)
            def f_out(c):
                vec.wait_ge(S["x1t_ready"], (c + 1) * NJ)
                vec.wait_ge(f_d_done[1], c * 8 + 8)
                vec.wait_ge(f_d_done[0], c * 8 + 8)
                for j in range(NJ):
                    V.tensor_tensor(x1t[c % 2][:, j * T:(j + 1) * T], bank[j][:, :], x1t[c % 2][:, j * T:(j + 1) * T],
                                    ALU.add).then_inc(S["out_ready"], 1)

            def f_group(c, g, unit, out=False, prepare=False, nxt_chunk=True):
                wkv.base, wkv.n = ((B + c + 1) * NJ + g + 1) * WKV_OPS, 0
                for r in range(4):
                    nxt = (c, (g, r + 1)) if r < 3 else ((c, (g + 1, 0)) if nxt_chunk else None)
                    f_step(c, g, r, nxt)
                    if out and r == 0:
                        f_out(c - 1)
                    if prepare and r in (1, 2):
                        x1_part(c + 1, 2 * (r - 1))
                        x1_part(c + 1, 2 * (r - 1) + 1)
                    if prepare and r == 2:
                        for j in range(NJ):
                            x1_low(c + 1, j)
                    if unit is not None:
                        if r == 0:
                            wkv_clamp(1, unit[0], unit[1], side_sb[:, 0, :], side_in[0], 2 * B + 2 + c * 4 + g)
                        elif r == 1:
                            wkv_scans(1, unit[0], unit[1])
                        elif r == 2:
                            wkv_total(1, unit[0], unit[1])
                        else:
                            wkv_recip(1, unit[0], unit[1])
                            wkv_scale(1, unit[0], unit[1])

            LAST = NF // 4 - 1
            f_split_lo_gu(0, (0, 0))
            wkv.base, wkv.n = (B + 1) * NJ * WKV_OPS, 1
            wkv_scans(1, 1, 0)
            wkv_total(1, 1, 0)
            wkv_recip(1, 1, 0)
            for j in range(NJ):
                x1_part(0, j)
            for j in range(NJ):
                x1_low(0, j)
            wkv.base, wkv.n = ((B + 1) * NJ + 1) * WKV_OPS, 0
            wkv_scale(1, 1, 0)
            for c in range(B):
                f_group(c, 0, (c + 1, 1) if c < B - 1 else None, out=c > 0)
                with vec.Fori(1, LAST) as g:
                    f_group(c, g, (c + 1, g + 1) if c < B - 1 else None)
                f_group(c, LAST, (c + 2, 0) if c < B - 2 else None, prepare=c < B - 1, nxt_chunk=c < B - 1)
            f_out(B - 1)

        @block.tensor
        def _(pe):
            pe.wait_ge(S["const_in"], N_CONST * DMA)
            pe.wait_ge(S["sgu_in"], DMA)
            pe.wait_ge(S["sdn_in"], 2 * DMA)

            def tokens(e, first=False):
                half = (e.off // 2) % 2
                pe.wait_ge(xg_in[half], (e.fours + 1) * DMA)
                if not first:
                    pe.wait_ge(S["xs_lo_ready"], e.pair)
                for j in range(NJ):
                    mm = pe.transpose(bank[1][:, j * P:(j + 1) * P], xg[:, half, j * P:(j + 1) * P], idt[:, :])
                mm.then_inc(S["xt_done"], 1)

            def turn_slots():
                pe.wait_ge(xrow_copied[TT - 1], B)
                pe.wait_ge(S["slots_ready"], 1)
                pe.transpose(bank[1][0:CAP, 0:E], slot_key[:, :], idt[0:E, 0:E]).then_inc(S["slots_t_done"], 1)

            def turn_rows(b, tt):
                pe.wait_ge(xrow_copied[(tt + 2) % TT], b + tt // 2)
                if tt == 1:
                    pe.wait_ge(S["keys_ready"], b)
                for j in range(NJ):
                    mm = pe.transpose(bank[1 + tt % 2][:, j * P:(j + 1) * P], x0[:, j * T + tt * P:j * T + (tt + 1) * P], idt[:, :])
                mm.then_inc(S["tok_t_done"], 1)

            def batch(b, last=False):
                pe.wait_ge(S["x0_ready"], (b + 1) * NJ)
                pe.wait_ge(S["pexp_ready"], b)
                for tt in range(TT):
                    for j in range(NJ):
                        mm = pe.matmul(bank[0][:, tt * E:(tt + 1) * E], x0[:, j * T + tt * P:j * T + (tt + 1) * P],
                                       gate_sb[:, j * E:(j + 1) * E], start=j == 0, stop=j == NJ - 1)
                mm.then_inc(S["logits_done"], 1)
                turn_rows(b, 0)
                turn_rows(b, 1)
                for m in range(SM):
                    pe.wait_ge(sh_h_ready[m % 2], b * (SM // 2) + m // 2)
                    if m < 2:
                        pe.wait_ge(sh_y_ready[2 * m + 1], b)
                    for side, dst in enumerate((gate_bank[m % 2], up_bank[m % 2])[:2 if m < SM - 1 else 1]):
                        for j in range(NJ):
                            mm = pe.matmul(dst[:, :], sgu[:, j, (2 * m + side) * P:(2 * m + side + 1) * P],
                                           x0[:, j * T:(j + 1) * T], start=j == 0, stop=j == NJ - 1)
                    mm.then_inc(S["sh_gu_done"], 1)
                    if m == 0:
                        turn_rows(b, 2)
                        turn_rows(b, 3)
                    if last and m == 3:
                        turn_slots()
                    if m == 1:
                        pe.wait_ge(S["sgu_in"], DMA)
                        pe.wait_ge(S["mask_ready"], b + 1)
                        pe.wait_ge(xrow_copied[3], b + 1)
                        for tt in range(TT):
                            mm = pe.transpose(bank[2][0:E, tt * P:(tt + 1) * P], mkey[:, tt, :], idt[:, :])
                        mm.then_inc(S["mask_t_done"], 1)
                if last:
                    pe.wait_ge(S["idx_ready"], 1)
                    tokens(Expert(0, 0), first=True)
                pe.wait_ge(sh_h_ready[0], b * (SM // 2) + SM // 2)
                for tt in range(TT):
                    if tt == 0:
                        pe.wait_ge(sh_y_ready[0], b)
                    for k in range(SM):
                        if tt == 0 and k == SM - 1:
                            pe.wait_ge(sh_h_ready[1], b * (SM // 2) + SM // 2)
                        rows = P if k < SM - 1 else SLAST
                        mm = pe.matmul(sh_bank[tt][:, :], h_sh[0:rows, k, tt * P:(tt + 1) * P], sdn[0:rows, k, :],
                                       start=k == 0, stop=k == SM - 1)
                    mm.then_inc(S["sh_d_done"], 1)

            with pe.Fori(0, B - 1) as b:
                batch(b)
            batch(B - 1, last=True)

            def gate_up(e):
                s, s4 = e.slot2, e.slot4
                pe.wait_ge(S["gu_lo_ready"], e.n + 1)
                pe.wait_ge(S["xs_lo_ready"], e.pair + 1)
                if isinstance(e.n, int) and e.n < 2:
                    pe.wait_ge(sh_y_ready[2 * e.n + 1], B)
                else:
                    pe.wait_ge(S["h_ready"], e.n - 1)
                for j in range(NJ):
                    for n, (x, w) in enumerate(((xs_hi, gu_hi), (xs_hi, gu_lo), (xs_lo, gu_hi))):
                        for side, dst in enumerate((gate_bank[s], up_bank[s])):
                            at = s * GUW + (2 * j + side) * I
                            mm = pe.matmul(dst[0:CAP, 0:I], x[:, s4, j, :], w[:, at:at + I],
                                           start=j == 0 and n == 0, stop=j == NJ - 1 and n == 2)
                mm.then_inc(S["gu_done"], 1)

            def turn_h(e):
                pe.wait_ge(S["bank_pad"], 1)
                pe.wait_ge(S["h_ready"], e.n + 1)
                if not (isinstance(e.i, int) and e.off < 1):
                    pe.wait_ge(S["hs_lo_ready"], e.n)
                for k, rows in KT:
                    mm = pe.transpose(bank[2][0:rows, k * CAP:(k + 1) * CAP], h_e[:, e.slot2, k * P:k * P + rows],
                                      idt[0:CAP, 0:CAP])
                mm.then_inc(S["ht_done"], 1)

            def down(e):
                s = e.slot2
                pe.wait_ge(S["hs_lo_ready"], e.n + 1)
                pe.wait_ge(S["dn_lo_ready"], e.n + 1)
                if not (isinstance(e.i, int) and e.off < 2):
                    pe.wait_ge(S["y_ready"], e.n - 1)
                for k, rows in KT:
                    for n, (h, w) in enumerate(((hs_hi, dn_hi), (hs_hi, dn_lo), (hs_lo, dn_hi))):
                        mm = pe.matmul(row_bank[s][0:CAP, :], h[0:rows, s, k * CAP:(k + 1) * CAP],
                                       w[0:rows, s, k * C:(k + 1) * C], start=k == 0 and n == 0,
                                       stop=k == len(KT) - 1 and n == 2)
                mm.then_inc(S["d_done"], 1)

            def step(e, gu=True, th=True, xt=True, dn=True):
                if gu:
                    gate_up(e)
                if th:
                    turn_h(e + -1)
                if xt and e.off % 2 == 0:
                    tokens(e + 2)
                if dn:
                    down(e + -2)

            for off in range(4):
                step(Expert(0, off), th=off >= 1, dn=off >= 2)
            with pe.Fori(1, E // 4 - 1) as i:
                for off in range(4):
                    step(Expert(i, off))
            for off in range(4):
                step(Expert(0, E - 4 + off), xt=off < 2)
            step(Expert(0, E), gu=False, xt=False)
            step(Expert(0, E + 1), gu=False, th=False, xt=False)

            def turn_tokens(c, j, tiles=range(TT)):
                for tt in tiles:
                    mm = pe.transpose(turn_bank[j][:, tt * P:(tt + 1) * P], xa[:, tt * C + j * P:tt * C + (j + 1) * P], idt[:, :])
                if tt == TT - 1:
                    mm.then_inc(S["xa_t_done"], 1)

            def f_gate_up(c, g, r, tokens=False):
                s = r % 2
                pe.wait_ge(w_gu_lo[r], c * 4 + g + 1)
                pe.wait_ge(f_h[s], c * 8 + g * 2 + r // 2)
                for side, dst in enumerate((gate_bank[s], up_bank[s])):
                    for j in range(NJ):
                        if tokens and side == 0:
                            pe.wait_ge(S["x1_lo_ready"], c * NJ + j + 1)
                        at = (2 * j + side) * P
                        for n, (w, x) in enumerate(((dn_hi, x1_hi), (dn_hi, x1_lo), (dn_lo, x1_hi))):
                            mm = pe.matmul(dst[:, :], w[:, s, at:at + P], x[c % 2][:, j * T:(j + 1) * T],
                                           start=j == 0 and n == 0, stop=j == NJ - 1 and n == 2)
                mm.then_inc(f_gu_done[s], 1)

            def f_down(c, g, r, first=False, last=False):
                s = r % 2
                pe.wait_ge(w_dn_lo[r], c * 4 + g + 1)
                pe.wait_ge(f_lo[s], c * 8 + g * 2 + r // 2 + 1)
                if first:
                    pe.wait_ge(S["out_ready"], c * NJ)
                for ct in range(NJ):
                    at = FGU + ct * P
                    for n, (w, h) in enumerate(((dn_hi, fh_hi), (dn_hi, fh_lo), (dn_lo, fh_hi))):
                        mm = pe.matmul(bank[ct][:, :], w[:, s, at:at + P], h[s], start=first and n == 0,
                                       stop=last and n == 2, skip_group_check=True)
                mm.then_inc(f_d_done[s], 1)

            def f_group(c, g, prepare=False):
                first_group = isinstance(g, int) and g == 0
                for r in range(4):
                    if prepare and r in (1, 2):
                        pe.wait_ge(S["x1t_ready"], (c + 1) * NJ + 2 * r)
                    if first_group and c == 0 and r < 2:
                        pe.wait_ge(S["x1t_ready"], 2 * r + 2)
                    f_gate_up(c, g, r, tokens=first_group and r == 0)
                    if prepare and r < 2:
                        for half in range(2):
                            pe.wait_ge(xa_in[half], (c + 2) * DMA)
                        pe.wait_ge(f_h[1 - r], c * 8 + g * 2 + r)
                        turn_tokens(c + 1, 2 * r)
                        turn_tokens(c + 1, 2 * r + 1)
                    if r:
                        f_down(c, g, r - 1, first=first_group and r == 1)
                    elif not first_group:
                        f_down(c, g - 1, 3)
                    elif c:
                        f_down(c - 1, LAST, 3, last=True)

            LAST = NF // 4 - 1
            pe.wait_ge(S["h_ready"], E)
            pe.wait_ge(S["y_ready"], E)
            for half in range(2):
                pe.wait_ge(xa_in[half], DMA)
                for j in range(NJ):
                    turn_tokens(0, j, (2 * half, 2 * half + 1))
            for c in range(B):
                f_group(c, 0)
                with pe.Fori(1, LAST) as g:
                    f_group(c, g)
                f_group(c, LAST, prepare=c < B - 1)
            f_down(B - 1, LAST, 3, last=True)


def channel_major(a, np):
    b, t, c = a.shape
    return np.ascontiguousarray(a.transpose(0, 2, 1).reshape(b, c // 128, 128, t).transpose(0, 2, 1, 3)).reshape(b, 128, -1)


def by_partition(w, np):
    return np.ascontiguousarray(w.reshape(-1, 128, w.shape[-1]).transpose(1, 0, 2))


def kernel(**inputs):
    import numpy as np
    from concourse import bacc
    from concourse.bass_utils import run_bass_kernel_spmd

    a = {k: np.asarray(v) for k, v in inputs.items()}
    B, T, C = a["x"].shape
    E, _, I = a["L0_ffn_w_gate"].shape
    IS = a["L0_ffn_sw_gate"].shape[1]
    F = a["L1_ffn_w_down"].shape[1]

    def layers(name):
        return np.concatenate([a[f"L{n}_cond_{name}"].reshape(4, 128).T for n in range(2)], axis=1)

    moe = np.concatenate([a["L0_ffn_w_gate"].reshape(E, 4, 128, I), a["L0_ffn_w_up"].reshape(E, 4, 128, I)], axis=3)
    moe = np.ascontiguousarray(moe.transpose(0, 2, 1, 3)).reshape(E, 128, -1)
    full = IS // 128
    tiles = []
    for m in range(full):
        tiles += [a["L0_ffn_sw_gate"][:, m * 128:(m + 1) * 128], a["L0_ffn_sw_up"][:, m * 128:(m + 1) * 128]]
    tiles += [a["L0_ffn_sw_gate"][:, full * 128:], a["L0_ffn_sw_up"][:, full * 128:]]
    shared_gu = by_partition(np.concatenate(tiles, axis=1), np)
    w = a["L1_ffn_w_gate_up"].T.reshape(4, 128, 2, F // 128, 128)
    w = w.transpose(3, 1, 0, 2, 4).reshape(F // 128, 128, -1)
    ffn = np.ascontiguousarray(np.concatenate([w, a["L1_ffn_w_down"].T.reshape(F // 128, 128, C)], axis=2))

    part = np.arange(128)
    arrays = {
        "x_t": channel_major(a["x"], np),
        "side_t": channel_major(a["fside_BxSxS_0"], np),
        "x_rows": np.ascontiguousarray(a["x"].reshape(B * T, C)),
        "cond": np.ascontiguousarray(a["cond_512"]),
        "wkv_w": np.ascontiguousarray(layers("w")),
        "wkv_u": np.ascontiguousarray(layers("u")),
        "gate_w": by_partition(np.ascontiguousarray(a["L0_ffn_gate_w"].T), np),
        "moe_gu": moe,
        "moe_down": np.ascontiguousarray(a["L0_ffn_w_down"]),
        "shared_gu": shared_gu,
        "shared_down": np.ascontiguousarray(a["L0_ffn_sw_down"]),
        "ffn_w": ffn,
        "ident": np.eye(128, dtype=np.float32),
        "expert_iota": np.tile(np.arange(E, dtype=np.float32), (128, 1)),
        "pair_expert": (2 * np.arange(E // 2)[None, :] + (part >= 64)[:, None]).astype(np.float32),
        "token_key": (B * T - (np.arange(B * T // 128)[None, :] * 128 + part[:, None])).astype(np.float32),
        "slot_col": np.arange(64, dtype=np.float32).reshape(64, 1),
    }
    nc = bacc.Bacc("TRN2", target_bir_lowering=False, num_devices=1)
    args = [nc.dram_tensor(f"in_{k}", v.shape, mybir.dt.from_np(v.dtype), kind="ExternalInput").ap() for k, v in arrays.items()]
    out = nc.dram_tensor("out_t", (B, 128, 4 * T), F32, kind="ExternalOutput").ap()
    adaln_ffn_kernel(nc, *args, out)
    r = run_bass_kernel_spmd(nc, [{f"in_{k}": v for k, v in arrays.items()}], core_ids=[0])
    y = r.results[0]["out_t"].reshape(B, 128, 4, T)
    return np.ascontiguousarray(y.transpose(0, 3, 2, 1)).reshape(B, T, C)
```
